# Optimizing a Trainium2 kernel written in Bass

```python
import numpy as np
import jax
import jax.numpy as jnp

def _softmax(x, axis=-1):
    return jax.nn.softmax(x, axis=axis)

def _gelu(x):
    return jax.nn.gelu(x, approximate=True)

def _silu(x):
    return jax.nn.silu(x)

def _sigmoid(x):
    return jax.nn.sigmoid(x)

def _layernorm(x, axis=-1, eps=1e-05):
    m = jnp.mean(x, axis=axis, keepdims=True)
    v = jnp.var(x, axis=axis, keepdims=True)
    return (x - m) / jnp.sqrt(v + eps)

def _scatter_add(tgt, idx, src, axis=0):
    return tgt.at[idx].add(src)

def _segment_sum(src, seg, n):
    return jax.ops.segment_sum(src, seg, n)
kernel_name = 'mk_adj_ffn_d4_adj_r2_a8bc15'

def setup_inputs(seed: int=0):
    np.random.seed(seed)
    _w = jnp.asarray

    def _rec_inputs():
        import jax
        import jax.numpy as jnp
        _gk = jax.random.key(seed)
        x = -0.0005207 + 1.001 * jax.random.normal(jax.random.fold_in(_gk, 1), (1354, 128), jnp.float32)
        _w = (1.0 + jnp.arange(1354, dtype=jnp.float32)) ** (-0.5)
        _w = _w / _w.mean()
        _pij = jnp.clip(0.0014771 * _w[:, None] * _w[None, :], 0.0, 1.0)
        _a = jax.random.uniform(jax.random.fold_in(_gk, 2), (1354, 1354)) < _pij
        _a = jnp.logical_or(_a, jnp.eye(1354, dtype=bool))
        _af = _a.astype(jnp.float32)
        _af = _af * jax.random.uniform(jax.random.fold_in(_gk, 3), (1354, 1354), jnp.float32, 0.05, 1)
        adj = _af
        return (x, adj)
    x, adj = _rec_inputs()

    def _L0_gnn_setup():
        import jax, jax.numpy as jnp
        import numpy as np
        D_IN = 128
        D_ATTN = 64
        STEPS = 2
        TOP_P = 0.9
        TAU = 1.0
        LN_EPS = 1e-05
        N_NODES = 4096

        def _top_p_attention(X, W1, W2, W3):
            q = X @ W1.T @ W2.T
            k = X @ W3.T
            logits = q @ k.T / TAU
            probs = jax.nn.softmax(logits, axis=-1)
            idx = jnp.argsort(-probs, axis=-1)
            sp = jnp.take_along_axis(probs, idx, axis=-1)
            cs = jnp.cumsum(sp, axis=-1)
            keep_sorted = cs - sp < TOP_P
            rows = jnp.arange(probs.shape[0])[:, None]
            mask = jnp.zeros(probs.shape, dtype=bool).at[rows, idx].set(keep_sorted)
            A = probs * mask
            return A / jnp.maximum(A.sum(-1, keepdims=True), 1e-12)
        key = jax.random.key(seed)
        ks = jax.random.split(key, 8)
        N, d, da, steps = (N_NODES, D_IN, D_ATTN, STEPS)
        X = jax.random.normal(ks[0], (N, d), dtype=jnp.float32)
        S = jax.random.uniform(ks[1], (N, N), dtype=jnp.float32)
        W1 = jax.random.normal(ks[2], (da, d), dtype=jnp.float32) / np.sqrt(d)
        W2 = jax.random.normal(ks[3], (da, da), dtype=jnp.float32) / np.sqrt(da)
        W3 = jax.random.normal(ks[4], (da, d), dtype=jnp.float32) / np.sqrt(d)
        U1 = jax.random.normal(ks[5], (steps, d, d), dtype=jnp.float32) / np.sqrt(d)
        U2 = jax.random.normal(ks[6], (steps, d, d), dtype=jnp.float32) / np.sqrt(d)
        ln_g = jnp.ones((d,), dtype=jnp.float32)
        ln_b = jnp.zeros((d,), dtype=jnp.float32)
        return {'X': X, 'S': S, 'W1': W1, 'W2': W2, 'W3': W3, 'U1': U1, 'U2': U2, 'ln_g': ln_g, 'ln_b': ln_b}
    _L0_gnn_all = _L0_gnn_setup()
    _L0_gnn_in = {k: v for k, v in _L0_gnn_all.items() if k in ('W1', 'W2', 'W3', 'U1', 'U2', 'ln_g', 'ln_b')}
    del _L0_gnn_all

    def _L0_ffn_setup():
        import jax, jax.numpy as jnp
        import numpy as np
        NUM_EXPERTS = 8
        TOP_K = 2
        B, S, D = (8, 4096, 128)

        def _moe(tokens, router_w, w1, b1, w2, b2):
            N = tokens.shape[0]
            E = router_w.shape[0]
            logits = tokens.astype(jnp.float32) @ router_w.astype(jnp.float32).T
            probs = jax.nn.softmax(logits, axis=-1)
            rw, re = jax.lax.top_k(probs, TOP_K)
            if TOP_K > 1:
                rw = rw / jnp.maximum(rw.sum(-1, keepdims=True), 1e-12)
            rw = rw.astype(tokens.dtype)
            combine = jnp.zeros((N, E), tokens.dtype).at[jnp.arange(N)[:, None], re].set(rw)
            out = tokens
            for e in range(E):
                h = jax.nn.gelu(tokens @ w1[e] + b1[e], approximate=False)
                y = h @ w2[e] + b2[e]
                out = out + combine[:, e:e + 1] * y
            return out
        key = jax.random.key(seed)
        ks = jax.random.split(key, 4)
        scale = 1.0 / np.sqrt(D).astype(np.float32)
        return {'input_embeddings': jax.random.normal(ks[0], (B, S, D), jnp.float32), 'router_w': jax.random.normal(ks[1], (NUM_EXPERTS, D), jnp.float32) * scale, 'w1': jax.random.normal(ks[2], (NUM_EXPERTS, D, D), jnp.float32) * scale, 'b1': jnp.zeros((NUM_EXPERTS, D), jnp.float32), 'w2': jax.random.normal(ks[3], (NUM_EXPERTS, D, D), jnp.float32) * scale, 'b2': jnp.zeros((NUM_EXPERTS, D), jnp.float32)}
    _L0_ffn_all = _L0_ffn_setup()
    _L0_ffn_in = {k: v for k, v in _L0_ffn_all.items() if k in ('router_w', 'w1', 'b1', 'w2', 'b2')}
    del _L0_ffn_all

    def _L1_gnn_setup():
        import jax, jax.numpy as jnp
        import numpy as np
        ALPHA = 0.2
        NEG_INF = -9000000000000000.0
        LN_EPS = 1e-05
        N = 2048
        IN_F = 128
        OUT_F = 128
        HEADS = 4
        HEAD_DIM = OUT_F // HEADS
        EDGE_PROB = 0.02
        key = jax.random.key(seed)
        kx, ka, kw, kav = jax.random.split(key, 4)
        x = jax.random.normal(kx, (N, IN_F), dtype=jnp.float32)
        adj = jax.random.bernoulli(ka, EDGE_PROB, (N, N)).astype(jnp.float32)
        adj = jnp.maximum(adj, jnp.eye(N, dtype=jnp.float32))

        def xavier(k, shape, gain=1.414):
            fan_in, fan_out = (shape[0], shape[1])
            bound = gain * np.sqrt(6.0 / (fan_in + fan_out))
            return jax.random.uniform(k, shape, jnp.float32, -bound, bound)
        W = xavier(kw, (IN_F, OUT_F))
        a = xavier(kav, (2 * HEAD_DIM, 1))
        gamma = jnp.ones((OUT_F,), dtype=jnp.float32)
        beta = jnp.zeros((OUT_F,), dtype=jnp.float32)
        return {'x': x, 'adj': adj, 'W': W, 'a': a, 'gamma': gamma, 'beta': beta}
    _L1_gnn_all = _L1_gnn_setup()
    _L1_gnn_in = {k: v for k, v in _L1_gnn_all.items() if k in ('W', 'a', 'gamma', 'beta')}
    del _L1_gnn_all

    def _L1_ffn_setup():
        import jax, jax.numpy as jnp
        import numpy as np
        B, A = (2048, 8)
        IN, OUT = (128, 128)
        SH1, SH2 = (128, 128)
        EH1, EH2 = (128, 64)
        E, TOPK = (4, 2)

        def _shared_mlp(x, W1, b1, W2, b2, W3, b3):
            h = jax.nn.relu(x @ W1 + b1)
            h = jax.nn.relu(h @ W2 + b2)
            return h @ W3 + b3

        def _experts_mlp(x, eW1, eb1, eW2, eb2, eW3, eb3):
            h = jax.nn.relu(jnp.einsum('baf,efh->ebah', x, eW1) + eb1[:, None, None, :])
            h = jax.nn.relu(jnp.einsum('ebah,ehg->ebag', h, eW2) + eb2[:, None, None, :])
            o = jnp.einsum('ebag,ego->ebao', h, eW3) + eb3[:, None, None, :]
            return jnp.moveaxis(o, 0, -1)
        key = jax.random.key(seed)
        ks = jax.random.split(key, 16)
        s = 0.05
        return {'x': jax.random.normal(ks[0], (B, A, IN), jnp.float32), 'sW1': jax.random.normal(ks[1], (IN, SH1), jnp.float32) * s, 'sb1': jnp.zeros((SH1,), jnp.float32), 'sW2': jax.random.normal(ks[2], (SH1, SH2), jnp.float32) * s, 'sb2': jnp.zeros((SH2,), jnp.float32), 'sW3': jax.random.normal(ks[3], (SH2, OUT), jnp.float32) * s, 'sb3': jnp.zeros((OUT,), jnp.float32), 'eW1': jax.random.normal(ks[4], (E, IN, EH1), jnp.float32) * s, 'eb1': jnp.zeros((E, EH1), jnp.float32), 'eW2': jax.random.normal(ks[5], (E, EH1, EH2), jnp.float32) * s, 'eb2': jnp.zeros((E, EH2), jnp.float32), 'eW3': jax.random.normal(ks[6], (E, EH2, OUT), jnp.float32) * s, 'eb3': jnp.zeros((E, OUT), jnp.float32), 'gW': jax.random.normal(ks[7], (IN, E), jnp.float32) * s, 'gb': jnp.zeros((E,), jnp.float32)}
    _L1_ffn_all = _L1_ffn_setup()
    _L1_ffn_in = {k: v for k, v in _L1_ffn_all.items() if k in ('sW1', 'sb1', 'sW2', 'sb2', 'sW3', 'sb3', 'eW1', 'eb1', 'eW2', 'eb2', 'eW3', 'eb3', 'gW', 'gb')}
    del _L1_ffn_all

    def _L2_gnn_setup():
        import jax, jax.numpy as jnp
        import numpy as np
        N, F_IN, F_OUT = (4096, 128, 128)
        EDGE_PROB = 0.004
        key = jax.random.key(seed)
        k1, k2, k3, k4 = jax.random.split(key, 4)
        X = jax.random.normal(k1, (N, F_IN), dtype=jnp.float32)
        adj = (jax.random.uniform(k2, (N, N)) < EDGE_PROB).astype(jnp.float32)
        W = jax.random.normal(k3, (F_OUT, F_IN), dtype=jnp.float32) * 0.05
        b = jnp.zeros((F_OUT,), dtype=jnp.float32)
        S = jax.random.normal(k4, (2 * F_OUT,), dtype=jnp.float32) * 0.05
        return {'X': X, 'adj': adj, 'W': W, 'b': b, 'S': S}
    _L2_gnn_all = _L2_gnn_setup()
    _L2_gnn_in = {k: v for k, v in _L2_gnn_all.items() if k in ('W', 'b', 'S')}
    del _L2_gnn_all

    def _L2_ffn_setup():
        import jax, jax.numpy as jnp
        import numpy as np
        E = 8
        K = 2
        D = 128
        H = 256
        DOUT = 128
        EPS = 1e-05
        key = jax.random.key(seed)
        ks = jax.random.split(key, 9)
        s = 0.02
        return {'x': jax.random.normal(ks[0], (4, 4096, D), jnp.float32), 'gamma': 1.0 + 0.05 * jax.random.normal(ks[1], (D,), jnp.float32), 'beta': 0.05 * jax.random.normal(ks[2], (D,), jnp.float32), 'Wr': 0.01 * jax.random.normal(ks[3], (D, E), jnp.float32), 'br': jnp.zeros((E,), jnp.float32), 'W1': s * jax.random.normal(ks[4], (E, D, H), jnp.float32), 'b1': s * jax.random.normal(ks[5], (E, H), jnp.float32), 'W2': s * jax.random.normal(ks[6], (E, H, DOUT), jnp.float32), 'b2': s * jax.random.normal(ks[7], (E, DOUT), jnp.float32)}
    _L2_ffn_all = _L2_ffn_setup()
    _L2_ffn_in = {k: v for k, v in _L2_ffn_all.items() if k in ('gamma', 'beta', 'Wr', 'br', 'W1', 'b1', 'W2', 'b2')}
    del _L2_ffn_all

    def _L3_gnn_setup():
        import jax, jax.numpy as jnp
        import numpy as np
        N = 4096
        DIM = 128
        HEADS = 4
        HD = DIM // HEADS
        SCALE = HD ** (-0.5)
        key = jax.random.key(seed)
        ks = jax.random.split(key, 8)
        x = jax.random.normal(ks[0], (N, DIM), dtype=jnp.float32)
        adj_matrix = jax.random.uniform(ks[1], (N, N), dtype=jnp.float32)
        attn_mask = jax.random.randint(ks[2], (N, N), 0, 2, dtype=jnp.int32)
        Wqkv = jax.random.normal(ks[3], (DIM, 3 * DIM), dtype=jnp.float32) * DIM ** (-0.5)
        bqkv = jnp.zeros((3 * DIM,), dtype=jnp.float32)
        Wout = jax.random.normal(ks[4], (DIM, DIM), dtype=jnp.float32) * DIM ** (-0.5)
        bout = jnp.zeros((DIM,), dtype=jnp.float32)
        graph_bias = jax.random.normal(ks[5], (1, 1, 1), dtype=jnp.float32) * 0.1
        return {'x': x, 'adj_matrix': adj_matrix, 'attn_mask': attn_mask, 'Wqkv': Wqkv, 'bqkv': bqkv, 'Wout': Wout, 'bout': bout, 'graph_bias': graph_bias}
    _L3_gnn_all = _L3_gnn_setup()
    _L3_gnn_in = {k: v for k, v in _L3_gnn_all.items() if k in ('Wqkv', 'bqkv', 'Wout', 'bout', 'graph_bias')}
    del _L3_gnn_all

    def _L3_ffn_setup():
        import jax, jax.numpy as jnp
        import numpy as np
        B, S, D, H, E, K = (8, 4096, 128, 512, 8, 2)
        key = jax.random.key(seed)
        ks = jax.random.split(key, 7)
        s_in = 1.0 / np.sqrt(D)
        s_hid = 1.0 / np.sqrt(H)
        return {'x': jax.random.normal(ks[0], (B, S, D), dtype=jnp.float32), 'Wg': jax.random.uniform(ks[1], (E, D), jnp.float32, -s_in, s_in), 'bg': jax.random.uniform(ks[2], (E,), jnp.float32, -s_in, s_in), 'W1': jax.random.uniform(ks[3], (E, H, D), jnp.float32, -s_in, s_in), 'b1': jax.random.uniform(ks[4], (E, H), jnp.float32, -s_in, s_in), 'W2': jax.random.uniform(ks[5], (E, D, H), jnp.float32, -s_hid, s_hid), 'b2': jax.random.uniform(ks[6], (E, D), jnp.float32, -s_hid, s_hid)}
    _L3_ffn_all = _L3_ffn_setup()
    _L3_ffn_in = {k: v for k, v in _L3_ffn_all.items() if k in ('Wg', 'bg', 'W1', 'b1', 'W2', 'b2')}
    del _L3_ffn_all
    return {'x': x, 'adj': adj, 'L0_gnn_W1': _L0_gnn_in['W1'], 'L0_gnn_W2': _L0_gnn_in['W2'], 'L0_gnn_W3': _L0_gnn_in['W3'], 'L0_gnn_U1': _L0_gnn_in['U1'], 'L0_gnn_U2': _L0_gnn_in['U2'], 'L0_gnn_ln_g': _L0_gnn_in['ln_g'], 'L0_gnn_ln_b': _L0_gnn_in['ln_b'], 'L0_ffn_router_w': _L0_ffn_in['router_w'], 'L0_ffn_w1': _L0_ffn_in['w1'], 'L0_ffn_b1': _L0_ffn_in['b1'], 'L0_ffn_w2': _L0_ffn_in['w2'], 'L0_ffn_b2': _L0_ffn_in['b2'], 'L1_gnn_W': _L1_gnn_in['W'], 'L1_gnn_a': _L1_gnn_in['a'], 'L1_gnn_gamma': _L1_gnn_in['gamma'], 'L1_gnn_beta': _L1_gnn_in['beta'], 'L1_ffn_sW1': _L1_ffn_in['sW1'], 'L1_ffn_sb1': _L1_ffn_in['sb1'], 'L1_ffn_sW2': _L1_ffn_in['sW2'], 'L1_ffn_sb2': _L1_ffn_in['sb2'], 'L1_ffn_sW3': _L1_ffn_in['sW3'], 'L1_ffn_sb3': _L1_ffn_in['sb3'], 'L1_ffn_eW1': _L1_ffn_in['eW1'], 'L1_ffn_eb1': _L1_ffn_in['eb1'], 'L1_ffn_eW2': _L1_ffn_in['eW2'], 'L1_ffn_eb2': _L1_ffn_in['eb2'], 'L1_ffn_eW3': _L1_ffn_in['eW3'], 'L1_ffn_eb3': _L1_ffn_in['eb3'], 'L1_ffn_gW': _L1_ffn_in['gW'], 'L1_ffn_gb': _L1_ffn_in['gb'], 'L2_gnn_W': _L2_gnn_in['W'], 'L2_gnn_b': _L2_gnn_in['b'], 'L2_gnn_S': _L2_gnn_in['S'], 'L2_ffn_gamma': _L2_ffn_in['gamma'], 'L2_ffn_beta': _L2_ffn_in['beta'], 'L2_ffn_Wr': _L2_ffn_in['Wr'], 'L2_ffn_br': _L2_ffn_in['br'], 'L2_ffn_W1': _L2_ffn_in['W1'], 'L2_ffn_b1': _L2_ffn_in['b1'], 'L2_ffn_W2': _L2_ffn_in['W2'], 'L2_ffn_b2': _L2_ffn_in['b2'], 'L3_gnn_Wqkv': _L3_gnn_in['Wqkv'], 'L3_gnn_bqkv': _L3_gnn_in['bqkv'], 'L3_gnn_Wout': _L3_gnn_in['Wout'], 'L3_gnn_bout': _L3_gnn_in['bout'], 'L3_gnn_graph_bias': _L3_gnn_in['graph_bias'], 'L3_ffn_Wg': _L3_ffn_in['Wg'], 'L3_ffn_bg': _L3_ffn_in['bg'], 'L3_ffn_W1': _L3_ffn_in['W1'], 'L3_ffn_b1': _L3_ffn_in['b1'], 'L3_ffn_W2': _L3_ffn_in['W2'], 'L3_ffn_b2': _L3_ffn_in['b2']}

def reference(x, adj, L0_gnn_W1, L0_gnn_W2, L0_gnn_W3, L0_gnn_U1, L0_gnn_U2, L0_gnn_ln_g, L0_gnn_ln_b, L0_ffn_router_w, L0_ffn_w1, L0_ffn_b1, L0_ffn_w2, L0_ffn_b2, L1_gnn_W, L1_gnn_a, L1_gnn_gamma, L1_gnn_beta, L1_ffn_sW1, L1_ffn_sb1, L1_ffn_sW2, L1_ffn_sb2, L1_ffn_sW3, L1_ffn_sb3, L1_ffn_eW1, L1_ffn_eb1, L1_ffn_eW2, L1_ffn_eb2, L1_ffn_eW3, L1_ffn_eb3, L1_ffn_gW, L1_ffn_gb, L2_gnn_W, L2_gnn_b, L2_gnn_S, L2_ffn_gamma, L2_ffn_beta, L2_ffn_Wr, L2_ffn_br, L2_ffn_W1, L2_ffn_b1, L2_ffn_W2, L2_ffn_b2, L3_gnn_Wqkv, L3_gnn_bqkv, L3_gnn_Wout, L3_gnn_bout, L3_gnn_graph_bias, L3_ffn_Wg, L3_ffn_bg, L3_ffn_W1, L3_ffn_b1, L3_ffn_W2, L3_ffn_b2):
    import jax
    import jax.numpy as jnp

    def _L0_gnn_ref(X, S, W1, W2, W3, U1, U2, ln_g, ln_b):
        import jax, jax.numpy as jnp
        import numpy as np
        D_IN = 128
        D_ATTN = 64
        STEPS = 2
        TOP_P = 0.9
        TAU = 1.0
        LN_EPS = 1e-05
        N_NODES = 4096

        def _top_p_attention(X, W1, W2, W3):
            q = X @ W1.T @ W2.T
            k = X @ W3.T
            logits = q @ k.T / TAU
            probs = jax.nn.softmax(logits, axis=-1)
            idx = jnp.argsort(-probs, axis=-1)
            sp = jnp.take_along_axis(probs, idx, axis=-1)
            cs = jnp.cumsum(sp, axis=-1)
            keep_sorted = cs - sp < TOP_P
            rows = jnp.arange(probs.shape[0])[:, None]
            mask = jnp.zeros(probs.shape, dtype=bool).at[rows, idx].set(keep_sorted)
            A = probs * mask
            return A / jnp.maximum(A.sum(-1, keepdims=True), 1e-12)
        N = X.shape[0]
        R = S + jnp.eye(N, dtype=X.dtype)
        R = R / R.sum(-1, keepdims=True)
        Z = jnp.zeros_like(X)
        Xf = X
        Xa = X
        for n in range(STEPS):
            A = _top_p_attention(Xa, W1, W2, W3)
            Xf = R @ Xf
            Xa = A @ Xa
            Z = Z + Xf @ U1[n].T + Xa @ U2[n].T
        h = X + Z
        mu = h.mean(-1, keepdims=True)
        var = jnp.mean((h - mu) ** 2, axis=-1, keepdims=True)
        return (h - mu) / jnp.sqrt(var + LN_EPS) * ln_g + ln_b

    def _L0_ffn_ref(input_embeddings, router_w, w1, b1, w2, b2):
        import jax, jax.numpy as jnp
        import numpy as np
        NUM_EXPERTS = 8
        TOP_K = 2
        B, S, D = (8, 4096, 128)

        def _moe(tokens, router_w, w1, b1, w2, b2):
            N = tokens.shape[0]
            E = router_w.shape[0]
            logits = tokens.astype(jnp.float32) @ router_w.astype(jnp.float32).T
            probs = jax.nn.softmax(logits, axis=-1)
            rw, re = jax.lax.top_k(probs, TOP_K)
            if TOP_K > 1:
                rw = rw / jnp.maximum(rw.sum(-1, keepdims=True), 1e-12)
            rw = rw.astype(tokens.dtype)
            combine = jnp.zeros((N, E), tokens.dtype).at[jnp.arange(N)[:, None], re].set(rw)
            out = tokens
            for e in range(E):
                h = jax.nn.gelu(tokens @ w1[e] + b1[e], approximate=False)
                y = h @ w2[e] + b2[e]
                out = out + combine[:, e:e + 1] * y
            return out
        b, s, d = input_embeddings.shape
        tokens = input_embeddings.reshape(b * s, d)
        return _moe(tokens, router_w, w1, b1, w2, b2).reshape(b, s, d)

    def _L1_gnn_ref(x, adj, W, a, gamma, beta):
        import jax, jax.numpy as jnp
        import numpy as np
        ALPHA = 0.2
        NEG_INF = -9000000000000000.0
        LN_EPS = 1e-05
        N = 2048
        IN_F = 128
        OUT_F = 128
        HEADS = 4
        HEAD_DIM = OUT_F // HEADS
        EDGE_PROB = 0.02
        n = x.shape[0]
        head_dim = a.shape[0] // 2
        heads = W.shape[1] // head_dim
        h = (x @ W).reshape(n, heads, head_dim)
        src = jnp.einsum('nhd,d->nh', h, a[:head_dim, 0])
        dst = jnp.einsum('nhd,d->nh', h, a[head_dim:, 0])
        e = src[:, :, None] + dst.T[None, :, :]
        e = jnp.where(e > 0, e, ALPHA * e)
        mask = adj[:, None, :] > 0
        e = jnp.where(mask, e, NEG_INF)
        attn = jax.nn.softmax(e, axis=-1)
        out = jnp.einsum('nhm,mhd->nhd', attn, h)
        out = out.reshape(n, heads * head_dim)
        mu = jnp.mean(out, axis=-1, keepdims=True)
        var = jnp.var(out, axis=-1, keepdims=True)
        out = (out - mu) / jnp.sqrt(var + LN_EPS) * gamma + beta
        return out

    def _L1_ffn_ref(x, sW1, sb1, sW2, sb2, sW3, sb3, eW1, eb1, eW2, eb2, eW3, eb3, gW, gb):
        import jax, jax.numpy as jnp
        import numpy as np
        B, A = (2048, 8)
        IN, OUT = (128, 128)
        SH1, SH2 = (128, 128)
        EH1, EH2 = (128, 64)
        E, TOPK = (4, 2)

        def _shared_mlp(x, W1, b1, W2, b2, W3, b3):
            h = jax.nn.relu(x @ W1 + b1)
            h = jax.nn.relu(h @ W2 + b2)
            return h @ W3 + b3

        def _experts_mlp(x, eW1, eb1, eW2, eb2, eW3, eb3):
            h = jax.nn.relu(jnp.einsum('baf,efh->ebah', x, eW1) + eb1[:, None, None, :])
            h = jax.nn.relu(jnp.einsum('ebah,ehg->ebag', h, eW2) + eb2[:, None, None, :])
            o = jnp.einsum('ebag,ego->ebao', h, eW3) + eb3[:, None, None, :]
            return jnp.moveaxis(o, 0, -1)
        all_out = _experts_mlp(x, eW1, eb1, eW2, eb2, eW3, eb3)
        shared = _shared_mlp(x, sW1, sb1, sW2, sb2, sW3, sb3)
        gates = jax.nn.softmax(x @ gW + gb, axis=-1)
        topv, topi = jax.lax.top_k(gates, TOPK)
        topw = jax.nn.softmax(topv, axis=-1)
        sel = jnp.take_along_axis(all_out, topi[:, :, None, :], axis=-1)
        gated = jnp.sum(sel * topw[:, :, None, :], axis=-1)
        return shared + gated

    def _L2_gnn_ref(X, adj, W, b, S):
        import jax, jax.numpy as jnp
        import numpy as np
        N, F_IN, F_OUT = (4096, 128, 128)
        EDGE_PROB = 0.004
        Xp = X @ W.T + b
        f = Xp.shape[1]
        n = X.shape[0]
        a_src = Xp @ S[:f]
        a_dst = Xp @ S[f:]
        e = jax.nn.leaky_relu(a_src[:, None] + a_dst[None, :])
        mask = (adj != 0) | jnp.eye(n, dtype=bool)
        e = jnp.where(mask, e, -jnp.inf)
        attn = jax.nn.softmax(e, axis=1)
        return jax.nn.sigmoid(attn @ Xp)

    def _L2_ffn_ref(x, gamma, beta, Wr, br, W1, b1, W2, b2):
        import jax, jax.numpy as jnp
        import numpy as np
        E = 8
        K = 2
        D = 128
        H = 256
        DOUT = 128
        EPS = 1e-05
        mu = jnp.mean(x, axis=-1, keepdims=True)
        var = jnp.mean(jnp.square(x - mu), axis=-1, keepdims=True)
        xn = (x - mu) * jax.lax.rsqrt(var + EPS) * gamma + beta
        logits = jnp.einsum('bsd,de->bse', xn, Wr) + br
        top_vals, top_idx = jax.lax.top_k(logits, K)
        w = jax.nn.softmax(top_vals, axis=-1)
        w_full = jnp.einsum('bsk,bske->bse', w, jax.nn.one_hot(top_idx, E, dtype=w.dtype))
        y = jnp.zeros(x.shape[:-1] + (DOUT,), x.dtype)
        for e in range(E):
            h = jax.nn.gelu(jnp.einsum('bsd,dh->bsh', xn, W1[e]) + b1[e], approximate=False)
            y_e = jnp.einsum('bsh,hd->bsd', h, W2[e]) + b2[e]
            y = y + y_e * w_full[..., e, None]
        return y

    def _L3_gnn_ref(x, adj_matrix, attn_mask, Wqkv, bqkv, Wout, bout, graph_bias):
        import jax, jax.numpy as jnp
        import numpy as np
        N = 4096
        DIM = 128
        HEADS = 4
        HD = DIM // HEADS
        SCALE = HD ** (-0.5)
        n, d = x.shape
        qkv = x @ Wqkv + bqkv
        q, k, v = jnp.split(qkv, 3, axis=-1)

        def split_heads(t):
            return t.reshape(n, HEADS, HD).transpose(1, 0, 2)
        qh, kh, vh = (split_heads(q), split_heads(k), split_heads(v))
        scores = jnp.einsum('hnd,hmd->hnm', qh, kh) * SCALE
        scores = scores + graph_bias * adj_matrix[None, :, :]
        scores = jnp.where(attn_mask[None, :, :] == 0, jnp.float32(-1000000000.0), scores)
        attn = jax.nn.softmax(scores, axis=-1)
        out = jnp.einsum('hnm,hmd->hnd', attn, vh)
        out = out.transpose(1, 0, 2).reshape(n, d)
        return out @ Wout + bout

    def _L3_ffn_ref(x, Wg, bg, W1, b1, W2, b2):
        import jax, jax.numpy as jnp
        import numpy as np
        B, S, D, H, E, K = (8, 4096, 128, 512, 8, 2)
        gate_scores = jnp.einsum('bsd,ed->bse', x, Wg) + bg
        topk_scores, topk_idx = jax.lax.top_k(gate_scores, K)
        topk_probs = jax.nn.softmax(topk_scores, axis=-1)
        combine = jnp.sum(topk_probs[..., None] * jax.nn.one_hot(topk_idx, E, dtype=x.dtype), axis=-2)
        out = jnp.zeros_like(x)
        for e in range(E):
            h = jax.nn.relu(jnp.einsum('bsd,hd->bsh', x, W1[e]) + b1[e])
            y = jnp.einsum('bsh,dh->bsd', h, W2[e]) + b2[e]
            out = out + combine[..., e:e + 1] * y
        return out
    x = x + _L0_gnn_ref(_layernorm(x, axis=-1), adj, L0_gnn_W1, L0_gnn_W2, L0_gnn_W3, L0_gnn_U1, L0_gnn_U2, L0_gnn_ln_g, L0_gnn_ln_b)
    x = x + _L0_ffn_ref(_layernorm(x, axis=-1)[None], L0_ffn_router_w, L0_ffn_w1, L0_ffn_b1, L0_ffn_w2, L0_ffn_b2)[0]
    x = x + _L1_gnn_ref(_layernorm(x, axis=-1), adj, L1_gnn_W, L1_gnn_a, L1_gnn_gamma, L1_gnn_beta)
    x = x + _L1_ffn_ref(_layernorm(x, axis=-1)[None], L1_ffn_sW1, L1_ffn_sb1, L1_ffn_sW2, L1_ffn_sb2, L1_ffn_sW3, L1_ffn_sb3, L1_ffn_eW1, L1_ffn_eb1, L1_ffn_eW2, L1_ffn_eb2, L1_ffn_eW3, L1_ffn_eb3, L1_ffn_gW, L1_ffn_gb)[0]
    x = x + _L2_gnn_ref(_layernorm(x, axis=-1), adj, L2_gnn_W, L2_gnn_b, L2_gnn_S)
    x = x + _L2_ffn_ref(_layernorm(x, axis=-1)[None], L2_ffn_gamma, L2_ffn_beta, L2_ffn_Wr, L2_ffn_br, L2_ffn_W1, L2_ffn_b1, L2_ffn_W2, L2_ffn_b2)[0]
    x = x + _L3_gnn_ref(_layernorm(x, axis=-1), adj, adj, L3_gnn_Wqkv, L3_gnn_bqkv, L3_gnn_Wout, L3_gnn_bout, L3_gnn_graph_bias)
    x = x + _L3_ffn_ref(_layernorm(x, axis=-1)[None], L3_ffn_Wg, L3_ffn_bg, L3_ffn_W1, L3_ffn_b1, L3_ffn_W2, L3_ffn_b2)[0]
    return x

_drawn_inputs = setup_inputs


def setup_inputs(seed=0):
    import zlib

    import numpy as np

    out = dict(_drawn_inputs(seed))
    spreads = {'L0_gnn_ln_g': (1.0, 0.2),
     'L0_gnn_ln_b': (0.0, 0.1),
     'L0_ffn_b1': (0.0, 0.414),
     'L0_ffn_b2': (0.0, 0.286),
     'L1_gnn_gamma': (1.0, 0.2),
     'L1_gnn_beta': (0.0, 0.1),
     'L1_ffn_sb1': (0.0, 0.8),
     'L1_ffn_sb2': (0.0, 0.589),
     'L1_ffn_sb3': (0.0, 0.1),
     'L1_ffn_eb1': (0.0, 0.8),
     'L1_ffn_eb2': (0.0, 0.8),
     'L1_ffn_eb3': (0.0, 0.361),
     'L1_ffn_gb': (0.0, 0.8),
     'L2_gnn_b': (0.0, 0.8),
     'L2_ffn_br': (0.0, 0.8),
     'L3_gnn_bqkv': (0.0, 0.8),
     'L3_gnn_bout': (0.0, 0.8)}
    factors = {'L1_ffn_eW1': 5.078,
     'L1_ffn_eW2': 4.433,
     'L1_ffn_eW3': 3.307,
     'L1_ffn_gW': 2.747,
     'L2_gnn_S': 8.0,
     'L2_ffn_gamma': 8.0,
     'L2_ffn_beta': 8.0,
     'L2_ffn_Wr': 6.937,
     'L2_ffn_W1': 5.999,
     'L2_ffn_b1': 32.022,
     'L2_ffn_W2': 5.898,
     'L2_ffn_b2': 45.727,
     'L3_ffn_bg': 26.183,
     'L3_ffn_b1': 59.522,
     'L3_ffn_b2': 43.077,
     'L3_ffn_Wg': 3.661,
     'L3_ffn_W1': 5.481,
     'L3_ffn_W2': 3.822}
    for name, (base, spread) in spreads.items():
        noise = np.random.default_rng([zlib.crc32(name.encode()), seed]).standard_normal(out[name].shape)
        drawn = base * np.exp(spread * noise) if base else spread * noise
        out[name] = jnp.asarray(drawn.astype(out[name].dtype))
    for name, factor in factors.items():
        out[name] = (out[name] * factor).astype(out[name].dtype)
    return out
```

```python
import math
from contextlib import ExitStack

import concourse.bass as bass
from concourse import mybir

F32 = mybir.dt.float32
ALU = mybir.AluOpType
ACT = mybir.ActivationFunctionType
AX = mybir.AxisListType

P = 128
N = 1354
T = (N + P - 1) // P
NP = T * P
BANK = 512
CHUNKS = [(0, 512), (512, 512), (1024, N - 1024)]
PCHUNKS = [(0, 512), (512, 512), (1024, NP - 1024)]
GROUPS = [(0, 4), (4, 8), (8, T)]
EPS = 1e-5
MASKED = -9e15
MASKED3 = -1e9
TOP_P = 0.9
STEPS = 2
HALVINGS = (5, 7)
ROUNDS = (1, 2)
REACH = 9.6


class Core:

    def __init__(self, nc, ctx):
        self.nc = nc
        self.used = []
        self.ps = ctx.enter_context(nc.psum_tensor("psum", [P, 8, BANK], F32))

        def sb(name, shape):
            return ctx.enter_context(nc.sbuf_tensor(name, shape, F32))

        self.x = sb("x", [P, T, P])
        self.n = sb("n", [P, T, P])
        self.nf = sb("nf", [P, NP])
        self.ident = sb("ident", [P, P])

    def sem(self, name):
        s = self.nc.alloc_semaphore(name)
        self.used.append(s)
        return s

    def sems(self, *names):
        return [self.sem(n) for n in names]

    def recycle(self):
        self.nc.clear_and_free_semaphores(self.used)
        self.nc.all_engine_barrier()
        self.used = []

    def banks(self, first, count, columns):
        return self.ps[:, first:first + count, :].rearrange("p b c -> p (b c)")[:, 0:columns]


class Chain:

    def __init__(self, nc, engine, sem):
        self.nc, self.engine, self.sem, self.count = nc, engine, sem, 0

    def link(self, ins):
        self.count += 1
        ins.then_inc(self.sem, 1)
        self.engine.wait_ge(self.sem, self.count)


def per_node(column):
    return column.unsqueeze(2).broadcast_to([P, T, P])


def over_tiles(row, width=P):
    return row.unsqueeze(1).broadcast_to([P, T, width])


def normalise(chain, dve, out, src, centred, square, stats, var_ready, root_ready, n_ready):
    nc = chain.nc
    total, neg_mean, var, root, rstd, t1 = [stats[:, i, :] for i in range(6)]
    chain.link(nc.vector.reduce_sum(total, src, AX.X))
    chain.link(nc.vector.tensor_scalar(neg_mean, total, -1.0 / P, None, ALU.mult))
    chain.link(nc.vector.tensor_tensor(centred, src, per_node(neg_mean), ALU.add))
    chain.link(nc.vector.tensor_tensor(square, centred, centred, ALU.mult))
    chain.link(nc.vector.reduce_sum(total, square, AX.X))
    nc.vector.tensor_scalar(var, total, 1.0 / P, EPS, ALU.mult, ALU.add).then_inc(var_ready, 1)
    dve.wait_ge(var_ready, 1)
    dve.wait_ge(root_ready, 1)
    chain.link(nc.vector.reciprocal(rstd, root))
    chain.link(nc.vector.tensor_tensor(t1, rstd, rstd, ALU.mult))
    chain.link(nc.vector.tensor_tensor(t1, t1, var, ALU.mult))
    chain.link(nc.vector.tensor_scalar(t1, t1, -0.5, 1.5, ALU.mult, ALU.add))
    chain.link(nc.vector.tensor_tensor(rstd, rstd, t1, ALU.mult))
    nc.vector.tensor_tensor(out, centred, per_node(rstd), ALU.mult).then_inc(n_ready, 1)


def turn_tiles(pe, core, src, turned, first_bank=0):
    nc = core.nc
    for g, (a, b) in enumerate(GROUPS):
        for t in range(a, b):
            mm = nc.tensor.transpose(core.ps[:, first_bank + g, (t - a) * P:(t - a + 1) * P],
                                     src[:, t, :], core.ident[:])
        mm.then_inc(turned, 1)


def layernorm_stage(core, name, affine=None):
    nc = core.nc
    with ExitStack() as ctx:
        centred = ctx.enter_context(nc.sbuf_tensor(f"{name}_centred", [P, T, P], F32))
        square = ctx.enter_context(nc.sbuf_tensor(f"{name}_square", [P, T, P], F32))
        stats = ctx.enter_context(nc.sbuf_tensor(f"{name}_stats", [P, 6, T], F32))
        gain = ctx.enter_context(nc.sbuf_tensor(f"{name}_gain", [P, 2], F32))
        steps, var_ready, root_ready, n_ready, turned, nf_ready, loaded = core.sems(
            *[f"{name}_{s}" for s in ("steps", "var_ready", "root_ready", "n_ready", "turned", "nf_ready", "affine")])
        with nc.Block() as block:
            @block.vector
            def _(dve):
                chain = Chain(nc, dve, steps)
                normalise(chain, dve, core.n[:], core.x[:], centred[:], square[:], stats,
                          var_ready, root_ready, n_ready)
                dve.wait_ge(turned, 3)
                a, w = PCHUNKS[2]
                if affine is None:
                    nc.vector.tensor_copy(core.nf[:, a:a + w], core.banks(2, 1, w)).then_inc(nf_ready, 1)
                else:
                    dve.wait_ge(loaded, 32)
                    nc.vector.tensor_scalar(core.nf[:, a:a + w], core.banks(2, 1, w), gain[:, 0:1], gain[:, 1:2],
                                            ALU.mult, ALU.add).then_inc(nf_ready, 1)

            @block.sync
            def _(sp):
                if affine is not None:
                    for i in range(2):
                        sp.dma_start(gain[:, i:i + 1], affine[i]).then_inc(loaded, 16)

            @block.scalar
            def _(act):
                act.wait_ge(var_ready, 1)
                nc.scalar.activation(stats[:, 3, :], stats[:, 2, :], ACT.Sqrt).then_inc(root_ready, 1)
                for g in range(2):
                    act.wait_ge(turned, g + 1)
                    a, w = PCHUNKS[g]
                    if affine is None:
                        nc.scalar.activation(core.nf[:, a:a + w], core.banks(g, 1, w), ACT.Copy).then_inc(nf_ready, 1)
                    else:
                        act.wait_ge(loaded, 32)
                        nc.scalar.activation(core.nf[:, a:a + w], core.banks(g, 1, w), ACT.Identity,
                                             bias=gain[:, 1:2], scale=gain[:, 0:1]).then_inc(nf_ready, 1)

            @block.tensor
            def _(pe):
                pe.wait_ge(n_ready, 1)
                turn_tiles(pe, core, core.n, turned)


def first_of_equals(chain, nc, eq, count, experts):
    chain.link(nc.vector.tensor_copy(count, eq))
    for e in range(1, experts):
        chain.link(nc.vector.tensor_tensor(count[:, :, e:e + 1], count[:, :, e:e + 1],
                                           count[:, :, e - 1:e], ALU.add))
    chain.link(nc.vector.tensor_scalar(count, count, 1.0, None, ALU.is_equal))
    chain.link(nc.vector.tensor_tensor(eq, eq, count, ALU.mult))


def router_stage(core, name, experts, wr, bias, b_out, comb, second_softmax, add_n, extra, feats, nodes):
    nc = core.nc
    cols = experts + extra
    with ExitStack() as ctx:
        def sb(n, shape):
            return ctx.enter_context(nc.sbuf_tensor(f"{name}_{n}", shape, F32))

        w = sb("router_w", [P, experts])
        brow = sb("router_b", [P, experts])
        bo = sb("b_out", [cols, P])
        combt = sb("comb_t", [cols, NP])
        lg, lg2, eq1, eq2, cnt, pr = [sb(f"lg{i}", [P, T, experts]) for i in range(6)]
        m1, m2, d, e2, w1, w2, sm, rs = [sb(f"st{i}", [P, T]) for i in range(8)]
        loaded, logits, steps, exp_in, exp_out, comb_ready, turned, combt_ready, biased = core.sems(
            *[f"{name}_{s}" for s in ("loaded", "logits", "rsteps", "exp_in", "exp_out", "comb_ready",
                                      "comb_turned", "combt_ready", "bias_out")])
        loads = [(w[:], wr), (bo[:], b_out)]
        if bias is not None:
            loads.append((brow[:], bias.partition_broadcast(P)))

        def bc(col):
            return col.unsqueeze(2).broadcast_to([P, T, experts])

        with nc.Block() as block:
            @block.sync
            def _(sp):
                for dst, src in loads:
                    sp.dma_start(dst, src).then_inc(loaded, 16)

            @block.tensor
            def _(pe):
                pe.wait_ge(loaded, 16 * len(loads))
                for t in range(T):
                    mm = nc.tensor.matmul(core.ps[:, 0, t * experts:(t + 1) * experts],
                                          feats[:, t * P:(t + 1) * P], w[:], start=True, stop=True)
                mm.then_inc(logits, 1)
                pe.wait_ge(comb_ready, 1)
                for g, (a, b) in enumerate(GROUPS):
                    for t in range(a, b):
                        mm = nc.tensor.transpose(core.ps[0:cols, 1 + g, (t - a) * P:(t - a + 1) * P],
                                                 comb[:, t, 0:cols], core.ident[:])
                    mm.then_inc(turned, 1)
                for g, (a, b) in enumerate(GROUPS):
                    pe.wait_ge(combt_ready, g + 1)
                    for t in range(a, b):
                        mm = nc.tensor.matmul(core.ps[:, 4 + g, (t - a) * P:(t - a + 1) * P],
                                              combt[:, t * P:(t + 1) * P], bo[:], start=True, stop=True)
                    mm.then_inc(biased, 1)

            @block.scalar
            def _(act):
                if second_softmax:
                    act.wait_ge(exp_in, 1)
                    nc.scalar.activation(pr[:], lg2[:], ACT.Exp).then_inc(exp_out, 1)
                act.wait_ge(exp_in, 1 + second_softmax)
                nc.scalar.activation(e2[:], d[:], ACT.Exp).then_inc(exp_out, 1)
                for g, (a, wd) in enumerate(PCHUNKS):
                    act.wait_ge(turned, g + 1)
                    nc.scalar.activation(combt[:, a:a + wd], core.ps[0:cols, 1 + g, 0:wd],
                                         ACT.Copy).then_inc(combt_ready, 1)

            @block.vector
            def _(dve):
                chain = Chain(nc, dve, steps)
                dve.wait_ge(logits, 1)
                raw = core.ps[:, 0, 0:T * experts].rearrange("p (t e) -> p t e", e=experts)
                if bias is not None:
                    dve.wait_ge(loaded, 16 * len(loads))
                    chain.link(nc.vector.tensor_tensor(lg[:], raw, over_tiles(brow[:], experts), ALU.add))
                else:
                    chain.link(nc.vector.tensor_copy(lg[:], raw))
                if second_softmax:
                    chain.link(nc.vector.reduce_max(m1[:], lg[:], AX.X))
                    nc.vector.tensor_tensor(lg2[:], lg[:], bc(m1[:]), ALU.subtract).then_inc(exp_in, 1)
                    dve.wait_ge(exp_out, 1)
                    chain.link(nc.vector.reduce_sum(sm[:], pr[:], AX.X))
                    chain.link(nc.vector.reciprocal(rs[:], sm[:]))
                    chain.link(nc.vector.tensor_tensor(lg[:], pr[:], bc(rs[:]), ALU.mult))
                chain.link(nc.vector.reduce_max(m1[:], lg[:], AX.X))
                chain.link(nc.vector.tensor_tensor(eq1[:], lg[:], bc(m1[:]), ALU.is_equal))
                first_of_equals(chain, nc, eq1[:], cnt[:], experts)
                chain.link(nc.vector.scalar_tensor_tensor(out=lg2[:], in0=eq1[:], scalar=-1e30, in1=lg[:],
                                                          op0=ALU.mult, op1=ALU.add))
                chain.link(nc.vector.reduce_max(m2[:], lg2[:], AX.X))
                chain.link(nc.vector.tensor_tensor(eq2[:], lg2[:], bc(m2[:]), ALU.is_equal))
                first_of_equals(chain, nc, eq2[:], cnt[:], experts)
                nc.vector.tensor_tensor(d[:], m2[:], m1[:], ALU.subtract).then_inc(exp_in, 1)
                dve.wait_ge(exp_out, 1 + second_softmax)
                chain.link(nc.vector.tensor_scalar(sm[:], e2[:], 1.0, None, ALU.add))
                chain.link(nc.vector.reciprocal(w1[:], sm[:]))
                chain.link(nc.vector.tensor_tensor(w2[:], w1[:], e2[:], ALU.mult))
                chain.link(nc.vector.tensor_tensor(eq1[:], eq1[:], bc(w1[:]), ALU.mult))
                chain.link(nc.vector.tensor_tensor(eq2[:], eq2[:], bc(w2[:]), ALU.mult))
                if extra:
                    chain.link(nc.vector.memset(comb[:, :, experts:cols], 1.0))
                nc.vector.tensor_tensor(comb[:, :, 0:experts], eq1[:], eq2[:], ALU.add).then_inc(comb_ready, 1)
                if add_n:
                    chain.link(nc.vector.tensor_tensor(core.x[:], core.x[:], nodes, ALU.add))
                for g, (a, b) in enumerate(GROUPS):
                    dve.wait_ge(biased, g + 1)
                    y = core.banks(4 + g, 1, (b - a) * P).rearrange("p (t c) -> p t c", c=P)
                    chain.link(nc.vector.tensor_tensor(core.x[:, a:b, :], core.x[:, a:b, :], y, ALU.add))


def ffn_stage(core, name, experts, parts, func, w1, b1, w2, comb, feats):
    nc = core.nc
    HB, YB = 0, 4
    U = 3 * parts
    with ExitStack() as ctx:
        def sb(n, shape):
            return ctx.enter_context(nc.sbuf_tensor(f"{name}_{n}", shape, F32))

        w1s, w2s = sb("w1s", [P, 2, parts, P]), sb("w2s", [P, 2, parts, P])
        b1s = sb("b1s", [P, 2, parts])
        hid = sb("hid", [P, 2, parts, NP])
        w_in0, w_in1, h_made, h_kept, y_made, y_added = core.sems(
            *[f"{name}_{s}" for s in ("w_in0", "w_in1", "h_made", "h_kept", "y_made", "y_added")])
        w_in = [w_in0, w_in1]

        def pairs(engine, body, first, last):
            for e in range(first):
                body(e)
            if last - first >= 4:
                with engine.Fori(first, last, 2) as e:
                    body(e)
                    body(e + 1, 1)
            else:
                for e in range(first, last):
                    body(e)
            for e in range(last, experts):
                body(e)

        with nc.Block() as block:
            @block.sync
            def _(sp):
                for e in range(experts):
                    if e >= 2:
                        sp.wait_ge(y_made, 3 * (e - 1))
                    sp.dma_start(w1s[:, e % 2], w1[e].rearrange("p (c k) -> p c k", k=P)).then_inc(w_in[e % 2], 16)
                    sp.dma_start(w2s[:, e % 2], w2[e]).then_inc(w_in[e % 2], 16)
                    sp.dma_start(b1s[:, e % 2], b1[e]).then_inc(w_in[e % 2], 16)

            @block.tensor
            def _(pe):
                def hidden(e):
                    s = e % 2
                    pe.wait_ge(w_in[s], 48 * (e // 2 + 1))
                    for c in range(parts):
                        for j, (a, w) in enumerate(PCHUNKS):
                            u = e * U + 3 * c + j
                            if u >= 4:
                                pe.wait_ge(h_kept, u - 3)
                            nc.tensor.matmul(core.ps[:, HB + u % 4, 0:w], w1s[:, s, c, :], feats[:, a:a + w],
                                             start=True, stop=True).then_inc(h_made, 1)

                def output(e):
                    s = e % 2
                    pe.wait_ge(h_kept, (e + 1) * U)
                    for g, (a, b) in enumerate(GROUPS):
                        if e >= 1:
                            pe.wait_ge(y_added, 3 * (e - 1) + g + 1)
                        for t in range(a, b):
                            for c in range(parts):
                                mm = nc.tensor.matmul(core.ps[:, YB + g, (t - a) * P:(t - a + 1) * P],
                                                      hid[:, s, c, t * P:(t + 1) * P], w2s[:, s, c, :],
                                                      start=(c == 0), stop=(c == parts - 1))
                        mm.then_inc(y_made, 1)

                hidden(0)
                for e in range(experts):
                    if e + 1 < experts:
                        hidden(e + 1)
                    output(e)

            @block.scalar
            def _(act):
                for e in range(experts):
                    s = e % 2
                    act.wait_ge(w_in[s], 48 * (e // 2 + 1))
                    if e >= 2:
                        act.wait_ge(y_made, 3 * (e - 1))
                    for c in range(parts):
                        for j, (a, w) in enumerate(PCHUNKS):
                            u = e * U + 3 * c + j
                            act.wait_ge(h_made, u + 1)
                            nc.scalar.activation(hid[:, s, c, a:a + w], core.ps[:, HB + u % 4, 0:w], func,
                                                 bias=b1s[:, s, c:c + 1]).then_inc(h_kept, 1)

            @block.vector
            def _(dve):
                for e in range(experts):
                    for g, (a, b) in enumerate(GROUPS):
                        dve.wait_ge(y_made, 3 * e + g + 1)
                        if e >= 1:
                            dve.wait_ge(y_added, 3 * (e - 1) + g + 1)
                        for t in range(a, b):
                            add = nc.vector.scalar_tensor_tensor(
                                out=core.x[:, t, :], in0=core.ps[:, YB + g, (t - a) * P:(t - a + 1) * P],
                                scalar=comb[:, t, e:e + 1], in1=core.x[:, t, :], op0=ALU.mult, op1=ALU.add)
                        add.then_inc(y_added, 1)


def deep_ffn_stage(core, name, experts, w1, b1, w2, b2, w3, comb, feats):
    nc = core.nc
    with ExitStack() as ctx:
        def sb(n, shape):
            return ctx.enter_context(nc.sbuf_tensor(f"{name}_{n}", shape, F32))

        w1s, w2s, w3s = [sb(n, [P, experts, P]) for n in ("w1s", "w2s", "w3s")]
        b1s, b2s = sb("b1s", [P, experts]), sb("b2s", [P, experts])
        h1, h2 = sb("h1", [P, 2, NP]), sb("h2", [P, 2, NP])
        loaded, h1_made, h1_kept, h2_made, h2_kept, y_made, y_added = core.sems(
            *[f"{name}_{s}" for s in ("loaded", "h1_made", "h1_kept", "h2_made", "h2_kept", "y_made", "y_added")])
        loads = [(w1s, w1), (w2s, w2), (w3s, w3), (b1s, b1), (b2s, b2)]
        HB, YB = 0, 4
        order = [(1, 0)]
        for e in range(experts):
            order += [(1, e + 1)] * (e + 1 < experts) + [(2, e)]
        at = {le: 3 * i for i, le in enumerate(order)}

        with nc.Block() as block:
            @block.sync
            def _(sp):
                for dst, src in loads:
                    sp.dma_start(dst[:], src).then_inc(loaded, 16)

            @block.tensor
            def _(pe):
                pe.wait_ge(loaded, 16 * len(loads))

                def free_bank(u):
                    if u >= 4:
                        layer, e = order[(u - 4) // 3]
                        pe.wait_ge(h1_kept if layer == 1 else h2_kept, 3 * e + (u - 4) % 3 + 1)

                def layer1(e):
                    for j, (a, w) in enumerate(PCHUNKS):
                        u = at[1, e] + j
                        free_bank(u)
                        nc.tensor.matmul(core.ps[:, HB + u % 4, 0:w], w1s[:, e, :], feats[:, a:a + w],
                                         start=True, stop=True).then_inc(h1_made, 1)

                def layer2(e):
                    for j, (a, w) in enumerate(PCHUNKS):
                        u = at[2, e] + j
                        free_bank(u)
                        pe.wait_ge(h1_kept, 3 * e + j + 1)
                        nc.tensor.matmul(core.ps[:, HB + u % 4, 0:w], w2s[:, e, :], h1[:, e % 2, a:a + w],
                                         start=True, stop=True).then_inc(h2_made, 1)

                def layer3(e):
                    for g, (a, b) in enumerate(GROUPS):
                        pe.wait_ge(h2_kept, 3 * e + g + 1)
                        if e >= 1:
                            pe.wait_ge(y_added, 3 * (e - 1) + g + 1)
                        for t in range(a, b):
                            mm = nc.tensor.matmul(core.ps[:, YB + g, (t - a) * P:(t - a + 1) * P],
                                                  h2[:, e % 2, t * P:(t + 1) * P], w3s[:, e, :],
                                                  start=True, stop=True)
                        mm.then_inc(y_made, 1)

                layer1(0)
                for e in range(experts):
                    if e + 1 < experts:
                        layer1(e + 1)
                    layer2(e)
                    if e >= 1:
                        layer3(e - 1)
                layer3(experts - 1)

            @block.scalar
            def _(act):
                act.wait_ge(loaded, 16 * len(loads))
                for layer, e in order:
                    made, kept, b, h = (h1_made, h1_kept, b1s, h1) if layer == 1 else (h2_made, h2_kept, b2s, h2)
                    if e >= 2:
                        if layer == 1:
                            act.wait_ge(h2_made, 3 * (e - 1))
                        else:
                            act.wait_ge(y_made, 3 * (e - 1))
                    for j, (a, w) in enumerate(PCHUNKS):
                        act.wait_ge(made, 3 * e + j + 1)
                        nc.scalar.activation(h[:, e % 2, a:a + w], core.ps[:, HB + (at[layer, e] + j) % 4, 0:w],
                                             ACT.Relu, bias=b[:, e:e + 1]).then_inc(kept, 1)

            @block.vector
            def _(dve):
                for e in range(experts):
                    for g, (a, b) in enumerate(GROUPS):
                        dve.wait_ge(y_made, 3 * e + g + 1)
                        if e >= 1:
                            dve.wait_ge(y_added, 3 * (e - 1) + g + 1)
                        for t in range(a, b):
                            add = nc.vector.scalar_tensor_tensor(
                                out=core.x[:, t, :], in0=core.ps[:, YB + g, (t - a) * P:(t - a + 1) * P],
                                scalar=comb[:, t, e:e + 1], in1=core.x[:, t, :], op0=ALU.mult, op1=ALU.add)
                        add.then_inc(y_added, 1)


def wait(engine, sem, value):
    if not isinstance(value, int) or value > 0:
        engine.wait_ge(sem, value)


class Items:

    def __init__(self, heads):
        self.heads, self.count = heads, heads * T

    def near(self, t, h, d):
        t, h = t + (h + d) // self.heads, (h + d) % self.heads
        if isinstance(t, int) and not 0 <= t < T:
            return None
        return t, h, t * self.heads + h, (h if self.heads > 1 else t) % 2

    def run(self, engine, step):
        step(-1, self.heads - 1)
        if self.heads > 1:
            for h in range(self.heads):
                step(0, h)
            with engine.Fori(1, T - 1) as t:
                for h in range(self.heads):
                    step(t, h)
            for h in range(self.heads):
                step(T - 1, h)
        else:
            for t in range(T):
                step(t, 0)
        step(T, 0)
        step(T + 1 // self.heads, 1 % self.heads)


class Mixing:

    TURN, OUT = 3, 6

    def __init__(self, core, ctx, name, items, values, width, out, out_width, source=None):
        nc = self.nc = core.nc
        self.core, self.items, self.values, self.width = core, items, values, width
        self.out, self.out_width = out, out_width
        if source is None:
            self.probs = ctx.enter_context(nc.sbuf_tensor(f"{name}_probs", [P, 2, NP], F32))
        self.source = source or (lambda t, s: self.probs[:, s, :])
        self.turned_probs = ctx.enter_context(nc.sbuf_tensor(f"{name}_turned_probs", [P, 2, NP], F32))
        (self.probs_ready, self.turned, self.out_made, self.out_read,
         *self.kept) = core.sems(*[f"{name}_{s}" for s in ("probs_ready", "turned", "out_made", "out_read",
                                                           "kept0", "kept1", "kept2")])

    def wait_probs_slot(self, engine, k):
        wait(engine, self.turned, 3 * (k - 1))

    def turn(self, pe, item):
        t, h, k, s = item
        pe.wait_ge(self.probs_ready, k + 1)
        for g, (a, b) in enumerate(GROUPS):
            wait(pe, self.kept[g], k)
            for j in range(a, b):
                mm = self.nc.tensor.transpose(self.core.ps[:, self.TURN + g, (j - a) * P:(j - a + 1) * P],
                                              self.source(t, s)[:, j * P:(j + 1) * P], self.core.ident[:])
            mm.then_inc(self.turned, 1)

    def keep(self, engine, copy, g, item):
        t, h, k, s = item
        wait(engine, self.out_made, k - 1)
        engine.wait_ge(self.turned, 3 * k + g + 1)
        a, w = PCHUNKS[g]
        copy(self.turned_probs[:, s, a:a + w], self.core.ps[:, self.TURN + g, 0:w]).then_inc(self.kept[g], 1)

    def mix(self, pe, item):
        t, h, k, s = item
        wait(pe, self.out_read, k - 1)
        for j in range(T):
            for g, (a, _) in enumerate(GROUPS):
                if j == a:
                    pe.wait_ge(self.kept[g], k + 1)
            mm = self.nc.tensor.matmul(self.core.ps[:, self.OUT + s, 0:self.width],
                                       self.turned_probs[:, s, j * P:(j + 1) * P], self.values(j, h),
                                       start=(j == 0), stop=(j == T - 1))
        mm.then_inc(self.out_made, 1)

    def take_out(self, engine, item, copy):
        t, h, k, s = item
        engine.wait_ge(self.out_made, k + 1)
        w = self.out_width
        copy(self.out[:, t, h * w:(h + 1) * w], self.core.ps[:, self.OUT + s, 0:w]).then_inc(self.out_read, 1)


def act_copy(nc):
    return lambda out, src: nc.scalar.activation(out, src, ACT.Copy)


def project_stage(core, name, feats, loads, by_feature, by_node):
    nc = core.nc
    loaded, made, kept, node_made, node_kept = core.sems(
        *[f"{name}_{s}" for s in ("loaded", "made", "kept", "node_made", "node_kept")])
    with nc.Block() as block:
        @block.sync
        def _(sp):
            for dst, src in loads:
                sp.dma_start(dst, src).then_inc(loaded, 16)

        @block.tensor
        def _(pe):
            pe.wait_ge(loaded, 16 * len(loads))
            for i, (out, w, scale, bias) in enumerate(by_feature):
                for j, (a, c) in enumerate(PCHUNKS):
                    if i:
                        pe.wait_ge(kept, 3 * (i - 1) + j + 1)
                    nc.tensor.matmul(core.ps[:, j, 0:c], w, feats[:, a:a + c], start=True, stop=True).then_inc(made, 1)
            for i, (out, w, bias) in enumerate(by_node):
                for g, (a, b) in enumerate(GROUPS):
                    if i:
                        pe.wait_ge(node_kept, 3 * (i - 1) + g + 1)
                    for t in range(a, b):
                        mm = nc.tensor.matmul(core.ps[:, 3 + g, (t - a) * P:(t - a + 1) * P],
                                              feats[:, t * P:(t + 1) * P], w, start=True, stop=True)
                    mm.then_inc(node_made, 1)

        @block.scalar
        def _(act):
            act.wait_ge(loaded, 16 * len(loads))
            for i, (out, w, scale, bias) in enumerate(by_feature):
                for j, (a, c) in enumerate(PCHUNKS):
                    act.wait_ge(made, 3 * i + j + 1)
                    if bias is None:
                        nc.scalar.activation(out[:, a:a + c], core.ps[:, j, 0:c], ACT.Copy, scale=scale).then_inc(kept, 1)
                    else:
                        nc.scalar.activation(out[:, a:a + c], core.ps[:, j, 0:c], ACT.Identity,
                                             bias=bias).then_inc(kept, 1)

        @block.vector
        def _(dve):
            dve.wait_ge(loaded, 16 * len(loads))
            for i, (out, w, bias) in enumerate(by_node):
                for g, (a, b) in enumerate(GROUPS):
                    dve.wait_ge(node_made, 3 * i + g + 1)
                    y = core.banks(3 + g, 1, (b - a) * P).rearrange("p (t c) -> p t c", c=P)
                    if bias is None:
                        nc.vector.tensor_copy(out[:, a:b, 0:P], y).then_inc(node_kept, 1)
                    else:
                        rep = bias.unsqueeze(1).broadcast_to([P, b - a, P])
                        nc.vector.tensor_tensor(out[:, a:b, 0:P], y, rep, ALU.add).then_inc(node_kept, 1)


def graph_attention(core, name, heads, slope, adj, w_dram, bias_dram, a_src, a_dst, out, sums, unlinked, self_loops):
    nc = core.nc
    dh = P // heads
    items = Items(heads)
    with ExitStack() as ctx:
        def sb(n, shape):
            return ctx.enter_context(nc.sbuf_tensor(f"{name}_{n}", shape, F32))

        w = sb("w", [P, P])
        bias_col, bias_rep = sb("bias_col", [P, 1]), sb("bias_rep", [P, P])
        src_rep, dst_col, dst_w = sb("src_rep", [P, P]), sb("dst_col", [P, 1]), sb("dst_w", [P, P])
        hf, ht, tmp = sb("hf", [P, NP]), sb("ht", [P, T, P]), sb("tmp", [P, T, P])
        dst = sb("dst", [P, heads, N])
        src, src_sl = sb("src", [P, T * heads]), sb("src_sl", [P, T * heads])
        other = sb("other", [P, P])
        slots = 2 if heads == 1 else 1
        links = sb("links", [P, slots, NP])
        mask = sb("mask", [P, NP])
        masked, soft = sb("masked", [P, 2, N]), sb("soft", [P, 2, N])
        row_max = sb("row_max", [P, 2])
        neg_z, neg_max = [sb(n, [P, T * heads]) for n in ("neg_z", "neg_max")]

        loads = [(w[:], w_dram)]
        for i in range(heads):
            loads.append((src_rep[:, i * dh:(i + 1) * dh], a_src.partition_broadcast(P)))
            loads.append((dst_col[i * dh:(i + 1) * dh, :], a_dst.unsqueeze(1)))
        if bias_dram is not None:
            loads.append((bias_col[:], bias_dram.unsqueeze(1)))
            loads.append((bias_rep[:], bias_dram.partition_broadcast(P)))
        project_stage(core, name, core.nf, loads,
                      [(hf, w[:], 1.0, bias_col[:, 0:1] if bias_dram is not None else None)],
                      [(ht, w[:], bias_rep[:] if bias_dram is not None else None)])

        mixing = Mixing(core, ctx, name, items, lambda j, h: ht[:, j, h * dh:(h + 1) * dh], dh, out, dh)
        adj_in = core.sems(*[f"{name}_adj_in{i}" for i in range(slots)])
        (steps, dst_w_ready, dst_made, dst_kept, ready, mask_made, maxed, shifted, front, scaled,
         rectified) = core.sems(*[f"{name}_{s}" for s in (
             "steps", "dst_w_ready", "dst_made", "dst_kept", "ready", "mask_made", "maxed", "shifted",
             "front", "scaled", "rectified")])

        with nc.Block() as block:
            @block.sync
            def _(sp):
                sp.dma_start(links[:, 0, :], adj[0:P, :]).then_inc(adj_in[0], 16)
                if slots == 2:
                    sp.dma_start(links[:, 1, :], adj[P:2 * P, :]).then_inc(adj_in[1], 16)
                    for t in range(2, T):
                        sp.wait_ge(mask_made, 2 * (t - 1) if self_loops else t - 1)
                        sp.dma_start(links[:, t % 2, :], adj[t * P:(t + 1) * P, :]).then_inc(adj_in[t % 2], 16)
                else:
                    with sp.Fori(1, T) as t:
                        sp.wait_ge(mask_made, t)
                        sp.dma_start(links[:, 0, :], adj[bass.ts(t, P), :]).then_inc(adj_in[0], 16)

            @block.tensor
            def _(pe):
                pe.wait_ge(dst_w_ready, 1)
                for i in range(heads):
                    for j, (a, c) in enumerate(CHUNKS):
                        if i:
                            pe.wait_ge(dst_kept, 3 * (i - 1) + j + 1)
                        nc.tensor.matmul(core.ps[:, j, 0:c], dst_w[i * dh:(i + 1) * dh, :],
                                         hf[i * dh:(i + 1) * dh, a:a + c], start=True, stop=True).then_inc(dst_made, 1)

                def step(t, h):
                    if item := items.near(t, h, 0):
                        mixing.turn(pe, item)
                    if item := items.near(t, h, -1):
                        mixing.mix(pe, item)

                items.run(pe, step)

            @block.scalar
            def _(act):
                for i in range(heads):
                    for j, (a, c) in enumerate(CHUNKS):
                        act.wait_ge(dst_made, 3 * i + j + 1)
                        nc.scalar.activation(dst[:, i, a:a + c], core.ps[:, j, 0:c], ACT.Copy).then_inc(dst_kept, 1)
                act.wait_ge(ready, 1)

                def step(t, h):
                    if item := items.near(t, h, 0):
                        _, _, k, s = item
                        act.wait_ge(rectified, k + 1)
                        mixing.wait_probs_slot(act, k)
                        nc.scalar.activation(mixing.probs[:, s, 0:N], soft[:, s, :], ACT.Exp,
                                             bias=neg_max[:, bass.ds(k, 1)],
                                             accum_out=sums[:, bass.ds(k, 1)]).then_inc(mixing.probs_ready, 1)
                    if item := items.near(t, h, 1):
                        _, _, k, s = item
                        act.wait_ge(front, k + 1)
                        wait(act, mixing.probs_ready, k - 1)
                        nc.scalar.activation(soft[:, s, :], masked[:, s, :], ACT.Identity,
                                             bias=src_sl[:, bass.ds(k, 1)], scale=slope).then_inc(scaled, 1)
                    if item := items.near(t, h, -1):
                        mixing.keep(act, act_copy(nc), 0, item)

                items.run(act, step)

            @block.vector
            def _(dve):
                chain = Chain(nc, dve, steps)
                nc.vector.tensor_copy(dst_w[:], dst_col[:, 0:1].broadcast_to([P, P])).then_inc(dst_w_ready, 1)
                chain.link(nc.vector.tensor_tensor(tmp[:], ht[:], over_tiles(src_rep[:]), ALU.mult))
                chain.link(nc.vector.reduce_sum(src[:], tmp[:].rearrange("p t (h d) -> p (t h) d", h=heads), AX.X))
                chain.link(nc.vector.tensor_scalar(src_sl[:], src[:], slope, None, ALU.mult))
                chain.link(nc.vector.tensor_scalar(other[:], core.ident[:], -1.0, 1.0, ALU.mult, ALU.add))
                nc.vector.memset(mixing.probs[:, :, N:NP], 0.0).then_inc(ready, 1)
                dve.wait_ge(dst_kept, 3 * heads)

                def step(t, h):
                    per = 2 if self_loops else 1
                    later = items.near(t, h, 1)
                    if later and later[1] == 0:
                        ti, _, k, _ = later
                        sl = ti % 2 if slots == 2 else 0
                        wait(dve, maxed, k)
                        dve.wait_ge(adj_in[sl], 16 * (ti // 2 + 1 if slots == 2 else ti + 1))
                        nc.vector.tensor_scalar(mask[:], links[:, sl, :], 0.0, MASKED, unlinked,
                                                ALU.mult).then_inc(mask_made, 1)
                        if self_loops:
                            dve.wait_ge(mask_made, 2 * ti + 1)
                            nc.vector.tensor_tensor(mask[:, ti * P:(ti + 1) * P], mask[:, ti * P:(ti + 1) * P],
                                                    other[:], ALU.mult).then_inc(mask_made, 1)
                        dve.wait_ge(mask_made, per * (ti + 1))
                    if item := items.near(t, h, 0):
                        _, _, k, s = item
                        wait(dve, rectified, k)
                        dve.wait_ge(scaled, k + 1)
                        nc.vector.scalar_tensor_tensor(out=soft[:, s, :], in0=masked[:, s, :],
                                                       scalar=src[:, bass.ds(k, 1)], in1=soft[:, s, :], op0=ALU.add,
                                                       op1=ALU.max).then_inc(rectified, 1)
                    if later:
                        _, hi, k, s = later
                        nc.vector.tensor_tensor_reduce(masked[:, s, :], dst[:, hi, :], mask[:, 0:N], 1.0, -3e38,
                                                       ALU.add, ALU.max, row_max[:, s:s + 1]).then_inc(maxed, 1)
                        dve.wait_ge(maxed, k + 1)
                        nc.vector.tensor_scalar(neg_z[:, bass.ds(k, 1)], row_max[:, s:s + 1],
                                                src[:, bass.ds(k, 1)], -1.0, ALU.add, ALU.mult).then_inc(shifted, 1)
                        dve.wait_ge(shifted, k + 1)
                        nc.vector.scalar_tensor_tensor(out=neg_max[:, bass.ds(k, 1)], in0=neg_z[:, bass.ds(k, 1)],
                                                       scalar=slope, in1=neg_z[:, bass.ds(k, 1)], op0=ALU.mult,
                                                       op1=ALU.min).then_inc(front, 1)
                    if item := items.near(t, h, -1):
                        mixing.keep(dve, nc.vector.tensor_copy, 1, item)
                        mixing.keep(dve, nc.vector.tensor_copy, 2, item)
                    if item := items.near(t, h, -2):
                        mixing.take_out(dve, item, nc.vector.tensor_copy)

                items.run(dve, step)


def gat_norm_stage(core, name, heads, out, sums, gain_dram, shift_dram):
    nc = core.nc
    with ExitStack() as ctx:
        def sb(n, shape):
            return ctx.enter_context(nc.sbuf_tensor(f"{name}_{n}", shape, F32))

        centred, square, stats = sb("centred", [P, T, P]), sb("square", [P, T, P]), sb("stats", [P, 6, T])
        gain, shift, inv = sb("gain", [P, P]), sb("shift", [P, P]), sb("inv", [P, T * heads])
        steps, loaded, var_ready, root_ready, n_ready = core.sems(
            *[f"{name}_{s}" for s in ("steps", "loaded", "var_ready", "root_ready", "n_ready")])
        with nc.Block() as block:
            @block.sync
            def _(sp):
                sp.dma_start(gain[:], gain_dram.partition_broadcast(P)).then_inc(loaded, 16)
                sp.dma_start(shift[:], shift_dram.partition_broadcast(P)).then_inc(loaded, 16)

            @block.scalar
            def _(act):
                act.wait_ge(var_ready, 1)
                nc.scalar.activation(stats[:, 3, :], stats[:, 2, :], ACT.Sqrt).then_inc(root_ready, 1)

            @block.vector
            def _(dve):
                chain = Chain(nc, dve, steps)
                if sums is not None:
                    chain.link(nc.vector.reciprocal(inv[:], sums))
                    view = out.rearrange("p t (h d) -> p (t h) d", h=heads)
                    rep = inv[:].unsqueeze(2).broadcast_to([P, T * heads, P // heads])
                    chain.link(nc.vector.tensor_tensor(view, view, rep, ALU.mult))
                normalise(chain, dve, out, out, centred[:], square[:], stats, var_ready, root_ready, n_ready)
                dve.wait_ge(n_ready, 1)
                dve.wait_ge(loaded, 32)
                chain.link(nc.vector.tensor_tensor(out, out, over_tiles(gain[:]), ALU.mult))
                chain.link(nc.vector.tensor_tensor(out, out, over_tiles(shift[:]), ALU.add))
                chain.link(nc.vector.tensor_tensor(core.x[:], core.x[:], out, ALU.add))


def gat_sigmoid_stage(core, name, out, sums):
    nc = core.nc
    with ExitStack() as ctx:
        inv = ctx.enter_context(nc.sbuf_tensor(f"{name}_inv", [P, T], F32))
        steps, ratio_ready, exp_ready = core.sems(*[f"{name}_{s}" for s in ("steps", "ratio_ready", "exp_ready")])
        with nc.Block() as block:
            @block.vector
            def _(dve):
                chain = Chain(nc, dve, steps)
                chain.link(nc.vector.reciprocal(inv[:], sums))
                nc.vector.tensor_tensor(out, out, per_node(inv[:]), ALU.mult).then_inc(ratio_ready, 1)
                dve.wait_ge(exp_ready, 1)
                chain.link(nc.vector.tensor_scalar(out, out, 1.0, None, ALU.add))
                chain.link(nc.vector.reciprocal(out, out))
                chain.link(nc.vector.tensor_tensor(core.x[:], core.x[:], out, ALU.add))

            @block.scalar
            def _(act):
                act.wait_ge(ratio_ready, 1)
                nc.scalar.activation(out, out, ACT.Exp, scale=-1.0).then_inc(exp_ready, 1)


def gat_layer(core, h, layer):
    nc = core.nc
    heads = 4 if layer == 1 else 1
    name = f"g{layer}"
    with ExitStack() as ctx:
        out = ctx.enter_context(nc.sbuf_tensor(f"{name}_out", [P, T, P], F32))
        sums = ctx.enter_context(nc.sbuf_tensor(f"{name}_sums", [P, T * heads], F32))
        if layer == 1:
            a = h["g1_a"]
            graph_attention(core, name, heads, 0.2, h["adj"], h["g1_w"], None, a[0:32], a[32:64], out, sums,
                            ALU.is_le, False)
            gat_norm_stage(core, "g1n", heads, out[:], sums[:], h["g1_gain"], h["g1_shift"])
        else:
            s = h["g2_s"]
            graph_attention(core, name, heads, 0.01, h["adj"], h["g2_w"], h["g2_b"], s[0:P], s[P:2 * P], out, sums,
                            ALU.is_equal, True)
            gat_sigmoid_stage(core, "g2s", out[:], sums[:])


def masked_attention(core, h):
    nc = core.nc
    name, heads = "g3", 4
    dh = P // heads
    items = Items(heads)
    with ExitStack() as ctx:
        def sb(n, shape):
            return ctx.enter_context(nc.sbuf_tensor(f"{name}_{n}", shape, F32))

        w, wo = sb("w", [P, 3, P]), sb("wo", [P, P])
        qk_bias, v_bias, o_bias, gb = sb("qk_bias", [P, 2]), sb("v_bias", [P, P]), sb("o_bias", [P, P]), sb("gb", [P, 1])
        q, kf, v = sb("q", [P, NP]), sb("k", [P, NP]), sb("v", [P, T, P])
        out, outf, sums = sb("out", [P, T, P]), sb("outf", [P, NP]), sb("sums", [P, T * heads])
        inv = sb("inv", [P, T * heads])
        q_tile = sb("q_tile", [P, P])
        links, edge, bias = sb("links", [P, NP]), sb("edge", [P, N]), sb("bias", [P, N])
        scores = sb("scores", [P, 2, N])
        row_max, neg_max = sb("row_max", [P, 2]), sb("neg_max", [P, T * heads])
        b = h["g3_b"]
        project_stage(core, name, core.nf,
                      [(w[:], h["g3_w"].rearrange("p (c k) -> p c k", k=P)), (wo[:], h["g3_wo"]),
                       (qk_bias[:, 0:1], b[0:P].unsqueeze(1)), (qk_bias[:, 1:2], b[P:2 * P].unsqueeze(1)),
                       (v_bias[:], b[2 * P:3 * P].partition_broadcast(P)),
                       (o_bias[:], h["g3_bo"].partition_broadcast(P)),
                       (gb[:], h["g3_gb"].partition_broadcast(P))],
                      [(q, w[:, 0, :], 1.0, qk_bias[:, 0:1]), (kf, w[:, 1, :], 1.0, qk_bias[:, 1:2])],
                      [(v, w[:, 2, :], v_bias[:])])

        mixing = Mixing(core, ctx, name, items, lambda j, hd: v[:, j, hd * dh:(hd + 1) * dh], dh, out, dh)
        (q_scaled, q_set, ready, scored, adj_in, edge_made, bias_made, maxed, front) = core.sems(
            *[f"{name}_{s}" for s in ("q_scaled", "q_set", "ready", "scored", "adj_in", "edge_made", "bias_made",
                                      "maxed", "front")])
        with nc.Block() as block:
            @block.sync
            def _(sp):
                sp.dma_start(links[:], h["adj"][0:P, :]).then_inc(adj_in, 16)
                with sp.Fori(1, T) as t:
                    sp.wait_ge(bias_made, t)
                    sp.dma_start(links[:], h["adj"][bass.ts(t, P), :]).then_inc(adj_in, 16)

            @block.tensor
            def _(pe):
                def step(t, hd):
                    if item := items.near(t, hd, 1):
                        ti, hi, k, s = item
                        pe.wait_ge(q_set, ti + 1)
                        wait(pe, maxed, k)
                        for j, (a, c) in enumerate(CHUNKS):
                            mm = nc.tensor.matmul(core.ps[:, j, 0:c], q_tile[hi * dh:(hi + 1) * dh, :],
                                                  kf[hi * dh:(hi + 1) * dh, a:a + c], start=True, stop=True)
                        mm.then_inc(scored, 1)
                    if item := items.near(t, hd, 0):
                        mixing.turn(pe, item)
                    if item := items.near(t, hd, -1):
                        mixing.mix(pe, item)

                items.run(pe, step)

            @block.scalar
            def _(act):
                act.wait_ge(ready, 1)

                def step(t, hd):
                    item = items.near(t, hd, 1)
                    if item and item[1] == 0:
                        ti, _, k, _ = item
                        wait(act, scored, k)
                        nc.scalar.activation(q_tile[:], q[:, bass.ts(ti, P)], ACT.Copy,
                                             scale=float(dh) ** -0.5).then_inc(q_set, 1)
                    if item := items.near(t, hd, 0):
                        _, _, k, s = item
                        act.wait_ge(front, k + 1)
                        mixing.wait_probs_slot(act, k)
                        nc.scalar.activation(mixing.probs[:, s, 0:N], scores[:, s, :], ACT.Exp,
                                             bias=neg_max[:, bass.ds(k, 1)],
                                             accum_out=sums[:, bass.ds(k, 1)]).then_inc(mixing.probs_ready, 1)
                    if item := items.near(t, hd, -1):
                        mixing.keep(act, act_copy(nc), 0, item)
                        mixing.keep(act, act_copy(nc), 1, item)

                items.run(act, step)

            @block.vector
            def _(dve):
                nc.vector.memset(mixing.probs[:, :, N:NP], 0.0).then_inc(ready, 1)

                def step(t, hd):
                    later = items.near(t, hd, 1)
                    if later and later[1] == 0:
                        ti, _, k, _ = later
                        wait(dve, maxed, k)
                        dve.wait_ge(adj_in, 16 * (ti + 1))
                        nc.vector.tensor_scalar(edge[:], links[:, 0:N], 0.0, MASKED3, ALU.is_equal,
                                                ALU.mult).then_inc(edge_made, 1)
                        dve.wait_ge(edge_made, ti + 1)
                        nc.vector.scalar_tensor_tensor(out=bias[:], in0=links[:, 0:N], scalar=gb[:, 0:1],
                                                       in1=edge[:], op0=ALU.mult, op1=ALU.add).then_inc(bias_made, 1)
                    if item := items.near(t, hd, -1):
                        mixing.keep(dve, nc.vector.tensor_copy, 2, item)
                    if later:
                        ti, hi, k, s = later
                        dve.wait_ge(bias_made, ti + 1)
                        wait(dve, mixing.probs_ready, k - 1)
                        dve.wait_ge(scored, k + 1)
                    if item := items.near(t, hd, -2):
                        mixing.take_out(dve, item, nc.vector.tensor_copy)
                    if later:
                        nc.vector.tensor_tensor_reduce(scores[:, s, :], core.banks(0, 3, N), bias[:], 1.0, -3e38,
                                                       ALU.add, ALU.max, row_max[:, s:s + 1]).then_inc(maxed, 1)
                        dve.wait_ge(maxed, k + 1)
                        nc.vector.tensor_scalar(neg_max[:, bass.ds(k, 1)], row_max[:, s:s + 1], -1.0, None,
                                                ALU.mult).then_inc(front, 1)

                items.run(dve, step)

        steps, normed, turned, outf_ready, projected = core.sems(
            *[f"{name}o_{s}" for s in ("steps", "normed", "turned", "outf_ready", "projected")])
        with nc.Block() as block:
            @block.vector
            def _(dve):
                chain = Chain(nc, dve, steps)
                chain.link(nc.vector.reciprocal(inv[:], sums[:]))
                view = out[:].rearrange("p t (h d) -> p (t h) d", h=heads)
                rep = inv[:].unsqueeze(2).broadcast_to([P, T * heads, dh])
                nc.vector.tensor_tensor(view, view, rep, ALU.mult).then_inc(normed, 1)
                chain.link(nc.vector.tensor_tensor(core.x[:], core.x[:], over_tiles(o_bias[:]), ALU.add))
                for g, (a, b) in enumerate(GROUPS):
                    dve.wait_ge(projected, g + 1)
                    y = core.banks(3 + g, 1, (b - a) * P).rearrange("p (t c) -> p t c", c=P)
                    chain.link(nc.vector.tensor_tensor(core.x[:, a:b, :], core.x[:, a:b, :], y, ALU.add))

            @block.tensor
            def _(pe):
                pe.wait_ge(normed, 1)
                turn_tiles(pe, core, out, turned)
                for g, (a, b) in enumerate(GROUPS):
                    pe.wait_ge(outf_ready, g + 1)
                    for t in range(a, b):
                        mm = nc.tensor.matmul(core.ps[:, 3 + g, (t - a) * P:(t - a + 1) * P],
                                              outf[:, t * P:(t + 1) * P], wo[:], start=True, stop=True)
                    mm.then_inc(projected, 1)

            @block.scalar
            def _(act):
                for g, (a, w_) in enumerate(PCHUNKS):
                    act.wait_ge(turned, g + 1)
                    nc.scalar.activation(outf[:, a:a + w_], core.banks(g, 1, w_), ACT.Copy).then_inc(outf_ready, 1)


def scores_stage(core, name, feats, w, probs, sums):
    nc = core.nc
    da = w["w1"].shape[1]
    with ExitStack() as ctx:
        def sb(n, shape):
            return ctx.enter_context(nc.sbuf_tensor(f"{name}_{n}", shape, F32))

        w1, w2, w3 = sb("w1", [P, da]), sb("w2", [da, da]), sb("w3", [P, da])
        low, q, kf = sb("low", [da, NP]), sb("q", [da, NP]), sb("k", [da, NP])
        neg_max = sb("neg_max", [P, T])
        loaded, low_made, q_made, k_made, low_kept, q_kept, k_kept, scored, maxed, shifted, done = core.sems(
            *[f"{name}_{s}" for s in ("loaded", "low_made", "q_made", "k_made", "low_kept", "q_kept", "k_kept",
                                      "scored", "maxed", "shifted", "done")])
        with nc.Block() as block:
            @block.sync
            def _(sp):
                for dst, src in ((w1, w["w1"]), (w2, w["w2"]), (w3, w["w3"])):
                    sp.dma_start(dst[:], src).then_inc(loaded, 16)

            @block.tensor
            def _(pe):
                pe.wait_ge(loaded, 48)
                for j, (a, c) in enumerate(PCHUNKS):
                    nc.tensor.matmul(core.ps[0:da, j, 0:c], w1[:], feats[:, a:a + c], start=True,
                                     stop=True).then_inc(low_made, 1)
                for j, (a, c) in enumerate(PCHUNKS):
                    nc.tensor.matmul(core.ps[0:da, 3 + j, 0:c], w3[:], feats[:, a:a + c], start=True,
                                     stop=True).then_inc(k_made, 1)
                for j, (a, c) in enumerate(PCHUNKS):
                    pe.wait_ge(low_kept, j + 1)
                    nc.tensor.matmul(core.ps[0:da, j, 0:c], w2[:], low[:, a:a + c], start=True,
                                     stop=True).then_inc(q_made, 1)
                pe.wait_ge(q_kept, 3)
                pe.wait_ge(k_kept, 3)
                for t in range(T):
                    wait(pe, done, t - 1)
                    for j, (a, c) in enumerate(CHUNKS):
                        mm = nc.tensor.matmul(core.ps[:, 3 * (t % 2) + j, 0:c], q[:, t * P:(t + 1) * P],
                                              kf[:, a:a + c], start=True, stop=True)
                    mm.then_inc(scored, 1)

            @block.scalar
            def _(act):
                for j, (a, c) in enumerate(PCHUNKS):
                    act.wait_ge(low_made, j + 1)
                    nc.scalar.activation(low[:, a:a + c], core.ps[0:da, j, 0:c], ACT.Copy).then_inc(low_kept, 1)
                for j, (a, c) in enumerate(PCHUNKS):
                    act.wait_ge(q_made, j + 1)
                    nc.scalar.activation(q[:, a:a + c], core.ps[0:da, j, 0:c], ACT.Copy).then_inc(q_kept, 1)
                for t in range(T):
                    act.wait_ge(maxed, t + 1)
                    s = core.banks(3 * (t % 2), 3, N)
                    nc.scalar.activation(probs[:, t, 0:N], s, ACT.Exp, bias=neg_max[:, t:t + 1],
                                         accum_out=sums[:, t:t + 1]).then_inc(done, 1)

            @block.vector
            def _(dve):
                for j, (a, c) in enumerate(PCHUNKS):
                    dve.wait_ge(k_made, j + 1)
                    nc.vector.tensor_copy(kf[:, a:a + c], core.ps[0:da, 3 + j, 0:c]).then_inc(k_kept, 1)
                for t in range(T):
                    dve.wait_ge(scored, t + 1)
                    nc.vector.tensor_reduce(neg_max[:, t:t + 1], core.banks(3 * (t % 2), 3, N), AX.X, ALU.max,
                                            negate=True).then_inc(maxed, 1)


def top_p_stage(core, name, halvings, rounds, probs, sums, adj_t, xf, spread, xa, mixed_xa):
    nc = core.nc
    all_rounds = -(-N // 8)
    last = N - (T - 1) * P
    items = Items(1)
    with ExitStack() as ctx:
        def sb(n, shape, dtype=F32):
            return ctx.enter_context(nc.sbuf_tensor(f"{name}_{n}", shape, dtype))

        low, middle, mass, room, flags = [sb(n, [P, T]) for n in ("low", "middle", "mass", "room", "flags")]
        below = sb("below", [P, T, NP])
        ratio = sb("ratio", [P, halvings])
        product = below[:, 0, 0:N]
        largest, keep = sb("largest", [P, T, 8]), sb("keep", [P, T, 8])
        before = sb("before", [P, T, 9])
        any_row, any_turned, any_block = sb("any_row", [P, 32]), sb("any_turned", [P, 32]), sb("any_block", [P, 1])
        open_rows = sb("open_rows", [P, 1], mybir.dt.int32)
        pause = sb("pause", [P, 2])
        block_in = sb("adj_t", [P, 2, T, P])
        mixing = Mixing(core, ctx, name, items, lambda j, h: xa[:, j, :], P + 1, mixed_xa, P + 1,
                        lambda t, s: probs[:, t, :])
        steps, halved, general, set_up, a_in0, a_in1, mixed, spread_kept = core.sems(
            *[f"{name}_{s}" for s in ("steps", "halved", "general", "set_up", "a_in0", "a_in1", "mixed",
                                      "spread_kept")])
        a_in = [a_in0, a_in1]
        with nc.Block() as block:
            @block.sync
            def _(sp):
                for t in range(T):
                    wait(sp, mixed, t - 1)
                    sp.dma_start(block_in[:, t % 2], adj_t[t]).then_inc(a_in[t % 2], 16)

            @block.tensor
            def _(pe):
                for t in range(T):
                    pe.wait_ge(a_in[t % 2], 16 * (t // 2 + 1))
                    wait(pe, spread_kept, t - 1)
                    for j in range(T):
                        mm = nc.tensor.matmul(core.ps[:, t % 2, 0:P + 1], block_in[:, t % 2, j, :], xf[:, j, :],
                                              start=(j == 0), stop=(j == T - 1))
                    mm.then_inc(mixed, 1)

                def step(t, h):
                    if item := items.near(t, h, 0):
                        mixing.turn(pe, item)
                    if item := items.near(t, h, -1):
                        mixing.mix(pe, item)

                items.run(pe, step)

            @block.scalar
            def _(act):
                for t in range(T):
                    act.wait_ge(mixed, t + 1)
                    nc.scalar.activation(spread[:, t, :], core.ps[:, t % 2, 0:P + 1], ACT.Copy).then_inc(spread_kept, 1)

                def step(t, h):
                    if item := items.near(t, h, 0):
                        for g in range(3):
                            mixing.keep(act, act_copy(nc), g, item)
                    if item := items.near(t, h, -1):
                        mixing.take_out(act, item, act_copy(nc))

                items.run(act, step)

            @block.vector
            def _(dve):
                chain = Chain(nc, dve, steps)
                for i in range(halvings):
                    nc.vector.memset(ratio[:, i:i + 1], math.exp(REACH / 2 ** (i + 1))).then_inc(set_up, 1)
                nc.vector.memset(low[:], math.exp(-REACH)).then_inc(set_up, 1)
                nc.vector.memset(any_row[:], 0.0).then_inc(set_up, 1)
                nc.vector.memset(flags[:], 0.0).then_inc(set_up, 1)
                nc.vector.memset(before[:, :, 8:9], 0.0).then_inc(set_up, 1)
                nc.vector.memset(below[:, :, N:NP], 0.0).then_inc(set_up, 1)
                nc.vector.tensor_scalar(room[:], sums[:], TOP_P, None, ALU.mult).then_inc(set_up, 1)
                nc.vector.memset(pause[:], 0.0).then_inc(set_up, 1)
                dve.wait_ge(set_up, halvings + 7)
                per = T + 4
                with dve.Fori(0, halvings) as i:
                    at = [0]

                    def link(ins):
                        at[0] += 1
                        ins.then_inc(halved, 1)
                        dve.wait_ge(halved, i * per + at[0])

                    link(nc.vector.tensor_scalar(middle[:], low[:], ratio[:, bass.ds(i, 1)], None, ALU.mult))
                    for t in range(T):
                        link(nc.vector.scalar_tensor_tensor(out=product, in0=probs[:, t, 0:N],
                                                            scalar=middle[:, t:t + 1], in1=probs[:, t, 0:N],
                                                            op0=ALU.is_gt, op1=ALU.mult,
                                                            accum_out=mass[:, t:t + 1]))
                    link(nc.vector.tensor_tensor(mass[:], mass[:], room[:], ALU.is_ge))
                    link(nc.vector.tensor_tensor(middle[:], middle[:], mass[:], ALU.mult))
                    link(nc.vector.tensor_tensor(low[:], low[:], middle[:], ALU.max))
                    assert at[0] == per

                chain.link(nc.vector.tensor_scalar(middle[:], low[:], math.exp(REACH / 2 ** halvings), None, ALU.mult))
                for t in range(T):
                    chain.link(nc.vector.scalar_tensor_tensor(out=below[:, t, 0:N], in0=probs[:, t, 0:N],
                                                              scalar=middle[:, t:t + 1], in1=probs[:, t, 0:N],
                                                              op0=ALU.is_le, op1=ALU.mult,
                                                              accum_out=mass[:, t:t + 1]))
                chain.link(nc.vector.tensor_tensor(mass[:], mass[:], sums[:], ALU.subtract))
                chain.link(nc.vector.tensor_tensor(room[:], room[:], mass[:], ALU.add))

                def take_round(link):
                    for t in range(T):
                        link(nc.vector.max(largest[:, t, :], below[:, t, :]))
                    link(nc.vector.tensor_copy(before[:, :, 0:1], before[:, :, 8:9]))
                    for i in range(8):
                        link(nc.vector.tensor_tensor(before[:, :, i + 1:i + 2], before[:, :, i:i + 1],
                                                     largest[:, :, i:i + 1], ALU.add))
                    rep = room[:].unsqueeze(2).broadcast_to([P, T, 8])
                    link(nc.vector.tensor_tensor(keep[:], before[:, :, 0:8], rep, ALU.is_lt))
                    link(nc.vector.tensor_tensor(largest[:], largest[:], keep[:], ALU.mult))
                    for t in range(T):
                        link(nc.vector.match_replace(below[:, t, :], largest[:, t, :], below[:, t, :], 0.0))

                for _ in range(rounds):
                    take_round(chain.link)
                chain.link(nc.vector.tensor_tensor(flags[:, 0:T - 1], before[:, 0:T - 1, 8], room[:, 0:T - 1],
                                                   ALU.is_lt))
                chain.link(nc.vector.tensor_tensor(flags[0:last, T - 1:T], before[0:last, T - 1, 8:9],
                                                   room[0:last, T - 1:T], ALU.is_lt))
                chain.link(nc.vector.reduce_max(any_row[:, 0:1], flags[:], AX.X))
                chain.link(nc.vector.transpose(any_turned[:], any_row[:]))
                chain.link(nc.vector.reduce_max(any_block[:], any_turned[:], AX.X))
                chain.link(nc.vector.tensor_copy(open_rows[:], any_block[:]))
                still_open = [dve.value_load(open_rows[b:b + 1, 0:1], min_val=0, max_val=1) for b in range(0, P, 32)]
                with dve.If(sum(still_open[1:], still_open[0]) > 0):
                    with dve.Fori(0, all_rounds - rounds) as i:
                        at = [0]
                        per_round = 2 * (2 * T + 11)

                        def link(ins):
                            ins.then_inc(general, 1)
                            dve.wait_ge(general, i * per_round + at[0] + 1)
                            nc.vector.tensor_copy(pause[:, 1:2], pause[:, 0:1]).then_inc(general, 1)
                            at[0] += 2

                        take_round(link)
                        assert at[0] == per_round
                for t in range(T):
                    nc.vector.tensor_tensor(probs[:, t, 0:N], probs[:, t, 0:N], below[:, t, 0:N],
                                            ALU.subtract).then_inc(mixing.probs_ready, 1)


def update_stage(core, name, z, xa, xf, mixed_xa, spread, u1, u2, xaf):
    nc = core.nc
    with ExitStack() as ctx:
        def sb(n, shape):
            return ctx.enter_context(nc.sbuf_tensor(f"{name}_{n}", shape, F32))

        w1, w2, xff = sb("w1", [P, P]), sb("w2", [P, P]), sb("xff", [P, NP])
        inv = sb("inv", [P, T])
        loaded, steps, mixed_ready, turned, kept, z_made = core.sems(
            *[f"{name}_{s}" for s in ("loaded", "steps", "mixed_ready", "turned", "kept", "z_made")])
        with nc.Block() as block:
            @block.sync
            def _(sp):
                sp.dma_start(w1[:], u1).then_inc(loaded, 16)
                sp.dma_start(w2[:], u2).then_inc(loaded, 16)

            @block.vector
            def _(dve):
                chain = Chain(nc, dve, steps)
                chain.link(nc.vector.reciprocal(inv[:], mixed_xa[:, :, P]))
                nc.vector.tensor_tensor(xa[:, :, 0:P], mixed_xa[:, :, 0:P], per_node(inv[:]),
                                        ALU.mult).then_inc(mixed_ready, 1)
                chain.link(nc.vector.tensor_tensor(spread[:], spread[:], xf[:], ALU.add))
                chain.link(nc.vector.reciprocal(inv[:], spread[:, :, P]))
                dve.wait_ge(mixed_ready, 1)
                nc.vector.tensor_tensor(xf[:, :, 0:P], spread[:, :, 0:P], per_node(inv[:]),
                                        ALU.mult).then_inc(mixed_ready, 1)
                for g, (a, b) in enumerate(GROUPS):
                    dve.wait_ge(z_made, g + 1)
                    y = core.banks(g, 1, (b - a) * P).rearrange("p (t c) -> p t c", c=P)
                    chain.link(nc.vector.tensor_tensor(z[:, a:b, :], z[:, a:b, :], y, ALU.add))

            @block.tensor
            def _(pe):
                pe.wait_ge(mixed_ready, 1)
                turn_tiles(pe, core, xa[:, :, 0:P], turned)
                pe.wait_ge(mixed_ready, 2)
                turn_tiles(pe, core, xf[:, :, 0:P], turned, 3)
                pe.wait_ge(loaded, 32)
                pe.wait_ge(kept, 6)
                for g, (a, b) in enumerate(GROUPS):
                    for t in range(a, b):
                        o = core.ps[:, g, (t - a) * P:(t - a + 1) * P]
                        nc.tensor.matmul(o, xff[:, t * P:(t + 1) * P], w1[:], start=True, stop=False)
                        mm = nc.tensor.matmul(o, xaf[:, t * P:(t + 1) * P], w2[:], start=False, stop=True)
                    mm.then_inc(z_made, 1)

            @block.scalar
            def _(act):
                for i, dst in enumerate((xaf, xff)):
                    for g, (a, w) in enumerate(PCHUNKS):
                        act.wait_ge(turned, 3 * i + g + 1)
                        nc.scalar.activation(dst[:, a:a + w], core.banks(3 * i + g, 1, w), ACT.Copy).then_inc(kept, 1)


def propagation_layer(core, h):
    nc = core.nc
    with ExitStack() as ctx:
        def sb(n, shape):
            return ctx.enter_context(nc.sbuf_tensor(f"g0_{n}", shape, F32))

        z = sb("z", [P, T, P])
        with ExitStack() as inner:
            def sbi(n, shape):
                return inner.enter_context(nc.sbuf_tensor(f"g0_{n}", shape, F32))

            xa, xf, mixed_xa, spread = [sbi(n, [P, T, P + 1]) for n in ("xa", "xf", "mixed_xa", "spread")]
            xaf = sbi("xaf", [P, NP])
            probs, sums = sbi("probs", [P, T, NP]), sbi("sums", [P, T])
            started = core.sem("g0_started")
            with nc.Block() as block:
                @block.vector
                def _(dve):
                    nc.vector.memset(xa[:, :, P:P + 1], 1.0).then_inc(started, 1)
                    nc.vector.memset(xf[:, :, P:P + 1], 1.0).then_inc(started, 1)
                    nc.vector.memset(probs[:, :, N:NP], 0.0).then_inc(started, 1)
                    nc.vector.tensor_copy(z[:], core.n[:]).then_inc(started, 1)
                    nc.vector.tensor_copy(xa[:, :, 0:P], core.n[:]).then_inc(started, 1)
                    nc.vector.tensor_copy(xf[:, :, 0:P], core.n[:]).then_inc(started, 1)

            w = {"w1": h["g0_w1"], "w2": h["g0_w2"], "w3": h["g0_w3"]}
            for n in range(STEPS):
                scores_stage(core, f"g0l{n}", core.nf if n == 0 else xaf, w, probs, sums)
                top_p_stage(core, f"g0p{n}", HALVINGS[n], ROUNDS[n], probs, sums, h["adj_t"], xf, spread, xa, mixed_xa)
                update_stage(core, f"g0u{n}", z, xa, xf, mixed_xa, spread, h["g0_u1"][n], h["g0_u2"][n], xaf)
                core.recycle()
        gat_norm_stage(core, "g0n", 1, z[:], None, h["g0_gain"], h["g0_shift"])


def load_stage(core, x, identity):
    nc = core.nc
    loaded, cleared = core.sems("x_loaded", "x_cleared")
    with nc.Block() as block:
        @block.vector
        def _(dve):
            nc.vector.memset(core.x[:, T - 1, :], 0.0).then_inc(cleared, 1)

        @block.sync
        def _(sp):
            full = (T - 1) * P
            sp.dma_start(core.x[:, 0:T - 1, :], x[0:full, :].rearrange("(t p) d -> p t d", p=P)).then_inc(loaded, 16)
            sp.dma_start(core.ident[:], identity).then_inc(loaded, 16)
            sp.wait_ge(cleared, 1)
            sp.dma_start(core.x[0:N - full, T - 1, :], x[full:N, :]).then_inc(loaded, 16)
            sp.wait_ge(loaded, 48)


def store_stage(core, out):
    nc = core.nc
    stored = core.sem("stored")
    with nc.Block() as block:
        @block.sync
        def _(sp):
            full = (T - 1) * P
            sp.dma_start(out[0:full, :].rearrange("(t p) d -> p t d", p=P), core.x[:, 0:T - 1, :]).then_inc(stored, 16)
            sp.dma_start(out[full:N, :], core.x[0:N - full, T - 1, :]).then_inc(stored, 16)
            sp.wait_ge(stored, 32)


def program(nc, h, out, only=None):
    with ExitStack() as ctx:
        core = Core(nc, ctx)
        comb = ctx.enter_context(nc.sbuf_tensor("comb", [P, T, 8], F32))
        load_stage(core, h["x"], h["identity"])

        def run(layer):
            return only is None or layer in only

        if run("g0"):
            layernorm_stage(core, "ln0g")
            propagation_layer(core, h)
            core.recycle()
        if run("f0"):
            layernorm_stage(core, "ln0f")
            router_stage(core, "r0", 8, h["f0_wr"], None, h["f0_b2"], comb, False, True, 0, core.nf, core.n[:])
            ffn_stage(core, "f0", 8, 1, ACT.Gelu, h["f0_w1"], h["f0_b1"], h["f0_w2"], comb, core.nf)
            core.recycle()
        if run("g1"):
            layernorm_stage(core, "ln1g")
            gat_layer(core, h, 1)
            core.recycle()
        if run("f1"):
            layernorm_stage(core, "ln1f")
            router_stage(core, "r1", 4, h["f1_wr"], h["f1_br"], h["f1_b3"], comb, True, False, 1, core.nf, None)
            deep_ffn_stage(core, "f1", 5, h["f1_w1"], h["f1_b1"], h["f1_w2"], h["f1_b2"], h["f1_w3"], comb, core.nf)
            core.recycle()
        if run("g2"):
            layernorm_stage(core, "ln2g")
            gat_layer(core, h, 2)
            core.recycle()
        if run("f2"):
            layernorm_stage(core, "ln2f", (h["f2_gamma"], h["f2_beta"]))
            router_stage(core, "r2", 8, h["f2_wr"], h["f2_br"], h["f2_b2"], comb, False, False, 0, core.nf, None)
            ffn_stage(core, "f2", 8, 2, ACT.Gelu, h["f2_w1"], h["f2_b1"], h["f2_w2"], comb, core.nf)
            core.recycle()
        if run("g3"):
            layernorm_stage(core, "ln3g")
            masked_attention(core, h)
            core.recycle()
        if run("f3"):
            layernorm_stage(core, "ln3f")
            router_stage(core, "r3", 8, h["f3_wr"], h["f3_br"], h["f3_b2"], comb, False, False, 0, core.nf, None)
            ffn_stage(core, "f3", 8, 4, ACT.Relu, h["f3_w1"], h["f3_b1"], h["f3_w2"], comb, core.nf)
        store_stage(core, out)


def kernel(**inputs):
    import numpy as np
    import concourse.bacc as bacc
    from concourse.bass_utils import run_bass_kernel_spmd

    i = {k: np.asarray(v) for k, v in inputs.items()}
    adj = np.zeros((NP, NP), np.float32)
    adj[0:N, 0:N] = i["adj"]
    adj[N:, 0] = 1.0

    def hidden_bias(b):
        return b.reshape(b.shape[0], -1, P).transpose(0, 2, 1)

    def second(w):
        return w.reshape(w.shape[0], -1, P, w.shape[2]).transpose(0, 2, 1, 3)

    ew2 = np.zeros((4, P, P), np.float32)
    ew2[:, :, 0:64] = i["L1_ffn_eW2"]
    ew3 = np.zeros((4, P, P), np.float32)
    ew3[:, 0:64, :] = i["L1_ffn_eW3"]
    eb2 = np.zeros((4, P), np.float32)
    eb2[:, 0:64] = i["L1_ffn_eb2"]

    def five(experts, shared):
        return np.concatenate([experts, shared[None]]).transpose(1, 0, 2)

    a = {
        "x": i["x"],
        "identity": np.eye(P, dtype=np.float32),
        "adj": adj,
        "adj_t": adj.reshape(T, P, T, P).transpose(0, 3, 2, 1),
        "g0_w1": i["L0_gnn_W1"].T, "g0_w2": i["L0_gnn_W2"].T, "g0_w3": i["L0_gnn_W3"].T,
        "g0_u1": i["L0_gnn_U1"].transpose(0, 2, 1), "g0_u2": i["L0_gnn_U2"].transpose(0, 2, 1),
        "g0_gain": i["L0_gnn_ln_g"], "g0_shift": i["L0_gnn_ln_b"],
        "f0_wr": i["L0_ffn_router_w"].T, "f0_w1": i["L0_ffn_w1"], "f0_b1": hidden_bias(i["L0_ffn_b1"]),
        "f0_w2": second(i["L0_ffn_w2"]), "f0_b2": i["L0_ffn_b2"],
        "g1_w": i["L1_gnn_W"], "g1_a": i["L1_gnn_a"][:, 0], "g1_gain": i["L1_gnn_gamma"],
        "g1_shift": i["L1_gnn_beta"],
        "f1_wr": i["L1_ffn_gW"], "f1_br": i["L1_ffn_gb"],
        "f1_w1": five(i["L1_ffn_eW1"], i["L1_ffn_sW1"]), "f1_w2": five(ew2, i["L1_ffn_sW2"]),
        "f1_w3": five(ew3, i["L1_ffn_sW3"]),
        "f1_b1": np.concatenate([i["L1_ffn_eb1"], i["L1_ffn_sb1"][None]]).T,
        "f1_b2": np.concatenate([eb2, i["L1_ffn_sb2"][None]]).T,
        "f1_b3": np.concatenate([i["L1_ffn_eb3"], i["L1_ffn_sb3"][None]]),
        "g2_w": i["L2_gnn_W"].T, "g2_b": i["L2_gnn_b"], "g2_s": i["L2_gnn_S"],
        "f2_gamma": i["L2_ffn_gamma"][:, None], "f2_beta": i["L2_ffn_beta"][:, None],
        "f2_wr": i["L2_ffn_Wr"], "f2_br": i["L2_ffn_br"], "f2_w1": i["L2_ffn_W1"],
        "f2_b1": hidden_bias(i["L2_ffn_b1"]), "f2_w2": second(i["L2_ffn_W2"]), "f2_b2": i["L2_ffn_b2"],
        "g3_w": i["L3_gnn_Wqkv"], "g3_b": i["L3_gnn_bqkv"], "g3_wo": i["L3_gnn_Wout"],
        "g3_bo": i["L3_gnn_bout"], "g3_gb": i["L3_gnn_graph_bias"].reshape(1),
        "f3_wr": i["L3_ffn_Wg"].T, "f3_br": i["L3_ffn_bg"], "f3_w1": i["L3_ffn_W1"].transpose(0, 2, 1),
        "f3_b1": hidden_bias(i["L3_ffn_b1"]), "f3_w2": second(i["L3_ffn_W2"].transpose(0, 2, 1)),
        "f3_b2": i["L3_ffn_b2"],
    }
    a = {f"in_{k}": np.ascontiguousarray(v) for k, v in a.items()}
    nc = bacc.Bacc("TRN2", target_bir_lowering=False, num_devices=1)
    h = {k[3:]: nc.dram_tensor(k, v.shape, F32, kind="ExternalInput").ap() for k, v in a.items()}
    out = nc.dram_tensor("out", (N, P), F32, kind="ExternalOutput").ap()
    program(nc, h, out)
    r = run_bass_kernel_spmd(nc, [a], core_ids=[0])
    return r.results[0]["out"]
```

```python
import math
from contextlib import ExitStack

import concourse.bass as bass
from concourse import mybir

F32 = mybir.dt.float32
ALU = mybir.AluOpType
ACT = mybir.ActivationFunctionType
AX = mybir.AxisListType

P = 128
N = 1354
T = (N + P - 1) // P
NP = T * P
BANK = 512
CHUNKS = [(0, 512), (512, 512), (1024, N - 1024)]
PCHUNKS = [(0, 512), (512, 512), (1024, NP - 1024)]
GROUPS = [(0, 4), (4, 8), (8, T)]
PARTS = [(0, T)]
BY_ACT = 4
EPS = 1e-5
MASKED = -9e15
MASKED3 = -1e9
TOP_P = 0.9
STEPS = 2
HALVINGS = (4, 5)
ROUNDS = (1, 2)
REACH = 5.6


class Core:

    def __init__(self, nc, ctx):
        self.nc = nc
        self.used = []
        self.ps = ctx.enter_context(nc.psum_tensor("psum", [P, 8, BANK], F32))

        def sb(name, shape):
            return ctx.enter_context(nc.sbuf_tensor(name, shape, F32))

        self.x = sb("x", [P, T, P])
        self.n = sb("n", [P, T, P])
        self.nf = sb("nf", [P, NP])
        self.ident = sb("ident", [P, P])

    def sem(self, name):
        s = self.nc.alloc_semaphore(name)
        self.used.append(s)
        return s

    def sems(self, *names):
        return [self.sem(n) for n in names]

    def recycle(self):
        self.nc.clear_and_free_semaphores(self.used)
        self.nc.all_engine_barrier()
        self.used = []

    def banks(self, first, count, columns):
        return self.ps[:, first:first + count, :].rearrange("p b c -> p (b c)")[:, 0:columns]


class Chain:

    def __init__(self, nc, engine, sem):
        self.nc, self.engine, self.sem, self.count = nc, engine, sem, 0

    def link(self, ins):
        self.mark(ins)
        self.engine.wait_ge(self.sem, self.count)

    def mark(self, ins):
        self.count += 1
        ins.then_inc(self.sem, 1)


def per_node(column):
    return column.unsqueeze(2).broadcast_to([P, T, P])


def over_tiles(row, width=P):
    return row.unsqueeze(1).broadcast_to([P, T, width])


def normalise(chain, dve, out, src, centred, square, stats, var_ready, root_ready, n_ready):
    nc = chain.nc
    total, neg_mean, var, root, rstd, t1 = [stats[:, i, :] for i in range(6)]
    chain.link(nc.vector.reduce_sum(total, src, AX.X))
    chain.link(nc.vector.tensor_scalar(neg_mean, total, -1.0 / P, None, ALU.mult))
    chain.link(nc.vector.tensor_tensor(centred, src, per_node(neg_mean), ALU.add))
    chain.link(nc.vector.tensor_tensor(square, centred, centred, ALU.mult))
    chain.link(nc.vector.reduce_sum(total, square, AX.X))
    nc.vector.tensor_scalar(var, total, 1.0 / P, EPS, ALU.mult, ALU.add).then_inc(var_ready, 1)
    dve.wait_ge(var_ready, 1)
    dve.wait_ge(root_ready, 1)
    chain.link(nc.vector.reciprocal(rstd, root))
    chain.link(nc.vector.tensor_tensor(t1, rstd, rstd, ALU.mult))
    chain.link(nc.vector.tensor_tensor(t1, t1, var, ALU.mult))
    chain.link(nc.vector.tensor_scalar(t1, t1, -0.5, 1.5, ALU.mult, ALU.add))
    chain.link(nc.vector.tensor_tensor(rstd, rstd, t1, ALU.mult))
    nc.vector.tensor_tensor(out, centred, per_node(rstd), ALU.mult).then_inc(n_ready, 1)


def turn_tiles(pe, core, src, turned, first_bank=0):
    nc = core.nc
    for g, (a, b) in enumerate(GROUPS):
        for t in range(a, b):
            mm = nc.tensor.transpose(core.ps[:, first_bank + g, (t - a) * P:(t - a + 1) * P],
                                     src[:, t, :], core.ident[:])
        mm.then_inc(turned, 1)


def layernorm_stage(core, name, affine=None, prefetch=None):
    nc = core.nc
    by_dve = 5
    scaled_by_dve = {0, 1, 2, 4, 5, 6, 8, 9}
    with ExitStack() as ctx:
        def sb(n, shape):
            return ctx.enter_context(nc.sbuf_tensor(f"{name}_{n}", shape, F32))

        centred, square = sb("centred", [P, by_dve, P]), sb("square", [P, T, P])
        total, neg_mean, sums, var, root, rstd, t1, shift = [sb(f"stat{i}", [P, T]) for i in range(8)]
        gain = sb("gain", [P, 2])
        (steps, mean_ready, squared, var_ready, root_ready, rstd_ready, scaled_dve, scaled_act, turned, nf_ready,
         loaded) = core.sems(*[f"{name}_{s}" for s in (
             "steps", "mean_ready", "squared", "var_ready", "root_ready", "rstd_ready", "scaled_dve",
             "scaled_act", "turned", "nf_ready", "affine")])
        with nc.Block() as block:
            @block.vector
            def _(dve):
                chain = Chain(nc, dve, steps)
                some = slice(0, by_dve)
                chain.link(nc.vector.reduce_sum(total[:], core.x[:], AX.X))
                nc.vector.tensor_scalar(neg_mean[:], total[:], -1.0 / P, None, ALU.mult).then_inc(mean_ready, 1)
                dve.wait_ge(mean_ready, 1)
                rep = neg_mean[:, some].unsqueeze(2).broadcast_to([P, by_dve, P])
                chain.link(nc.vector.tensor_tensor(centred[:], core.x[:, some, :], rep, ALU.add))
                chain.link(nc.vector.tensor_tensor(square[:, some, :], centred[:], centred[:], ALU.mult))
                chain.link(nc.vector.reduce_sum(sums[:, some], square[:, some, :], AX.X))
                dve.wait_ge(squared, 1 + T - by_dve)
                nc.vector.tensor_scalar(var[:], sums[:], 1.0 / P, EPS, ALU.mult, ALU.add).then_inc(var_ready, 1)
                dve.wait_ge(var_ready, 1)
                dve.wait_ge(root_ready, 1)
                chain.link(nc.vector.reciprocal(rstd[:], root[:]))
                chain.link(nc.vector.tensor_tensor(t1[:], rstd[:], rstd[:], ALU.mult))
                chain.link(nc.vector.tensor_tensor(t1[:], t1[:], var[:], ALU.mult))
                chain.link(nc.vector.tensor_scalar(t1[:], t1[:], -0.5, 1.5, ALU.mult, ALU.add))
                chain.link(nc.vector.tensor_tensor(rstd[:], rstd[:], t1[:], ALU.mult))
                nc.vector.tensor_tensor(shift[:], neg_mean[:], rstd[:], ALU.mult).then_inc(rstd_ready, 1)
                dve.wait_ge(rstd_ready, 1)
                for t in sorted(scaled_by_dve):
                    nc.vector.tensor_scalar(core.n[:, t, :], core.x[:, t, :], rstd[:, t:t + 1], shift[:, t:t + 1],
                                            ALU.mult, ALU.add).then_inc(scaled_dve, 1)
                a, w = PCHUNKS[2]
                dve.wait_ge(turned, 3)
                if affine is None:
                    nc.vector.tensor_copy(core.nf[:, a:a + w], core.banks(2, 1, w)).then_inc(nf_ready, 1)
                else:
                    dve.wait_ge(loaded, 32)
                    nc.vector.tensor_scalar(core.nf[:, a:a + w], core.banks(2, 1, w), gain[:, 0:1], gain[:, 1:2],
                                            ALU.mult, ALU.add).then_inc(nf_ready, 1)

            @block.sync
            def _(sp):
                if affine is not None:
                    for i in range(2):
                        sp.dma_start(gain[:, i:i + 1], affine[i]).then_inc(loaded, 16)
                if prefetch is not None:
                    prefetch(sp)

            @block.scalar
            def _(act):
                nc.scalar.activation(root[:, 0:1], core.ident[:, 0:1], ACT.Sqrt).then_inc(squared, 1)
                act.wait_ge(squared, 1)
                act.wait_ge(mean_ready, 1)
                for t in range(by_dve, T):
                    nc.scalar.activation(square[:, t, :], core.x[:, t, :], ACT.Square, bias=neg_mean[:, t:t + 1],
                                         accum_out=sums[:, t:t + 1]).then_inc(squared, 1)
                act.wait_ge(var_ready, 1)
                nc.scalar.activation(root[:], var[:], ACT.Sqrt).then_inc(root_ready, 1)
                act.wait_ge(rstd_ready, 1)
                for t in range(T):
                    if t not in scaled_by_dve:
                        nc.scalar.activation(core.n[:, t, :], core.x[:, t, :], ACT.Identity, bias=shift[:, t:t + 1],
                                             scale=rstd[:, t:t + 1]).then_inc(scaled_act, 1)
                for g in range(2):
                    act.wait_ge(turned, g + 1)
                    a, w = PCHUNKS[g]
                    if affine is None:
                        nc.scalar.activation(core.nf[:, a:a + w], core.banks(g, 1, w), ACT.Copy).then_inc(nf_ready, 1)
                    else:
                        act.wait_ge(loaded, 32)
                        nc.scalar.activation(core.nf[:, a:a + w], core.banks(g, 1, w), ACT.Identity,
                                             bias=gain[:, 1:2], scale=gain[:, 0:1]).then_inc(nf_ready, 1)

            @block.tensor
            def _(pe):
                for g, (a, b) in enumerate(GROUPS):
                    for t in range(a, b):
                        done = len([i for i in scaled_by_dve if i <= t])
                        if t in scaled_by_dve:
                            pe.wait_ge(scaled_dve, done)
                        else:
                            pe.wait_ge(scaled_act, t + 1 - done)
                        mm = nc.tensor.transpose(core.ps[:, g, (t - a) * P:(t - a + 1) * P], core.n[:, t, :],
                                                 core.ident[:])
                    mm.then_inc(turned, 1)


def first_of_equals(chain, nc, eq, count, experts):
    chain.link(nc.vector.tensor_copy(count, eq))
    for e in range(1, experts):
        chain.link(nc.vector.tensor_tensor(count[:, :, e:e + 1], count[:, :, e:e + 1],
                                           count[:, :, e - 1:e], ALU.add))
    chain.link(nc.vector.tensor_scalar(count, count, 1.0, None, ALU.is_equal))
    chain.link(nc.vector.tensor_tensor(eq, eq, count, ALU.mult))


class Router:

    LOGITS, OUT = 7, 4

    def __init__(self, core, ctx, name, experts, wr, bias, b_out, comb, second_softmax, add_n, extra, feats):
        self.core, self.nc, self.experts, self.cols = core, core.nc, experts, experts + extra
        self.comb, self.second_softmax, self.add_n, self.extra, self.feats = comb, second_softmax, add_n, extra, feats

        def sb(n, shape):
            return ctx.enter_context(core.nc.sbuf_tensor(f"{name}_{n}", shape, F32))

        self.w, self.bo = sb("router_w", [P, experts]), sb("b_out", [self.cols, P])
        self.brow = sb("router_b", [P, experts]) if bias is not None else None
        self.combt = sb("comb_t", [self.cols, NP])
        self.scratch = [sb(f"lg{i}", [P, T, experts]) for i in range(6)]
        self.stats = [sb(f"st{i}", [P, T]) for i in range(8)]
        (self.loaded, self.logits_made, self.steps, self.exp_in, self.exp_out, self.comb_ready, self.turned,
         self.combt_ready, self.biased, self.bias_added) = core.sems(
            *[f"{name}_{s}" for s in ("loaded", "logits", "rsteps", "exp_in", "exp_out", "comb_ready",
                                      "comb_turned", "combt_ready", "bias_out", "bias_added")])
        self.loads = [(self.w[:], wr), (self.bo[:], b_out)]
        if bias is not None:
            self.loads.append((self.brow[:], bias.partition_broadcast(P)))

    def load(self, sp):
        for dst, src in self.loads:
            sp.dma_start(dst, src).then_inc(self.loaded, 16)

    def logits(self, pe):
        pe.wait_ge(self.loaded, 16 * len(self.loads))
        for t in range(T):
            mm = self.nc.tensor.matmul(self.core.ps[:, self.LOGITS, t * self.experts:(t + 1) * self.experts],
                                       self.feats[:, t * P:(t + 1) * P], self.w[:], start=True, stop=True)
        mm.then_inc(self.logits_made, 1)

    def turn(self, pe):
        pe.wait_ge(self.comb_ready, 1)
        for g, (a, b) in enumerate(GROUPS):
            for t in range(a, b):
                mm = self.nc.tensor.transpose(
                    self.core.ps[0:self.cols, self.OUT + g, (t - a) * P:(t - a + 1) * P],
                    self.comb[:, t, 0:self.cols], self.core.ident[:])
            mm.then_inc(self.turned, 1)

    def biases(self, pe):
        for g, (a, b) in enumerate(GROUPS):
            pe.wait_ge(self.combt_ready, g + 1)
            for t in range(a, b):
                mm = self.nc.tensor.matmul(self.core.ps[:, self.OUT + g, (t - a) * P:(t - a + 1) * P],
                                           self.combt[:, t * P:(t + 1) * P], self.bo[:], start=True, stop=True)
            mm.then_inc(self.biased, 1)

    def exponentials(self, act):
        pr, lg2 = self.scratch[5], self.scratch[1]
        d, e2 = self.stats[2], self.stats[3]
        if self.second_softmax:
            act.wait_ge(self.exp_in, 1)
            self.nc.scalar.activation(pr[:], lg2[:], ACT.Exp).then_inc(self.exp_out, 1)
        act.wait_ge(self.exp_in, 1 + self.second_softmax)
        self.nc.scalar.activation(e2[:], d[:], ACT.Exp).then_inc(self.exp_out, 1)

    def keep(self, act):
        for g, (a, wd) in enumerate(PCHUNKS):
            act.wait_ge(self.turned, g + 1)
            self.nc.scalar.activation(self.combt[:, a:a + wd], self.core.ps[0:self.cols, self.OUT + g, 0:wd],
                                      ACT.Copy).then_inc(self.combt_ready, 1)

    def choose(self, dve):
        nc, core, comb, experts, cols = self.nc, self.core, self.comb, self.experts, self.cols
        lg, lg2, eq1, eq2, cnt, pr = self.scratch
        m1, m2, d, e2, w1, w2, sm, rs = self.stats

        def bc(col):
            return col.unsqueeze(2).broadcast_to([P, T, experts])

        chain = self.chain = Chain(nc, dve, self.steps)
        dve.wait_ge(self.logits_made, 1)
        raw = core.ps[:, self.LOGITS, 0:T * experts].rearrange("p (t e) -> p t e", e=experts)
        if self.brow is not None:
            dve.wait_ge(self.loaded, 16 * len(self.loads))
            chain.link(nc.vector.tensor_tensor(lg[:], raw, over_tiles(self.brow[:], experts), ALU.add))
        else:
            chain.link(nc.vector.tensor_copy(lg[:], raw))
        if self.second_softmax:
            chain.link(nc.vector.reduce_max(m1[:], lg[:], AX.X))
            nc.vector.tensor_tensor(lg2[:], lg[:], bc(m1[:]), ALU.subtract).then_inc(self.exp_in, 1)
            dve.wait_ge(self.exp_out, 1)
            chain.link(nc.vector.reduce_sum(sm[:], pr[:], AX.X))
            chain.link(nc.vector.reciprocal(rs[:], sm[:]))
            chain.link(nc.vector.tensor_tensor(lg[:], pr[:], bc(rs[:]), ALU.mult))
        chain.link(nc.vector.reduce_max(m1[:], lg[:], AX.X))
        chain.link(nc.vector.tensor_tensor(eq1[:], lg[:], bc(m1[:]), ALU.is_equal))
        first_of_equals(chain, nc, eq1[:], cnt[:], experts)
        chain.link(nc.vector.scalar_tensor_tensor(out=lg2[:], in0=eq1[:], scalar=-1e30, in1=lg[:],
                                                  op0=ALU.mult, op1=ALU.add))
        chain.link(nc.vector.reduce_max(m2[:], lg2[:], AX.X))
        nc.vector.tensor_tensor(d[:], m2[:], m1[:], ALU.subtract).then_inc(self.exp_in, 1)
        chain.link(nc.vector.tensor_tensor(eq2[:], lg2[:], bc(m2[:]), ALU.is_equal))
        first_of_equals(chain, nc, eq2[:], cnt[:], experts)
        dve.wait_ge(self.exp_out, 1 + self.second_softmax)
        chain.link(nc.vector.tensor_scalar(sm[:], e2[:], 1.0, None, ALU.add))
        chain.link(nc.vector.reciprocal(w1[:], sm[:]))
        chain.link(nc.vector.tensor_tensor(w2[:], w1[:], e2[:], ALU.mult))
        chain.link(nc.vector.tensor_tensor(eq1[:], eq1[:], bc(w1[:]), ALU.mult))
        chain.link(nc.vector.tensor_tensor(eq2[:], eq2[:], bc(w2[:]), ALU.mult))
        if self.extra:
            chain.link(nc.vector.memset(comb[:, :, experts:cols], 1.0))
        nc.vector.tensor_tensor(comb[:, :, 0:experts], eq1[:], eq2[:], ALU.add).then_inc(self.comb_ready, 1)
        if self.add_n:
            chain.link(nc.vector.tensor_tensor(core.x[:], core.x[:], core.n[:], ALU.add))

    def add_biases(self, dve):
        for g, (a, b) in enumerate(GROUPS):
            dve.wait_ge(self.biased, g + 1)
            y = self.core.banks(self.OUT + g, 1, (b - a) * P).rearrange("p (t c) -> p t c", c=P)
            self.nc.vector.tensor_tensor(self.core.x[:, a:b, :], self.core.x[:, a:b, :], y,
                                         ALU.add).then_inc(self.bias_added, 1)


def ffn_stage(core, name, affine, router_inputs, experts, parts, func, w1, b1, w2, comb, feats):
    nc = core.nc
    HB, YB = 0, 4
    U = 3 * parts
    with ExitStack() as ctx:
        def sb(n, shape):
            return ctx.enter_context(nc.sbuf_tensor(f"{name}_{n}", shape, F32))

        router = Router(core, ctx, *router_inputs)
        w1s, w2s = sb("w1s", [P, experts, parts, P]), sb("w2s", [P, experts, parts, P])
        b1s = sb("b1s", [P, experts, parts])
        hid = sb("hid", [P, 2, parts, NP])
        b_in, h_made, h_kept, y_made, y_added = core.sems(
            *[f"{name}_{s}" for s in ("b_in", "h_made", "h_kept", "y_made", "y_added")])
        w_in = core.sems(*[f"{name}_w_in{e}" for e in range(experts)])

        def load(sp):
            router.load(sp)
            sp.dma_start(b1s[:], b1).then_inc(b_in, 16)
            for e in range(experts):
                sp.dma_start(w1s[:, e], w1[e].rearrange("p (c k) -> p c k", k=P)).then_inc(w_in[e], 16)
                sp.dma_start(w2s[:, e], w2[e]).then_inc(w_in[e], 16)

        layernorm_stage(core, f"{name}_ln", affine, load)
        with nc.Block() as block:
            @block.tensor
            def _(pe):
                def hidden(e):
                    pe.wait_ge(w_in[e], 32)
                    for c in range(parts):
                        for j, (a, w) in enumerate(PCHUNKS):
                            u = e * U + 3 * c + j
                            if u >= 4:
                                pe.wait_ge(h_kept, u - 3)
                            nc.tensor.matmul(core.ps[:, HB + u % 4, 0:w], w1s[:, e, c, :], feats[:, a:a + w],
                                             start=True, stop=True).then_inc(h_made, 1)

                def output(e):
                    pe.wait_ge(h_kept, (e + 1) * U)
                    for g, (a, b) in enumerate(GROUPS):
                        if e >= 1:
                            pe.wait_ge(y_added, 3 * (e - 1) + g + 1)
                        else:
                            pe.wait_ge(router.bias_added, g + 1)
                        for t in range(a, b):
                            for c in range(parts):
                                mm = nc.tensor.matmul(core.ps[:, YB + g, (t - a) * P:(t - a + 1) * P],
                                                      hid[:, e % 2, c, t * P:(t + 1) * P], w2s[:, e, c, :],
                                                      start=(c == 0), stop=(c == parts - 1))
                        mm.then_inc(y_made, 1)

                router.logits(pe)
                hidden(0)
                hidden(1)
                router.turn(pe)
                router.biases(pe)
                for e in range(experts):
                    output(e)
                    if e + 2 < experts:
                        hidden(e + 2)

            @block.scalar
            def _(act):
                act.wait_ge(b_in, 16)
                for e in range(experts):
                    if e >= 2:
                        act.wait_ge(y_made, 3 * (e - 1))
                    for c in range(parts):
                        for j, (a, w) in enumerate(PCHUNKS):
                            u = e * U + 3 * c + j
                            act.wait_ge(h_made, u + 1)
                            nc.scalar.activation(hid[:, e % 2, c, a:a + w], core.ps[:, HB + u % 4, 0:w], func,
                                                 bias=b1s[:, e, c:c + 1]).then_inc(h_kept, 1)
                    if e == 0:
                        router.exponentials(act)
                    if e == 1:
                        router.keep(act)

            @block.vector
            def _(dve):
                router.choose(dve)
                router.add_biases(dve)
                for e in range(experts):
                    for g, (a, b) in enumerate(GROUPS):
                        dve.wait_ge(y_made, 3 * e + g + 1)
                        if e >= 1:
                            dve.wait_ge(y_added, 3 * (e - 1) + g + 1)
                        else:
                            dve.wait_ge(router.comb_ready, 1)
                            dve.wait_ge(router.bias_added, g + 1)
                        for t in range(a, b):
                            add = nc.vector.scalar_tensor_tensor(
                                out=core.x[:, t, :], in0=core.ps[:, YB + g, (t - a) * P:(t - a + 1) * P],
                                scalar=comb[:, t, e:e + 1], in1=core.x[:, t, :], op0=ALU.mult, op1=ALU.add)
                        add.then_inc(y_added, 1)


def deep_ffn_stage(core, name, router_inputs, experts, w1, b1, w2, b2, w3, comb, feats):
    nc = core.nc
    with ExitStack() as ctx:
        def sb(n, shape):
            return ctx.enter_context(nc.sbuf_tensor(f"{name}_{n}", shape, F32))

        router = Router(core, ctx, *router_inputs)
        w1s, w2s, w3s = [sb(n, [P, experts, P]) for n in ("w1s", "w2s", "w3s")]
        b1s, b2s = sb("b1s", [P, experts]), sb("b2s", [P, experts])
        h1, h2 = sb("h1", [P, 2, NP]), sb("h2", [P, 2, NP])
        loaded, h1_made, h1_kept, h2_made, h2_kept, y_made, y_added = core.sems(
            *[f"{name}_{s}" for s in ("loaded", "h1_made", "h1_kept", "h2_made", "h2_kept", "y_made", "y_added")])
        loads = [(w1s, w1), (w2s, w2), (w3s, w3), (b1s, b1), (b2s, b2)]
        HB, YB = 0, 4
        order = [(1, 0)]
        for e in range(experts):
            order += [(1, e + 1)] * (e + 1 < experts) + [(2, e)]
        at = {le: 3 * i for i, le in enumerate(order)}

        def load(sp):
            router.load(sp)
            for dst, src in loads:
                sp.dma_start(dst[:], src).then_inc(loaded, 16)

        layernorm_stage(core, f"{name}_ln", None, load)
        with nc.Block() as block:
            @block.tensor
            def _(pe):
                router.logits(pe)
                pe.wait_ge(loaded, 16 * len(loads))

                def free_bank(u):
                    if u >= 4:
                        layer, e = order[(u - 4) // 3]
                        pe.wait_ge(h1_kept if layer == 1 else h2_kept, 3 * e + (u - 4) % 3 + 1)

                def layer1(e):
                    for j, (a, w) in enumerate(PCHUNKS):
                        u = at[1, e] + j
                        free_bank(u)
                        nc.tensor.matmul(core.ps[:, HB + u % 4, 0:w], w1s[:, e, :], feats[:, a:a + w],
                                         start=True, stop=True).then_inc(h1_made, 1)

                def layer2(e):
                    for j, (a, w) in enumerate(PCHUNKS):
                        u = at[2, e] + j
                        free_bank(u)
                        pe.wait_ge(h1_kept, 3 * e + j + 1)
                        nc.tensor.matmul(core.ps[:, HB + u % 4, 0:w], w2s[:, e, :], h1[:, e % 2, a:a + w],
                                         start=True, stop=True).then_inc(h2_made, 1)

                def layer3(e):
                    for g, (a, b) in enumerate(GROUPS):
                        pe.wait_ge(h2_kept, 3 * e + g + 1)
                        if e >= 1:
                            pe.wait_ge(y_added, 3 * (e - 1) + g + 1)
                        else:
                            pe.wait_ge(router.bias_added, g + 1)
                        for t in range(a, b):
                            mm = nc.tensor.matmul(core.ps[:, YB + g, (t - a) * P:(t - a + 1) * P],
                                                  h2[:, e % 2, t * P:(t + 1) * P], w3s[:, e, :],
                                                  start=True, stop=True)
                        mm.then_inc(y_made, 1)

                layer1(0)
                for e in range(experts):
                    if e + 1 < experts:
                        layer1(e + 1)
                    layer2(e)
                    if e == 0:
                        router.turn(pe)
                        router.biases(pe)
                    if e >= 1:
                        layer3(e - 1)
                layer3(experts - 1)

            @block.scalar
            def _(act):
                act.wait_ge(loaded, 16 * len(loads))
                for layer, e in order:
                    made, kept, b, h = (h1_made, h1_kept, b1s, h1) if layer == 1 else (h2_made, h2_kept, b2s, h2)
                    if e >= 2:
                        if layer == 1:
                            act.wait_ge(h2_made, 3 * (e - 1))
                        else:
                            act.wait_ge(y_made, 3 * (e - 1))
                    for j, (a, w) in enumerate(PCHUNKS):
                        act.wait_ge(made, 3 * e + j + 1)
                        nc.scalar.activation(h[:, e % 2, a:a + w], core.ps[:, HB + (at[layer, e] + j) % 4, 0:w],
                                             ACT.Relu, bias=b[:, e:e + 1]).then_inc(kept, 1)
                    if (layer, e) == (1, 1):
                        router.exponentials(act)
                    if (layer, e) == (2, 0):
                        router.keep(act)

            @block.vector
            def _(dve):
                router.choose(dve)
                router.add_biases(dve)
                for e in range(experts):
                    for g, (a, b) in enumerate(GROUPS):
                        dve.wait_ge(y_made, 3 * e + g + 1)
                        if e >= 1:
                            dve.wait_ge(y_added, 3 * (e - 1) + g + 1)
                        else:
                            dve.wait_ge(router.comb_ready, 1)
                            dve.wait_ge(router.bias_added, g + 1)
                        for t in range(a, b):
                            add = nc.vector.scalar_tensor_tensor(
                                out=core.x[:, t, :], in0=core.ps[:, YB + g, (t - a) * P:(t - a + 1) * P],
                                scalar=comb[:, t, e:e + 1], in1=core.x[:, t, :], op0=ALU.mult, op1=ALU.add)
                        add.then_inc(y_added, 1)


def wait(engine, sem, value):
    if not isinstance(value, int) or value > 0:
        engine.wait_ge(sem, value)


class Items:

    def __init__(self, heads):
        self.heads, self.count = heads, heads * T

    def near(self, t, h, d):
        t, h = t + (h + d) // self.heads, (h + d) % self.heads
        if isinstance(t, int) and not 0 <= t < T:
            return None
        return t, h, t * self.heads + h, (h if self.heads > 1 else t) % 2

    def run(self, engine, step):
        step(-1, self.heads - 1)
        if self.heads > 1:
            for h in range(self.heads):
                step(0, h)
            with engine.Fori(1, T - 1) as t:
                for h in range(self.heads):
                    step(t, h)
            for h in range(self.heads):
                step(T - 1, h)
        else:
            for t in range(T):
                step(t, 0)
        step(T, 0)
        step(T + 1 // self.heads, 1 % self.heads)


class Mixing:

    TURN, OUT = 3, 6

    def __init__(self, core, ctx, name, items, values, width, out, out_width, source=None):
        nc = self.nc = core.nc
        self.core, self.items, self.values, self.width = core, items, values, width
        self.out, self.out_width = out, out_width
        if source is None:
            self.probs = ctx.enter_context(nc.sbuf_tensor(f"{name}_probs", [P, 2, NP], F32))
        self.source = source or (lambda t, s: self.probs[:, s, :])
        self.turned_probs = ctx.enter_context(nc.sbuf_tensor(f"{name}_turned_probs", [P, 2, NP], F32))
        (self.probs_ready, self.turned, self.out_made, self.out_read,
         *self.kept) = core.sems(*[f"{name}_{s}" for s in ("probs_ready", "turned", "out_made", "out_read",
                                                           "kept0", "kept1", "kept2")])

    def wait_probs_slot(self, engine, k):
        wait(engine, self.turned, 3 * (k - 1))

    def turn(self, pe, item):
        t, h, k, s = item
        pe.wait_ge(self.probs_ready, k + 1)
        for g, (a, b) in enumerate(GROUPS):
            wait(pe, self.kept[g], k)
            for j in range(a, b):
                mm = self.nc.tensor.transpose(self.core.ps[:, self.TURN + g, (j - a) * P:(j - a + 1) * P],
                                              self.source(t, s)[:, j * P:(j + 1) * P], self.core.ident[:])
            mm.then_inc(self.turned, 1)

    def keep(self, engine, copy, g, item):
        t, h, k, s = item
        wait(engine, self.out_made, k - 1)
        engine.wait_ge(self.turned, 3 * k + g + 1)
        a, w = PCHUNKS[g]
        copy(self.turned_probs[:, s, a:a + w], self.core.ps[:, self.TURN + g, 0:w]).then_inc(self.kept[g], 1)

    def mix(self, pe, item):
        t, h, k, s = item
        wait(pe, self.out_read, k - 1)
        for j in range(T):
            for g, (a, _) in enumerate(GROUPS):
                if j == a:
                    pe.wait_ge(self.kept[g], k + 1)
            mm = self.nc.tensor.matmul(self.core.ps[:, self.OUT + s, 0:self.width],
                                       self.turned_probs[:, s, j * P:(j + 1) * P], self.values(j, h),
                                       start=(j == 0), stop=(j == T - 1))
        mm.then_inc(self.out_made, 1)

    def take_out(self, engine, item, copy):
        t, h, k, s = item
        engine.wait_ge(self.out_made, k + 1)
        w = self.out_width
        copy(self.out[:, t, h * w:(h + 1) * w], self.core.ps[:, self.OUT + s, 0:w]).then_inc(self.out_read, 1)


def act_copy(nc):
    return lambda out, src: nc.scalar.activation(out, src, ACT.Copy)


def project_stage(core, name, feats, loads, by_feature, by_node):
    nc = core.nc
    loaded, made, kept, node_made, node_kept = core.sems(
        *[f"{name}_{s}" for s in ("loaded", "made", "kept", "node_made", "node_kept")])

    def load(sp):
        for dst, src in loads:
            sp.dma_start(dst, src).then_inc(loaded, 16)

    layernorm_stage(core, f"{name}_ln", None, load)
    with nc.Block() as block:
        @block.tensor
        def _(pe):
            pe.wait_ge(loaded, 16 * len(loads))
            for i, (out, w, scale, bias) in enumerate(by_feature):
                for j, (a, c) in enumerate(PCHUNKS):
                    if i:
                        pe.wait_ge(kept, 3 * (i - 1) + j + 1)
                    nc.tensor.matmul(core.ps[:, j, 0:c], w, feats[:, a:a + c], start=True, stop=True).then_inc(made, 1)
            for i, (out, w, bias) in enumerate(by_node):
                for g, (a, b) in enumerate(GROUPS):
                    if i:
                        pe.wait_ge(node_kept, 3 * (i - 1) + g + 1)
                    for t in range(a, b):
                        mm = nc.tensor.matmul(core.ps[:, 3 + g, (t - a) * P:(t - a + 1) * P],
                                              feats[:, t * P:(t + 1) * P], w, start=True, stop=True)
                    mm.then_inc(node_made, 1)

        @block.scalar
        def _(act):
            act.wait_ge(loaded, 16 * len(loads))
            for i, (out, w, scale, bias) in enumerate(by_feature):
                for j, (a, c) in enumerate(PCHUNKS):
                    act.wait_ge(made, 3 * i + j + 1)
                    if bias is None:
                        nc.scalar.activation(out[:, a:a + c], core.ps[:, j, 0:c], ACT.Copy, scale=scale).then_inc(kept, 1)
                    else:
                        nc.scalar.activation(out[:, a:a + c], core.ps[:, j, 0:c], ACT.Identity,
                                             bias=bias).then_inc(kept, 1)

        @block.vector
        def _(dve):
            dve.wait_ge(loaded, 16 * len(loads))
            for i, (out, w, bias) in enumerate(by_node):
                for g, (a, b) in enumerate(GROUPS):
                    dve.wait_ge(node_made, 3 * i + g + 1)
                    y = core.banks(3 + g, 1, (b - a) * P).rearrange("p (t c) -> p t c", c=P)
                    if bias is None:
                        nc.vector.tensor_copy(out[:, a:b, 0:P], y).then_inc(node_kept, 1)
                    else:
                        rep = bias.unsqueeze(1).broadcast_to([P, b - a, P])
                        nc.vector.tensor_tensor(out[:, a:b, 0:P], y, rep, ALU.add).then_inc(node_kept, 1)


def graph_attention(core, name, heads, slope, adj, w_dram, bias_dram, a_src, a_dst, out, sums, unlinked, self_loops):
    nc = core.nc
    dh = P // heads
    items = Items(heads)
    with ExitStack() as ctx:
        def sb(n, shape):
            return ctx.enter_context(nc.sbuf_tensor(f"{name}_{n}", shape, F32))

        w = sb("w", [P, P])
        bias_col, bias_rep = sb("bias_col", [P, 1]), sb("bias_rep", [P, P])
        src_rep, dst_col, dst_w = sb("src_rep", [P, P]), sb("dst_col", [P, 1]), sb("dst_w", [P, P])
        hf, ht, tmp = sb("hf", [P, NP]), sb("ht", [P, T, P]), sb("tmp", [P, T, P])
        dst = sb("dst", [P, heads, N])
        src, src_sl = sb("src", [P, T * heads]), sb("src_sl", [P, T * heads])
        other = sb("other", [P, P])
        slots = 2 if heads == 1 else 1
        links = sb("links", [P, slots, NP])
        mask = sb("mask", [P, NP])
        masked, soft = sb("masked", [P, 2, N]), sb("soft", [P, 2, N])
        row_max = sb("row_max", [P, 2])
        neg_z, neg_max = [sb(n, [P, T * heads]) for n in ("neg_z", "neg_max")]

        loads = [(w[:], w_dram)]
        for i in range(heads):
            loads.append((src_rep[:, i * dh:(i + 1) * dh], a_src.partition_broadcast(P)))
            loads.append((dst_col[i * dh:(i + 1) * dh, :], a_dst.unsqueeze(1)))
        if bias_dram is not None:
            loads.append((bias_col[:], bias_dram.unsqueeze(1)))
            loads.append((bias_rep[:], bias_dram.partition_broadcast(P)))
        project_stage(core, name, core.nf, loads,
                      [(hf, w[:], 1.0, bias_col[:, 0:1] if bias_dram is not None else None)],
                      [(ht, w[:], bias_rep[:] if bias_dram is not None else None)])

        mixing = Mixing(core, ctx, name, items, lambda j, h: ht[:, j, h * dh:(h + 1) * dh], dh, out, dh)
        adj_in = core.sems(*[f"{name}_adj_in{i}" for i in range(slots)])
        (steps, dst_w_ready, dst_made, dst_kept, ready, mask_made, maxed, shifted, front, scaled,
         rectified) = core.sems(*[f"{name}_{s}" for s in (
             "steps", "dst_w_ready", "dst_made", "dst_kept", "ready", "mask_made", "maxed", "shifted",
             "front", "scaled", "rectified")])

        with nc.Block() as block:
            @block.sync
            def _(sp):
                sp.dma_start(links[:, 0, :], adj[0:P, :]).then_inc(adj_in[0], 16)
                if slots == 2:
                    sp.dma_start(links[:, 1, :], adj[P:2 * P, :]).then_inc(adj_in[1], 16)
                    for t in range(2, T):
                        sp.wait_ge(mask_made, 2 * (t - 1) if self_loops else t - 1)
                        sp.dma_start(links[:, t % 2, :], adj[t * P:(t + 1) * P, :]).then_inc(adj_in[t % 2], 16)
                else:
                    with sp.Fori(1, T) as t:
                        sp.wait_ge(mask_made, t)
                        sp.dma_start(links[:, 0, :], adj[bass.ts(t, P), :]).then_inc(adj_in[0], 16)

            @block.tensor
            def _(pe):
                pe.wait_ge(dst_w_ready, 1)
                for i in range(heads):
                    for j, (a, c) in enumerate(CHUNKS):
                        if i:
                            pe.wait_ge(dst_kept, 3 * (i - 1) + j + 1)
                        nc.tensor.matmul(core.ps[:, j, 0:c], dst_w[i * dh:(i + 1) * dh, :],
                                         hf[i * dh:(i + 1) * dh, a:a + c], start=True, stop=True).then_inc(dst_made, 1)

                def step(t, h):
                    if item := items.near(t, h, 0):
                        mixing.turn(pe, item)
                    if item := items.near(t, h, -1):
                        mixing.mix(pe, item)

                items.run(pe, step)

            @block.scalar
            def _(act):
                for i in range(heads):
                    for j, (a, c) in enumerate(CHUNKS):
                        act.wait_ge(dst_made, 3 * i + j + 1)
                        nc.scalar.activation(dst[:, i, a:a + c], core.ps[:, j, 0:c], ACT.Copy).then_inc(dst_kept, 1)
                act.wait_ge(ready, 1)

                def step(t, h):
                    if item := items.near(t, h, 0):
                        _, _, k, s = item
                        act.wait_ge(rectified, k + 1)
                        mixing.wait_probs_slot(act, k)
                        nc.scalar.activation(mixing.probs[:, s, 0:N], soft[:, s, :], ACT.Exp,
                                             bias=neg_max[:, bass.ds(k, 1)],
                                             accum_out=sums[:, bass.ds(k, 1)]).then_inc(mixing.probs_ready, 1)
                    if item := items.near(t, h, 1):
                        _, _, k, s = item
                        act.wait_ge(front, k + 1)
                        wait(act, mixing.probs_ready, k - 1)
                        nc.scalar.activation(soft[:, s, :], masked[:, s, :], ACT.Identity,
                                             bias=src_sl[:, bass.ds(k, 1)], scale=slope).then_inc(scaled, 1)
                    if item := items.near(t, h, -1):
                        mixing.keep(act, act_copy(nc), 0, item)

                items.run(act, step)

            @block.vector
            def _(dve):
                chain = Chain(nc, dve, steps)
                nc.vector.tensor_copy(dst_w[:], dst_col[:, 0:1].broadcast_to([P, P])).then_inc(dst_w_ready, 1)
                chain.link(nc.vector.tensor_tensor(tmp[:], ht[:], over_tiles(src_rep[:]), ALU.mult))
                chain.link(nc.vector.reduce_sum(src[:], tmp[:].rearrange("p t (h d) -> p (t h) d", h=heads), AX.X))
                chain.link(nc.vector.tensor_scalar(src_sl[:], src[:], slope, None, ALU.mult))
                chain.link(nc.vector.tensor_scalar(other[:], core.ident[:], -1.0, 1.0, ALU.mult, ALU.add))
                nc.vector.memset(mixing.probs[:, :, N:NP], 0.0).then_inc(ready, 1)
                dve.wait_ge(dst_kept, 3 * heads)

                def step(t, h):
                    per = 2 if self_loops else 1
                    later = items.near(t, h, 1)
                    if later and later[1] == 0:
                        ti, _, k, _ = later
                        sl = ti % 2 if slots == 2 else 0
                        wait(dve, maxed, k)
                        dve.wait_ge(adj_in[sl], 16 * (ti // 2 + 1 if slots == 2 else ti + 1))
                        nc.vector.tensor_scalar(mask[:], links[:, sl, :], 0.0, MASKED, unlinked,
                                                ALU.mult).then_inc(mask_made, 1)
                        if self_loops:
                            dve.wait_ge(mask_made, 2 * ti + 1)
                            nc.vector.tensor_tensor(mask[:, ti * P:(ti + 1) * P], mask[:, ti * P:(ti + 1) * P],
                                                    other[:], ALU.mult).then_inc(mask_made, 1)
                        dve.wait_ge(mask_made, per * (ti + 1))
                    if item := items.near(t, h, 0):
                        _, _, k, s = item
                        wait(dve, rectified, k)
                        dve.wait_ge(scaled, k + 1)
                        nc.vector.scalar_tensor_tensor(out=soft[:, s, :], in0=masked[:, s, :],
                                                       scalar=src[:, bass.ds(k, 1)], in1=soft[:, s, :], op0=ALU.add,
                                                       op1=ALU.max).then_inc(rectified, 1)
                    if later:
                        _, hi, k, s = later
                        nc.vector.tensor_tensor_reduce(masked[:, s, :], dst[:, hi, :], mask[:, 0:N], 1.0, -3e38,
                                                       ALU.add, ALU.max, row_max[:, s:s + 1]).then_inc(maxed, 1)
                        dve.wait_ge(maxed, k + 1)
                        nc.vector.tensor_scalar(neg_z[:, bass.ds(k, 1)], row_max[:, s:s + 1],
                                                src[:, bass.ds(k, 1)], -1.0, ALU.add, ALU.mult).then_inc(shifted, 1)
                        dve.wait_ge(shifted, k + 1)
                        nc.vector.scalar_tensor_tensor(out=neg_max[:, bass.ds(k, 1)], in0=neg_z[:, bass.ds(k, 1)],
                                                       scalar=slope, in1=neg_z[:, bass.ds(k, 1)], op0=ALU.mult,
                                                       op1=ALU.min).then_inc(front, 1)
                    if item := items.near(t, h, -1):
                        mixing.keep(dve, nc.vector.tensor_copy, 1, item)
                        mixing.keep(dve, nc.vector.tensor_copy, 2, item)
                    if item := items.near(t, h, -2):
                        mixing.take_out(dve, item, nc.vector.tensor_copy)

                items.run(dve, step)


def four_head_attention(core, h, out, sums):
    nc = core.nc
    name, heads, slope = "g1", 4, 0.2
    dh = P // heads
    dv = dh + 1
    last = N - (T - 1) * P
    slots = 4
    rows = 2 * heads
    pieces = [(i, a, w) for i in range(2) for a, w in CHUNKS]
    with ExitStack() as ctx:
        def sb(n, shape, stack=ctx):
            return stack.enter_context(nc.sbuf_tensor(f"{name}_{n}", shape, F32))

        w = sb("w", [P, P])
        src_rep, dst_rep, dst_col, dst_w = (sb("src_rep", [P, P]), sb("dst_rep", [P, P]), sb("dst_col", [P, 1]),
                                            sb("dst_w", [P, P]))
        ht, v = sb("ht", [P, T, P]), sb("v", [P, T, heads, dv])
        src, dst_node, dst_slope = [sb(n, [P, T * heads]) for n in ("src", "dst_node", "dst_slope")]
        row_max, score_max = sb("row_max", [P, T * heads]), sb("score_max", [P, T * heads])
        shifts, shift_rows = sb("shifts", [P, T, rows]), sb("shift_rows", [rows, NP])
        select = sb("select", [rows, rows, P])
        no_links, value_sum = sb("no_links", [P, T]), sb("value_sum", [P, P])
        ones = sb("ones", [P, P])
        links_t = sb("links_t", [P, T, NP])
        a_src, a_dst = h["g1_a"][0:dh], h["g1_a"][dh:2 * dh]
        (steps, dst_w_ready, dst_made, dst_kept, mask_made, maxed, links_t_in, shifts_ready, shifts_turned,
         shifts_kept, sum_made, adj_in0, adj_in1) = core.sems(*[f"{name}_{s}" for s in (
             "steps", "dst_w_ready", "dst_made", "dst_kept", "mask_made", "maxed", "links_t_in", "shifts_ready",
             "shifts_turned", "shifts_kept", "sum_made", "adj_in0", "adj_in1")])
        adj_in = [adj_in0, adj_in1]

        with ExitStack() as first:
            hf, tmp = sb("hf", [P, NP], first), sb("tmp", [P, T, P], first)
            tmp2 = sb("tmp2", [P, T, P], first)
            dst = sb("dst", [P, heads, N], first)
            links, mask = sb("links", [P, 2, NP], first), sb("mask", [P, 2, NP], first)
            masked = sb("masked", [P, 2, N], first)
            loads = [(w[:], h["g1_w"])]
            for i in range(heads):
                loads.append((src_rep[:, i * dh:(i + 1) * dh], a_src.partition_broadcast(P)))
                loads.append((dst_rep[:, i * dh:(i + 1) * dh], a_dst.partition_broadcast(P)))
                loads.append((dst_col[i * dh:(i + 1) * dh, :], a_dst.unsqueeze(1)))
            project_stage(core, name, core.nf, loads, [(hf, w[:], 1.0, None)], [(ht, w[:], None)])

            with nc.Block() as block:
                @block.sync
                def _(sp):
                    for t in range(T):
                        wait(sp, mask_made, t - 1)
                        sp.dma_start(links[:, t % 2, :], h["adj"][t * P:(t + 1) * P, :]).then_inc(adj_in[t % 2], 16)
                        if t >= 1:
                            j = t - 1
                            sp.dma_start(links_t[:, j, :].rearrange("p (t c) -> p t c", c=P),
                                         h["adj_t"][:, :, j, :].rearrange("t p c -> p t c")).then_inc(links_t_in, 16)
                    sp.dma_start(links_t[:, T - 1, :].rearrange("p (t c) -> p t c", c=P),
                                 h["adj_t"][:, :, T - 1, :].rearrange("t p c -> p t c")).then_inc(links_t_in, 16)

                @block.gpsimd
                def _(pool):
                    for t in range(T):
                        pool.wait_ge(adj_in[t % 2], 16 * (t // 2 + 1))
                        wait(pool, maxed, heads * (t - 1))
                        nc.gpsimd.tensor_scalar(mask[:, t % 2, :], links[:, t % 2, :], 0.0, MASKED, ALU.is_le,
                                                ALU.mult).then_inc(mask_made, 1)

                @block.tensor
                def _(pe):
                    pe.wait_ge(dst_w_ready, 1)
                    for i in range(heads):
                        for j, (a, c) in enumerate(CHUNKS):
                            if i >= 2:
                                pe.wait_ge(dst_kept, 3 * (i - 2) + j + 1)
                            nc.tensor.matmul(core.ps[:, 3 * (i % 2) + j, 0:c], dst_w[i * dh:(i + 1) * dh, :],
                                             hf[i * dh:(i + 1) * dh, a:a + c], start=True,
                                             stop=True).then_inc(dst_made, 1)
                    for t in range(T):
                        k = P if t < T - 1 else last
                        mm = nc.tensor.matmul(core.ps[:, 7, 0:P], ones[0:k, :], ht[0:k, t, :], start=(t == 0),
                                              stop=(t == T - 1))
                    mm.then_inc(sum_made, 1)

                @block.scalar
                def _(act):
                    for i in range(heads):
                        for j, (a, c) in enumerate(CHUNKS):
                            act.wait_ge(dst_made, 3 * i + j + 1)
                            nc.scalar.activation(dst[:, i, a:a + c], core.ps[:, 3 * (i % 2) + j, 0:c],
                                                 ACT.Copy).then_inc(dst_kept, 1)
                    act.wait_ge(sum_made, 1)
                    nc.scalar.activation(value_sum[:], core.ps[:, 7, 0:P], ACT.Copy).then_inc(dst_kept, 1)

                @block.vector
                def _(dve):
                    chain = Chain(nc, dve, steps)
                    chain.link(nc.vector.memset(ones[:], 1.0))
                    nc.vector.tensor_copy(dst_w[:], dst_col[:, 0:1].broadcast_to([P, P])).then_inc(dst_w_ready, 1)
                    chain.mark(nc.vector.tensor_tensor(tmp[:], ht[:], over_tiles(src_rep[:]), ALU.mult))
                    chain.link(nc.vector.tensor_tensor(tmp2[:], ht[:], over_tiles(dst_rep[:]), ALU.mult))
                    chain.mark(nc.vector.reduce_sum(src[:], tmp[:].rearrange("p t (h d) -> p (t h) d", h=heads), AX.X))
                    chain.link(nc.vector.reduce_sum(dst_node[:], tmp2[:].rearrange("p t (h d) -> p (t h) d", h=heads),
                                                    AX.X))
                    chain.mark(nc.vector.tensor_scalar(dst_slope[:], dst_node[:], slope, None, ALU.mult))
                    chain.mark(nc.vector.tensor_copy(v[:, :, :, 0:dh], ht[:].rearrange("p t (h d) -> p t h d", h=heads)))
                    chain.mark(nc.vector.memset(v[:, :, :, dh:dv], 1.0))
                    chain.mark(nc.vector.tensor_copy(select[:], core.ident[0:rows, 0:rows].unsqueeze(2)
                                                     .broadcast_to([rows, rows, P])))
                    for t in range(T):
                        dve.wait_ge(mask_made, t + 1)
                        for i in range(heads):
                            k = t * heads + i
                            if t == 0:
                                dve.wait_ge(dst_kept, 3 * (i + 1))
                            wait(dve, maxed, k - 1)
                            nc.vector.tensor_tensor_reduce(masked[:, k % 2, :], dst[:, i, :], mask[:, t % 2, 0:N],
                                                           1.0, -3e38, ALU.add, ALU.max,
                                                           row_max[:, k:k + 1]).then_inc(maxed, 1)
                    dve.wait_ge(maxed, heads * T)
                    chain.link(nc.vector.tensor_scalar(no_links[:], row_max[:].rearrange("p (t h) -> p t h", h=heads)
                                                       [:, :, 0], MASKED / 2, None, ALU.is_lt))
                    chain.link(nc.vector.tensor_tensor(row_max[:], row_max[:], src[:], ALU.add))
                    chain.link(nc.vector.scalar_tensor_tensor(out=score_max[:], in0=row_max[:], scalar=slope,
                                                              in1=row_max[:], op0=ALU.mult, op1=ALU.max))
                    by_head = [s[:].rearrange("p (t h) -> p t h", h=heads) for s in (src, score_max)]
                    chain.mark(nc.vector.tensor_tensor(shifts[:, :, 0:heads], by_head[0], by_head[1], ALU.subtract))
                    chain.link(nc.vector.scalar_tensor_tensor(out=shifts[:, :, heads:rows], in0=by_head[0],
                                                              scalar=slope, in1=by_head[1], op0=ALU.mult,
                                                              op1=ALU.subtract))

        upper, lower = sb("upper", [P, slots, N]), sb("lower", [P, slots, N])
        shift_rep = sb("shift_rep", [P, 2, 2, N])
        out_t = sb("out_t", [dv, 2, NP])
        (rep_made, rep_kept, exp_made, joined, probs_ready, mixed, out_t_kept, out_turned, out_read,
         fixes, ready) = core.sems(*[f"{name}_{s}" for s in (
             "rep_made", "rep_kept", "exp_made", "joined", "probs_ready", "mixed", "out_t_kept", "out_turned",
             "out_read", "fixes", "ready")])
        items = [(hd, j) for hd in range(heads) for j in range(T)]

        def depth(j):
            return P if j < T - 1 else last

        with nc.Block() as block:
            @block.tensor
            def _(pe):
                for g, (a, b) in enumerate(GROUPS):
                    for t in range(a, b):
                        mm = nc.tensor.transpose(core.ps[0:rows, g, (t - a) * P:(t - a + 1) * P], shifts[:, t, :],
                                                 core.ident[:])
                    mm.then_inc(shifts_turned, 1)

                def replicate(hd, n):
                    i, a, c = pieces[n]
                    r = 6 * hd + n
                    wait(pe, rep_kept, r - 1)
                    nc.tensor.matmul(core.ps[:, 6 + r % 2, 0:c], select[:, i * heads + hd, :],
                                     shift_rows[:, a:a + c], start=True, stop=True).then_inc(rep_made, 1)

                def turn_out(hd):
                    pe.wait_ge(out_t_kept, 3 * (hd + 1))
                    for t in range(T):
                        mm = nc.tensor.transpose(core.ps[:, 3 * (hd % 2), t * dv:(t + 1) * dv],
                                                 out_t[:, hd % 2, t * P:(t + 1) * P], core.ident[0:dv, 0:dv])
                    mm.then_inc(out_turned, 1)

                pe.wait_ge(shifts_kept, 3)
                for n in range(6):
                    replicate(0, n)
                pe.wait_ge(ready, 1)
                for k, (hd, j) in enumerate(items):
                    if j == 0:
                        wait(pe, out_read, hd - 1)
                    pe.wait_ge(probs_ready, k + 1)
                    for c, (a, wd) in enumerate(CHUNKS):
                        mm = nc.tensor.matmul(core.ps[0:dv, 3 * (hd % 2) + c, 0:wd], v[0:depth(j), j, hd, :],
                                              upper[0:depth(j), k % slots, a:a + wd], start=(j == 0), stop=(j == T - 1))
                    mm.then_inc(mixed, 1)
                    if j < 6 and hd + 1 < heads:
                        replicate(hd + 1, j)
                    if j == 3 and hd >= 1:
                        turn_out(hd - 1)
                turn_out(heads - 1)

            @block.scalar
            def _(act):
                for g, (a, c) in enumerate(PCHUNKS):
                    act.wait_ge(shifts_turned, g + 1)
                    nc.scalar.activation(shift_rows[:, a:a + c], core.ps[0:rows, g, 0:c], ACT.Copy).then_inc(
                        shifts_kept, 1)

                def keep_rep(hd, n):
                    i, a, c = pieces[n]
                    act.wait_ge(rep_made, 6 * hd + n + 1)
                    wait(act, exp_made, 2 * T * (hd - 1))
                    nc.scalar.activation(shift_rep[:, hd % 2, i, a:a + c], core.ps[:, 6 + (6 * hd + n) % 2, 0:c],
                                         ACT.Copy).then_inc(rep_kept, 1)

                def keep_out(hd):
                    act.wait_ge(mixed, T * (hd + 1))
                    wait(act, out_turned, hd - 1)
                    for c, (a, wd) in enumerate(CHUNKS):
                        nc.scalar.activation(out_t[:, hd % 2, a:a + wd], core.ps[0:dv, 3 * (hd % 2) + c, 0:wd],
                                             ACT.Copy).then_inc(out_t_kept, 1)

                for n in range(6):
                    keep_rep(0, n)
                for k, (hd, j) in enumerate(items):
                    if j == 0:
                        act.wait_ge(rep_kept, 6 * (hd + 1))
                    wait(act, mixed, k - slots + 1)
                    m = depth(j)
                    for i, (dest, bias) in enumerate(((upper, dst_node), (lower, dst_slope))):
                        at = j * heads + hd
                        nc.scalar.activation(dest[0:m, k % slots, :], shift_rep[0:m, hd % 2, i, :], ACT.Exp,
                                             bias=bias[0:m, at:at + 1]).then_inc(exp_made, 1)
                    if 4 <= j < 10 and hd + 1 < heads:
                        keep_rep(hd + 1, j - 4)
                    if j == 2 and hd >= 1:
                        keep_out(hd - 1)
                keep_out(heads - 1)

            @block.vector
            def _(dve):
                nc.vector.memset(out_t[:, :, N:NP], 1.0).then_inc(ready, 1)
                dve.wait_ge(links_t_in, 16 * T)

                def take_out(hd):
                    dve.wait_ge(out_turned, hd + 1)
                    y = core.ps[:, 3 * (hd % 2), 0:T * dv].rearrange("p (t d) -> p t d", d=dv)
                    nc.vector.tensor_copy(out[:, :, hd * dh:(hd + 1) * dh], y[:, :, 0:dh]).then_inc(fixes, 1)
                    nc.vector.tensor_copy(sums[:].rearrange("p (t h) -> p t h", h=heads)[:, :, hd:hd + 1],
                                          y[:, :, dh:dv]).then_inc(out_read, 1)

                for k in range(len(items) + 1):
                    if k < len(items):
                        hd, j = items[k]
                        m = depth(j)
                        dve.wait_ge(exp_made, 2 * (k + 1))
                        nc.vector.tensor_tensor(upper[0:m, k % slots, :], upper[0:m, k % slots, :], lower[0:m, k % slots, :],
                                                ALU.max).then_inc(joined, 1)
                    if k >= 1:
                        hd, j = items[k - 1]
                        m = depth(j)
                        dve.wait_ge(joined, k)
                        nc.vector.scalar_tensor_tensor(out=upper[0:m, (k - 1) % slots, :], in0=links_t[0:m, j, 0:N],
                                                       scalar=0.0, in1=upper[0:m, (k - 1) % slots, :], op0=ALU.is_gt,
                                                       op1=ALU.min).then_inc(probs_ready, 1)
                        if j == 5 and hd >= 1:
                            take_out(hd - 1)
                take_out(heads - 1)
                dve.wait_ge(fixes, heads)
                dve.wait_ge(out_read, heads)
                fix = upper[:].rearrange("p s n -> p (s n)")[:, 0:T * P].rearrange("p (t c) -> p t c", c=P)
                dve.wait_ge(mixed, len(items))
                nc.vector.tensor_tensor(fix, over_tiles(value_sum[:]), per_node(no_links[:]), ALU.mult).then_inc(fixes, 1)
                dve.wait_ge(fixes, heads + 1)
                nc.vector.tensor_tensor(out[:], out[:], fix, ALU.add).then_inc(fixes, 1)
                by_head = sums[:].rearrange("p (t h) -> p t h", h=heads)
                nc.vector.scalar_tensor_tensor(out=by_head, in0=no_links[:].unsqueeze(2).broadcast_to([P, T, heads]),
                                               scalar=float(N), in1=by_head, op0=ALU.mult,
                                               op1=ALU.add).then_inc(fixes, 1)


def gat_norm_stage(core, name, heads, out, sums, gain_dram, shift_dram):
    nc = core.nc
    with ExitStack() as ctx:
        def sb(n, shape):
            return ctx.enter_context(nc.sbuf_tensor(f"{name}_{n}", shape, F32))

        centred, square, stats = sb("centred", [P, T, P]), sb("square", [P, T, P]), sb("stats", [P, 6, T])
        gain, shift, inv = sb("gain", [P, P]), sb("shift", [P, P]), sb("inv", [P, T * heads])
        steps, loaded, var_ready, root_ready, n_ready = core.sems(
            *[f"{name}_{s}" for s in ("steps", "loaded", "var_ready", "root_ready", "n_ready")])
        with nc.Block() as block:
            @block.sync
            def _(sp):
                sp.dma_start(gain[:], gain_dram.partition_broadcast(P)).then_inc(loaded, 16)
                sp.dma_start(shift[:], shift_dram.partition_broadcast(P)).then_inc(loaded, 16)

            @block.scalar
            def _(act):
                act.wait_ge(var_ready, 1)
                nc.scalar.activation(stats[:, 3, :], stats[:, 2, :], ACT.Sqrt).then_inc(root_ready, 1)

            @block.vector
            def _(dve):
                chain = Chain(nc, dve, steps)
                if sums is not None:
                    chain.link(nc.vector.reciprocal(inv[:], sums))
                    view = out.rearrange("p t (h d) -> p (t h) d", h=heads)
                    rep = inv[:].unsqueeze(2).broadcast_to([P, T * heads, P // heads])
                    chain.link(nc.vector.tensor_tensor(view, view, rep, ALU.mult))
                normalise(chain, dve, out, out, centred[:], square[:], stats, var_ready, root_ready, n_ready)
                dve.wait_ge(n_ready, 1)
                dve.wait_ge(loaded, 32)
                chain.link(nc.vector.tensor_tensor(out, out, over_tiles(gain[:]), ALU.mult))
                chain.link(nc.vector.tensor_tensor(out, out, over_tiles(shift[:]), ALU.add))
                chain.link(nc.vector.tensor_tensor(core.x[:], core.x[:], out, ALU.add))


def gat_sigmoid_stage(core, name, out, sums):
    nc = core.nc
    with ExitStack() as ctx:
        inv = ctx.enter_context(nc.sbuf_tensor(f"{name}_inv", [P, T], F32))
        steps, ratio_ready, exp_ready = core.sems(*[f"{name}_{s}" for s in ("steps", "ratio_ready", "exp_ready")])
        with nc.Block() as block:
            @block.vector
            def _(dve):
                chain = Chain(nc, dve, steps)
                chain.link(nc.vector.reciprocal(inv[:], sums))
                nc.vector.tensor_tensor(out, out, per_node(inv[:]), ALU.mult).then_inc(ratio_ready, 1)
                dve.wait_ge(exp_ready, 1)
                chain.link(nc.vector.tensor_scalar(out, out, 1.0, None, ALU.add))
                chain.link(nc.vector.reciprocal(out, out))
                chain.link(nc.vector.tensor_tensor(core.x[:], core.x[:], out, ALU.add))

            @block.scalar
            def _(act):
                act.wait_ge(ratio_ready, 1)
                nc.scalar.activation(out, out, ACT.Exp, scale=-1.0).then_inc(exp_ready, 1)


def gat_layer(core, h, layer):
    nc = core.nc
    heads = 4 if layer == 1 else 1
    name = f"g{layer}"
    with ExitStack() as ctx:
        out = ctx.enter_context(nc.sbuf_tensor(f"{name}_out", [P, T, P], F32))
        sums = ctx.enter_context(nc.sbuf_tensor(f"{name}_sums", [P, T * heads], F32))
        if layer == 1:
            four_head_attention(core, h, out, sums)
            gat_norm_stage(core, "g1n", heads, out[:], sums[:], h["g1_gain"], h["g1_shift"])
        else:
            s = h["g2_s"]
            graph_attention(core, name, heads, 0.01, h["adj"], h["g2_w"], h["g2_b"], s[0:P], s[P:2 * P], out, sums,
                            ALU.is_equal, True)
            gat_sigmoid_stage(core, "g2s", out[:], sums[:])


def masked_attention(core, h):
    nc = core.nc
    name, heads = "g3", 4
    dh = P // heads
    dv = dh + 1
    last = N - (T - 1) * P
    slots = 4
    score_banks, out_bank = 5, 5
    bf16 = mybir.dt.bfloat16
    items = [(hd, j) for hd in range(heads) for j in range(T)]

    def depth(j):
        return P if j < T - 1 else last

    def group(g):
        return slice(g * dh, (g + 1) * dh)

    def side_groups(hd):
        return (hd + 1) % heads, (hd + 2) % heads

    with ExitStack() as ctx:
        def sb(n, shape, stack=ctx, dtype=F32):
            return stack.enter_context(nc.sbuf_tensor(f"{name}_{n}", shape, dtype))

        w, wo = sb("w", [P, 3, P]), sb("wo", [dv, heads, P + 1])
        qk_bias, v_bias, o_bias, gb = sb("qk_bias", [P, 2]), sb("v_bias", [P, P]), sb("o_bias", [P, P]), sb("gb", [P, 1])
        values = sb("values", [P, T, heads, dv])
        q_main, k_main, q_side, k_side = [sb(n, [P, heads, NP], dtype=bf16)
                                          for n in ("q_main", "k_main", "q_side", "k_side")]
        row_max = sb("row_max", [P, T, heads])
        max_parts = sb("max_parts", [P, T, heads, dh])
        bias_t = sb("bias_t", [P, T, NP])
        b = h["g3_b"]
        (copied, split, parted, moved, cleared, set_up, adj_in0, adj_in1, edge_made, bias_made, bias_turned,
         bias_kept, scored, maxed, steps) = core.sems(*[f"{name}_{s}" for s in (
             "copied", "split", "parted", "moved", "cleared", "set_up", "adj_in0", "adj_in1", "edge_made",
             "bias_made", "bias_turned", "bias_kept", "scored", "maxed", "steps")])
        adj_in = [adj_in0, adj_in1]

        second = ctx.enter_context(ExitStack())
        parts = [[sb(f"part{i}{p}", [P, NP], second, bf16) for p in range(3)] for i in range(2)]
        with ExitStack() as first:
            q, kf, v = sb("q", [P, NP], first), sb("k", [P, NP], first), sb("v", [P, T, P], first)
            rest = [sb(f"rest{i}", [P, NP], first) for i in range(2)]
            project_stage(core, name, core.nf,
                          [(w[:], h["g3_w"].rearrange("p (c k) -> p c k", k=P)),
                           (wo[0:dh, :, 0:P], h["g3_wo"].rearrange("(h d) c -> d h c", d=dh)),
                           (qk_bias[:, 0:1], b[0:P].unsqueeze(1)), (qk_bias[:, 1:2], b[P:2 * P].unsqueeze(1)),
                           (v_bias[:], b[2 * P:3 * P].partition_broadcast(P)),
                           (o_bias[:], h["g3_bo"].partition_broadcast(P)),
                           (gb[:], h["g3_gb"].partition_broadcast(P))],
                          [(q, w[:, 0, :], 1.0, qk_bias[:, 0:1]), (kf, w[:, 1, :], 1.0, qk_bias[:, 1:2])],
                          [(v, w[:, 2, :], v_bias[:])])

            with nc.Block() as block:
                @block.gpsimd
                def _(pool):
                    nc.gpsimd.memset(q_side[:], 0.0).then_inc(cleared, 1)
                    nc.gpsimd.memset(k_side[:], 1.0).then_inc(cleared, 1)
                    nc.gpsimd.memset(max_parts[:], 0.0).then_inc(cleared, 1)

                @block.scalar
                def _(act):
                    nc.scalar.activation(q[:], q[:], ACT.Copy, scale=float(dh) ** -0.5).then_inc(split, 1)
                    act.wait_ge(split, 1)
                    nc.scalar.activation(parts[0][0][:], q[:], ACT.Copy).then_inc(parted, 1)
                    nc.scalar.activation(parts[1][0][:], kf[:], ACT.Copy).then_inc(parted, 1)
                    for i in range(2):
                        act.wait_ge(split, 2 + i)
                        nc.scalar.activation(parts[i][1][:], rest[i][:], ACT.Copy).then_inc(parted, 1)

                @block.vector
                def _(dve):
                    for i, src in enumerate((q, kf)):
                        dve.wait_ge(parted, 1 + i)
                        nc.vector.tensor_tensor(rest[i][:], src[:], parts[i][0][:], ALU.subtract).then_inc(split, 1)
                    nc.vector.memset(values[:, :, :, dh:dv], 1.0).then_inc(set_up, 1)
                    nc.vector.tensor_copy(values[:, :, :, 0:dh],
                                          v[:].rearrange("p t (h d) -> p t h d", h=heads)).then_inc(set_up, 1)
                    nc.vector.memset(wo[dh:dv, :, :], 0.0).then_inc(set_up, 1)
                    nc.vector.memset(wo[0:dh, :, P:P + 1], 0.0).then_inc(set_up, 1)
                    dve.wait_ge(set_up, 4)
                    nc.vector.memset(wo[dh:dv, :, P:P + 1], 1.0).then_inc(set_up, 1)
                    for i in range(2):
                        dve.wait_ge(parted, 3 + i)
                        nc.vector.tensor_tensor(parts[i][2][:], rest[i][:], parts[i][1][:],
                                                ALU.subtract).then_inc(set_up, 1)

        moves = []
        for dest, i, order in ((q_main, 0, (0, 0, 1, 1)), (k_main, 1, (0, 1, 0, 1))):
            moves += [(dest[group(g), hd, :], parts[i][p][group(hd), :])
                      for hd in range(heads) for g, p in enumerate(order)]
        for hd in range(heads):
            s1, s2 = side_groups(hd)
            moves += [(dest[group(g), hd, :], parts[i][p][group(hd), :])
                      for dest, g, i, p in ((q_side, s1, 0, 0), (k_side, s1, 1, 2), (q_side, s2, 0, 2), (k_side, s2, 1, 0))]
        by_dve, by_dma = moves[:26], moves[26:]
        links, edge, bias = [sb(n, [P, 2, NP], second) for n in ("links", "edge", "bias")]
        biased = sb("biased", [P, 2, N], second)
        max_rest = sb("max_rest", [P, T, heads], second)
        max_high = sb("max_high", [P, 2, T, heads], second, bf16)
        with nc.Block() as block:
            @block.sync
            def _(sp):
                for t in range(T):
                    wait(sp, bias_made, t - 1)
                    sp.dma_start(links[:, t % 2, :], h["adj"][t * P:(t + 1) * P, :]).then_inc(adj_in[t % 2], 16)

            @block.gpsimd
            def _(pool):
                for t in range(T):
                    pool.wait_ge(adj_in[t % 2], 16 * (t // 2 + 1))
                    wait(pool, bias_made, t - 1)
                    nc.gpsimd.tensor_scalar(edge[:, t % 2, :], links[:, t % 2, :], 0.0, MASKED3, ALU.is_equal,
                                            ALU.mult).then_inc(edge_made, 1)

            @block.tensor
            def _(pe):
                pe.wait_ge(moved, 16 * len(by_dma))
                pe.wait_ge(copied, len(by_dve))
                for t in range(T):
                    for hd in range(heads):
                        k = t * heads + hd
                        wait(pe, maxed, k - 1)
                        for left, right in ((q_main, k_main), (q_side, k_side)):
                            for c, (a, wd) in enumerate(CHUNKS):
                                mm = nc.tensor.matmul(core.ps[:, 3 * (k % 2) + c, 0:wd],
                                                      left[:, hd, t * P:(t + 1) * P], right[:, hd, a:a + wd],
                                                      start=(left is q_main), stop=(left is q_side))
                        mm.then_inc(scored, 1)
                    pe.wait_ge(bias_made, t + 1)
                    for g, (a, e) in enumerate(GROUPS):
                        u = 3 * t + g
                        wait(pe, bias_kept, u - 1)
                        for j in range(a, e):
                            mm = nc.tensor.transpose(core.ps[:, 6 + u % 2, (j - a) * P:(j - a + 1) * P],
                                                     bias[:, t % 2, j * P:(j + 1) * P], core.ident[:])
                        mm.then_inc(bias_turned, 1)

            @block.scalar
            def _(act):
                for dest, src in by_dma:
                    act.dma_start(dest, src).then_inc(moved, 16)
                for t in range(T):
                    for g, (a, e) in enumerate(GROUPS):
                        u = 3 * t + g
                        act.wait_ge(bias_turned, u + 1)
                        y = core.banks(6 + u % 2, 1, (e - a) * P).rearrange("p (t c) -> p t c", c=P)
                        nc.scalar.activation(bias_t[:, a:e, t * P:(t + 1) * P], y, ACT.Copy).then_inc(bias_kept, 1)

            @block.vector
            def _(dve):
                for dest, src in by_dve:
                    nc.vector.tensor_copy(dest, src).then_inc(copied, 1)
                for t in range(T):
                    dve.wait_ge(edge_made, t + 1)
                    wait(dve, bias_turned, 3 * (t - 1))
                    wait(dve, maxed, heads * t)
                    nc.vector.scalar_tensor_tensor(out=bias[:, t % 2, :], in0=links[:, t % 2, :],
                                                   scalar=gb[:, 0:1], in1=edge[:, t % 2, :], op0=ALU.mult,
                                                   op1=ALU.add).then_inc(bias_made, 1)
                    dve.wait_ge(bias_made, t + 1)
                    for hd in range(heads):
                        k = t * heads + hd
                        dve.wait_ge(scored, k + 1)
                        wait(dve, maxed, k - 1)
                        nc.vector.tensor_tensor_reduce(biased[:, k % 2, :], core.banks(3 * (k % 2), 3, N),
                                                       bias[:, t % 2, 0:N], 1.0, -3e38, ALU.add, ALU.max,
                                                       row_max[:, t, hd:hd + 1]).then_inc(maxed, 1)
                dve.wait_ge(maxed, heads * T)
                chain = Chain(nc, dve, steps)
                part = [max_parts[:, :, :, p] for p in range(3)]
                chain.link(nc.vector.tensor_scalar(max_rest[:], row_max[:], -1.0, None, ALU.mult))
                for p in range(2):
                    chain.link(nc.vector.tensor_copy(max_high[:, p], max_rest[:]))
                    chain.mark(nc.vector.tensor_copy(part[p], max_high[:, p]))
                    chain.link(nc.vector.tensor_tensor(max_rest[:], max_rest[:], max_high[:, p], ALU.subtract))
                chain.link(nc.vector.tensor_copy(part[2], max_rest[:]))
        second.close()

        scores = sb("scores", [P, slots, N])
        out_t = sb("out_t", [dv, heads, NP])
        inv = sb("inv", [P, 2, T, 2])
        (max_turned, max_set, made, added, probs_ready, mixed, out_kept, ready, projected, taken,
         final) = core.sems(*[f"{name}_{s}" for s in (
             "max_turned", "max_set", "turned_scores", "added", "probs_ready", "mixed", "out_kept", "ready", "projected",
             "taken", "final")])
        with nc.Block() as block:
            @block.tensor
            def _(pe):
                for g, (a, e) in enumerate(GROUPS):
                    for t in range(a, e):
                        mm = nc.tensor.transpose(core.ps[:, out_bank + g, (t - a) * P:(t - a + 1) * P],
                                                 max_parts[:, t].rearrange("p h d -> p (h d)"), core.ident[:])
                    mm.then_inc(max_turned, 1)

                def score(k):
                    hd, j = items[k]
                    if j == 0:
                        pe.wait_ge(max_set, 3 * (hd + 1))
                    for c, (a, wd) in enumerate(CHUNKS):
                        u = 3 * k + c
                        wait(pe, added, u + 1 - score_banks)
                        for left, right in ((k_main, q_main), (k_side, q_side)):
                            mm = nc.tensor.matmul(core.ps[0:depth(j), u % score_banks, 0:wd],
                                                  left[:, hd, j * P:j * P + depth(j)], right[:, hd, a:a + wd],
                                                  start=(left is k_main), stop=(left is k_side))
                        mm.then_inc(made, 1)

                score(0)
                for k, (hd, j) in enumerate(items):
                    if k + 1 < len(items):
                        score(k + 1)
                    if j == 0:
                        pe.wait_ge(out_kept, 3 * hd) if hd else pe.wait_ge(max_set, 3 * heads)
                    pe.wait_ge(probs_ready, k + 1)
                    for c, (a, wd) in enumerate(CHUNKS):
                        mm = nc.tensor.matmul(core.ps[0:dv, out_bank + c, 0:wd], values[0:depth(j), j, hd, :],
                                              scores[0:depth(j), k % slots, a:a + wd], start=(j == 0),
                                              stop=(j == T - 1))
                    mm.then_inc(mixed, 1)

            @block.scalar
            def _(act):
                for g, (a, c) in enumerate(PCHUNKS):
                    act.wait_ge(max_turned, g + 1)
                for hd in range(heads):
                    for g, (a, c) in enumerate(PCHUNKS):
                        nc.scalar.activation(q_side[group(hd), hd, a:a + c], core.ps[group(hd), out_bank + g, 0:c],
                                             ACT.Copy).then_inc(max_set, 1)

                def keep_out(hd):
                    act.wait_ge(mixed, T * (hd + 1))
                    for c, (a, wd) in enumerate(CHUNKS):
                        nc.scalar.activation(out_t[:, hd, a:a + wd], core.ps[0:dv, out_bank + c, 0:wd],
                                             ACT.Copy).then_inc(out_kept, 1)

                for k, (hd, j) in enumerate(items):
                    act.wait_ge(added, 3 * (k + 1))
                    m = depth(j)
                    nc.scalar.activation(scores[0:m, k % slots, :], scores[0:m, k % slots, :],
                                         ACT.Exp).then_inc(probs_ready, 1)
                    if j == 0 and hd:
                        keep_out(hd - 1)
                keep_out(heads - 1)

            @block.vector
            def _(dve):
                nc.vector.memset(out_t[:, :, N:NP], 1.0).then_inc(ready, 1)
                for k, (hd, j) in enumerate(items):
                    m = depth(j)
                    wait(dve, mixed, k + 1 - slots)
                    for c, (a, wd) in enumerate(CHUNKS):
                        u = 3 * k + c
                        dve.wait_ge(made, u + 1)
                        nc.vector.tensor_tensor(scores[0:m, k % slots, a:a + wd],
                                                core.ps[0:m, u % score_banks, 0:wd], bias_t[0:m, j, a:a + wd],
                                                ALU.add).then_inc(added, 1)

        with nc.Block() as block:
            units = [(pair, t) for pair in range(heads // 2) for t in range(T)]

            @block.tensor
            def _(pe):
                for u, (pair, t) in enumerate(units):
                    wait(pe, taken, u - 7)
                    for i in range(2):
                        mm = nc.tensor.matmul(core.ps[:, u % 8, i * (P + 1):(i + 1) * (P + 1)],
                                              out_t[:, 2 * pair + i, t * P:(t + 1) * P], wo[:, 2 * pair + i, :],
                                              start=True, stop=True)
                    mm.then_inc(projected, 1)

            @block.vector
            def _(dve):
                chain = Chain(nc, dve, final)
                chain.link(nc.vector.tensor_tensor(core.x[:], core.x[:], over_tiles(o_bias[:]), ALU.add))

                def add(u, i):
                    pair, t = units[u]
                    dve.wait_ge(final, chain.count - (i == 1 and u + 1 < len(units)))
                    ins = nc.vector.scalar_tensor_tensor(out=core.x[:, t, :],
                                                         in0=core.ps[:, u % 8, i * (P + 1):i * (P + 1) + P],
                                                         scalar=inv[:, pair, t, i:i + 1], in1=core.x[:, t, :],
                                                         op0=ALU.mult, op1=ALU.add)
                    if i == 0:
                        chain.mark(ins)
                    else:
                        ins.then_inc(taken, 1)

                for u, (pair, t) in enumerate(units):
                    dve.wait_ge(projected, u + 1)
                    if pair:
                        dve.wait_ge(taken, u - T + 1)
                    y = core.ps[:, u % 8, 0:2 * (P + 1)].rearrange("p (i c) -> p i c", c=P + 1)
                    chain.mark(nc.vector.reciprocal(inv[:, pair, t, :], y[:, :, P]))
                    if u >= 1:
                        add(u - 1, 1)
                    add(u, 0)
                add(len(units) - 1, 1)


def scores_stage(core, name, feats, w, probs, sums):
    nc = core.nc
    da = w["w1"].shape[1]
    bf16 = mybir.dt.bfloat16
    lower, upper = slice(0, da), slice(da, 2 * da)
    with ExitStack() as ctx:
        def sb(n, shape, dtype=F32):
            return ctx.enter_context(nc.sbuf_tensor(f"{name}_{n}", shape, dtype))

        w1, w2, w3 = sb("w1", [P, da]), sb("w2", [da, 2, da]), sb("w3", [P, 2, da])
        low = sb("low", [da, NP])
        rest_q, rest_k = sb("rest_q", [P, NP]), sb("rest_k", [P, NP])
        q1, q2, q13, k12, k2, k31 = [sb(n, [P, NP], bf16) for n in ("q1", "q2", "q13", "k12", "k2", "k31")]
        row_max, neg_max, zeros = sb("row_max", [P, T]), sb("neg_max", [P, T]), sb("zeros", [P, N])
        loaded, low_made, q_made, k_made, low_kept, q_parts, k_parts, rests, stacked, scored, maxed, negated, done = core.sems(
            *[f"{name}_{s}" for s in ("loaded", "low_made", "q_made", "k_made", "low_kept", "q_parts", "k_parts",
                                      "rests", "stacked", "scored", "maxed", "negated", "done")])
        with nc.Block() as block:
            @block.sync
            def _(sp):
                sp.dma_start(w1[:], w["w1"]).then_inc(loaded, 16)
                for i in range(2):
                    sp.dma_start(w2[:, i, :], w["w2"]).then_inc(loaded, 16)
                    sp.dma_start(w3[:, i, :], w["w3"]).then_inc(loaded, 16)

            @block.tensor
            def _(pe):
                pe.wait_ge(loaded, 80)
                for j, (a, c) in enumerate(PCHUNKS):
                    nc.tensor.matmul(core.ps[0:da, j, 0:c], w1[:], feats[:, a:a + c], start=True,
                                     stop=True).then_inc(low_made, 1)
                for j, (a, c) in enumerate(PCHUNKS):
                    mm = nc.tensor.matmul(core.ps[:, 3 + j, 0:c], w3[:].rearrange("p i d -> p (i d)"),
                                          feats[:, a:a + c], start=True, stop=True)
                mm.then_inc(k_made, 1)
                for j, (a, c) in enumerate(PCHUNKS):
                    pe.wait_ge(low_kept, j + 1)
                    mm = nc.tensor.matmul(core.ps[:, j, 0:c], w2[:].rearrange("p i d -> p (i d)"),
                                          low[:, a:a + c], start=True, stop=True)
                mm.then_inc(q_made, 1)
                pe.wait_ge(stacked, 5)
                for t in range(T):
                    wait(pe, maxed, t - 1)
                    for left, right in ((q1, k12), (q2, k12), (q13, k31)):
                        for j, (a, c) in enumerate(CHUNKS):
                            mm = nc.tensor.matmul(core.ps[:, 3 * (t % 2) + j, 0:c], left[:, t * P:(t + 1) * P],
                                                  right[:, a:a + c], start=(left is q1), stop=(left is q13))
                    mm.then_inc(scored, 1)

            @block.scalar
            def _(act):
                for j, (a, c) in enumerate(PCHUNKS):
                    act.wait_ge(low_made, j + 1)
                    nc.scalar.activation(low[:, a:a + c], core.ps[0:da, j, 0:c], ACT.Copy).then_inc(low_kept, 1)
                act.wait_ge(k_made, 1)
                nc.scalar.activation(k12[:], core.banks(3, 3, NP), ACT.Copy).then_inc(k_parts, 1)
                act.wait_ge(q_made, 1)
                nc.scalar.activation(q1[:], core.banks(0, 3, NP), ACT.Copy).then_inc(q_parts, 1)
                act.wait_ge(rests, 1)
                nc.scalar.activation(k2[:], rest_k[:], ACT.Copy).then_inc(k_parts, 1)
                act.wait_ge(rests, 2)
                nc.scalar.activation(q2[:], rest_q[:], ACT.Copy).then_inc(q_parts, 1)
                for t in range(T):
                    act.wait_ge(negated, t + 2)
                    nc.scalar.activation(probs[:, t, 0:N], probs[:, t, 0:N], ACT.Exp, bias=neg_max[:, t:t + 1],
                                         accum_out=sums[:, t:t + 1]).then_inc(done, 1)

            @block.vector
            def _(dve):
                nc.vector.memset(zeros[:], 0.0).then_inc(negated, 1)
                dve.wait_ge(k_parts, 1)
                nc.vector.tensor_tensor(rest_k[:], core.banks(3, 3, NP), k12[:], ALU.subtract).then_inc(rests, 1)
                nc.vector.tensor_copy(k31[upper, :], k12[upper, :]).then_inc(stacked, 1)
                dve.wait_ge(q_parts, 1)
                nc.vector.tensor_tensor(rest_q[:], core.banks(0, 3, NP), q1[:], ALU.subtract).then_inc(rests, 1)
                nc.vector.tensor_copy(q13[lower, :], q1[lower, :]).then_inc(stacked, 1)
                dve.wait_ge(k_parts, 2)
                nc.vector.tensor_tensor(k31[lower, :], rest_k[lower, :], k2[lower, :],
                                        ALU.subtract).then_inc(stacked, 1)
                dve.wait_ge(rests, 1)
                dve.wait_ge(stacked, 1)
                nc.vector.tensor_copy(k12[upper, :], k2[upper, :]).then_inc(stacked, 1)
                dve.wait_ge(q_parts, 2)
                nc.vector.tensor_tensor(q13[upper, :], rest_q[upper, :], q2[upper, :],
                                        ALU.subtract).then_inc(stacked, 1)
                dve.wait_ge(negated, 1)
                for t in range(T):
                    dve.wait_ge(scored, t + 1)
                    nc.vector.tensor_tensor_reduce(probs[:, t, 0:N], core.banks(3 * (t % 2), 3, N), zeros[:], 1.0,
                                                   -3e38, ALU.add, ALU.max, row_max[:, t:t + 1]).then_inc(maxed, 1)
                    dve.wait_ge(maxed, t + 1)
                    nc.vector.tensor_scalar(neg_max[:, t:t + 1], row_max[:, t:t + 1], -1.0, None,
                                            ALU.mult).then_inc(negated, 1)


def top_p_stage(core, name, halvings, rounds, probs, sums, adj_t, xf, spread, xa, mixed_xa):
    nc = core.nc
    all_rounds = -(-N // 8)
    last = N - (T - 1) * P
    items = Items(1)
    with ExitStack() as ctx:
        def sb(n, shape, dtype=F32):
            return ctx.enter_context(nc.sbuf_tensor(f"{name}_{n}", shape, dtype))

        low, middle, mass, room, flags = [sb(n, [P, T]) for n in ("low", "middle", "mass", "room", "flags")]
        below = sb("below", [P, T, NP])
        ratio = sb("ratio", [P, halvings])
        product = sb("product", [P, 2, N])
        largest, keep = sb("largest", [P, T, 8]), sb("keep", [P, T, 8])
        before = sb("before", [P, T, 9])
        any_row, any_turned, any_block = sb("any_row", [P, 32]), sb("any_turned", [P, 32]), sb("any_block", [P, 1])
        open_rows = sb("open_rows", [P, 1], mybir.dt.int32)
        pause = sb("pause", [P, 2])
        first_act, end_act = PARTS[0][1] - BY_ACT, PARTS[0][1]
        neg_middle, relu_sum, sign_sum = [sb(n, [P, T]) for n in ("neg_middle", "relu_sum", "sign_sum")]
        block_in = sb("adj_t", [P, 2, T, P])
        mixing = Mixing(core, ctx, name, items, lambda j, h: xa[:, j, :], P + 1, mixed_xa, P + 1,
                        lambda t, s: probs[:, t, :])
        steps, set_up, a_in0, a_in1, mixed, spread_kept, middle_set, summed = core.sems(
            *[f"{name}_{s}" for s in ("steps", "set_up", "a_in0", "a_in1", "mixed", "spread_kept", "middle_set",
                                      "summed")])
        halved = core.sems(*[f"{name}_halved{i}" for i in range(len(PARTS))])
        general = core.sems(*[f"{name}_general{i}" for i in range(len(PARTS))])
        a_in = [a_in0, a_in1]
        with nc.Block() as block:
            @block.sync
            def _(sp):
                for t in range(T):
                    wait(sp, mixed, t - 1)
                    sp.dma_start(block_in[:, t % 2], adj_t[t]).then_inc(a_in[t % 2], 16)

            @block.tensor
            def _(pe):
                for t in range(T):
                    pe.wait_ge(a_in[t % 2], 16 * (t // 2 + 1))
                    wait(pe, spread_kept, t - 1)
                    for j in range(T):
                        mm = nc.tensor.matmul(core.ps[:, t % 2, 0:P + 1], block_in[:, t % 2, j, :], xf[:, j, :],
                                              start=(j == 0), stop=(j == T - 1))
                    mm.then_inc(mixed, 1)

                def step(t, h):
                    if item := items.near(t, h, 0):
                        mixing.turn(pe, item)
                    if item := items.near(t, h, -1):
                        mixing.mix(pe, item)

                items.run(pe, step)

            @block.scalar
            def _(act):
                with act.Fori(0, halvings) as i:
                    act.wait_ge(middle_set, i + 1)
                    for t in range(first_act, end_act):
                        nc.scalar.activation(below[:, t, 0:N], probs[:, t, 0:N], ACT.Relu, bias=neg_middle[:, t:t + 1],
                                             accum_out=relu_sum[:, t:t + 1]).then_inc(summed, 1)
                        nc.scalar.activation(below[:, t - BY_ACT, 0:N], probs[:, t, 0:N], ACT.Sign,
                                             bias=neg_middle[:, t:t + 1],
                                             accum_out=sign_sum[:, t:t + 1]).then_inc(summed, 1)
                for t in range(T):
                    act.wait_ge(mixed, t + 1)
                    nc.scalar.activation(spread[:, t, :], core.ps[:, t % 2, 0:P + 1], ACT.Copy).then_inc(spread_kept, 1)

                def step(t, h):
                    if item := items.near(t, h, 0):
                        for g in range(3):
                            mixing.keep(act, act_copy(nc), g, item)
                    if item := items.near(t, h, -1):
                        mixing.take_out(act, item, act_copy(nc))

                items.run(act, step)

            @block.vector
            def _(dve):
                chain = Chain(nc, dve, steps)
                for i in range(halvings):
                    nc.vector.memset(ratio[:, i:i + 1], math.exp(REACH / 2 ** (i + 1))).then_inc(set_up, 1)
                nc.vector.memset(low[:], math.exp(-REACH)).then_inc(set_up, 1)
                nc.vector.memset(any_row[:], 0.0).then_inc(set_up, 1)
                nc.vector.memset(flags[:], 0.0).then_inc(set_up, 1)
                nc.vector.memset(before[:, :, 8:9], 0.0).then_inc(set_up, 1)
                nc.vector.memset(below[:, :, N:NP], 0.0).then_inc(set_up, 1)
                nc.vector.tensor_scalar(room[:], sums[:], TOP_P, None, ALU.mult).then_inc(set_up, 1)
                nc.vector.memset(pause[:], 0.0).then_inc(set_up, 1)
                dve.wait_ge(set_up, halvings + 7)

                def select(a, b, halved, general):
                    tiles = range(a, b)
                    shared = a == 0
                    own = b - BY_ACT if shared else b
                    per = own - a + 4 + 3 * shared
                    with dve.Fori(0, halvings) as i:
                        at = [0]

                        def link(ins, behind=0):
                            at[0] += 1
                            ins.then_inc(halved, 1)
                            dve.wait_ge(halved, i * per + at[0] - behind)

                        link(nc.vector.tensor_scalar(middle[:, a:b], low[:, a:b], ratio[:, bass.ds(i, 1)], None,
                                                     ALU.mult))
                        if shared:
                            nc.vector.tensor_scalar(neg_middle[:, own:b], middle[:, own:b], -1.0, None,
                                                    ALU.mult).then_inc(middle_set, 1)
                        for t in range(a, own):
                            link(nc.vector.scalar_tensor_tensor(out=product[:, t % 2, :], in0=probs[:, t, 0:N],
                                                                scalar=middle[:, t:t + 1], in1=probs[:, t, 0:N],
                                                                op0=ALU.is_gt, op1=ALU.mult,
                                                                accum_out=mass[:, t:t + 1]), t + 1 < own)
                        if shared:
                            dve.wait_ge(summed, i * (2 * BY_ACT) + 2 * BY_ACT)
                            link(nc.vector.tensor_scalar(mass[:, own:b], sign_sum[:, own:b], 0.5, N / 2,
                                                         ALU.mult, ALU.add))
                            link(nc.vector.tensor_tensor(mass[:, own:b], mass[:, own:b], middle[:, own:b], ALU.mult))
                            link(nc.vector.tensor_tensor(mass[:, own:b], mass[:, own:b], relu_sum[:, own:b], ALU.add))
                        link(nc.vector.tensor_tensor(mass[:, a:b], mass[:, a:b], room[:, a:b], ALU.is_ge))
                        link(nc.vector.tensor_tensor(middle[:, a:b], middle[:, a:b], mass[:, a:b], ALU.mult))
                        link(nc.vector.tensor_tensor(low[:, a:b], low[:, a:b], middle[:, a:b], ALU.max))
                        assert at[0] == per

                    chain.link(nc.vector.tensor_scalar(middle[:, a:b], low[:, a:b], math.exp(REACH / 2 ** halvings),
                                                       None, ALU.mult))
                    for t in tiles:
                        ins = nc.vector.scalar_tensor_tensor(out=below[:, t, 0:N], in0=probs[:, t, 0:N],
                                                             scalar=middle[:, t:t + 1], in1=probs[:, t, 0:N],
                                                             op0=ALU.is_le, op1=ALU.mult,
                                                             accum_out=mass[:, t:t + 1])
                        (chain.link if t + 1 == b else chain.mark)(ins)
                    chain.link(nc.vector.tensor_tensor(mass[:, a:b], mass[:, a:b], sums[:, a:b], ALU.subtract))
                    chain.link(nc.vector.tensor_tensor(room[:, a:b], room[:, a:b], mass[:, a:b], ALU.add))

                    def take_round(link, mark):
                        for t in tiles:
                            (link if t + 1 == b else mark)(nc.vector.max(largest[:, t, :], below[:, t, :]))
                        link(nc.vector.tensor_copy(before[:, a:b, 0:1], before[:, a:b, 8:9]))
                        for i in range(8):
                            link(nc.vector.tensor_tensor(before[:, a:b, i + 1:i + 2], before[:, a:b, i:i + 1],
                                                         largest[:, a:b, i:i + 1], ALU.add))
                        rep = room[:, a:b].unsqueeze(2).broadcast_to([P, b - a, 8])
                        link(nc.vector.tensor_tensor(keep[:, a:b, :], before[:, a:b, 0:8], rep, ALU.is_lt))
                        link(nc.vector.tensor_tensor(largest[:, a:b, :], largest[:, a:b, :], keep[:, a:b, :], ALU.mult))
                        for t in tiles:
                            (link if t + 1 == b else mark)(
                                nc.vector.match_replace(below[:, t, :], largest[:, t, :], below[:, t, :], 0.0))

                    for _ in range(rounds):
                        take_round(chain.link, chain.mark)
                    full = b if b < T else T - 1
                    if full > a:
                        chain.link(nc.vector.tensor_tensor(flags[:, a:full], before[:, a:full, 8], room[:, a:full],
                                                           ALU.is_lt))
                    if b == T:
                        chain.link(nc.vector.tensor_tensor(flags[0:last, T - 1:T], before[0:last, T - 1, 8:9],
                                                           room[0:last, T - 1:T], ALU.is_lt))
                    chain.link(nc.vector.reduce_max(any_row[:, 0:1], flags[:, a:b], AX.X))
                    chain.link(nc.vector.transpose(any_turned[:], any_row[:]))
                    chain.link(nc.vector.reduce_max(any_block[:], any_turned[:], AX.X))
                    chain.link(nc.vector.tensor_copy(open_rows[:], any_block[:]))
                    still_open = [dve.value_load(open_rows[q:q + 1, 0:1], min_val=0, max_val=1)
                                  for q in range(0, P, 32)]
                    with dve.If(sum(still_open[1:], still_open[0]) > 0):
                        with dve.Fori(0, all_rounds - rounds) as i:
                            at = [0]
                            per_round = 2 * (b - a) + 2 + 2 * 11

                            def link(ins):
                                ins.then_inc(general, 1)
                                dve.wait_ge(general, i * per_round + at[0] + 1)
                                nc.vector.tensor_copy(pause[:, 1:2], pause[:, 0:1]).then_inc(general, 1)
                                at[0] += 2

                            def mark(ins):
                                ins.then_inc(general, 1)
                                at[0] += 1

                            take_round(link, mark)
                            assert at[0] == per_round
                    for t in tiles:
                        nc.vector.tensor_tensor(probs[:, t, 0:N], probs[:, t, 0:N], below[:, t, 0:N],
                                                ALU.subtract).then_inc(mixing.probs_ready, 1)

                for part, (a, b) in enumerate(PARTS):
                    select(a, b, halved[part], general[part])


def update_stage(core, name, z, xa, xf, mixed_xa, spread, u1, u2, xaf):
    nc = core.nc
    with ExitStack() as ctx:
        def sb(n, shape):
            return ctx.enter_context(nc.sbuf_tensor(f"{name}_{n}", shape, F32))

        w1, w2, xff = sb("w1", [P, P]), sb("w2", [P, P]), sb("xff", [P, NP])
        inv = sb("inv", [P, T])
        loaded, steps, mixed_ready, turned, kept, z_made = core.sems(
            *[f"{name}_{s}" for s in ("loaded", "steps", "mixed_ready", "turned", "kept", "z_made")])
        with nc.Block() as block:
            @block.sync
            def _(sp):
                sp.dma_start(w1[:], u1).then_inc(loaded, 16)
                sp.dma_start(w2[:], u2).then_inc(loaded, 16)

            @block.vector
            def _(dve):
                chain = Chain(nc, dve, steps)
                chain.link(nc.vector.reciprocal(inv[:], mixed_xa[:, :, P]))
                nc.vector.tensor_tensor(xa[:, :, 0:P], mixed_xa[:, :, 0:P], per_node(inv[:]),
                                        ALU.mult).then_inc(mixed_ready, 1)
                chain.link(nc.vector.tensor_tensor(spread[:], spread[:], xf[:], ALU.add))
                chain.link(nc.vector.reciprocal(inv[:], spread[:, :, P]))
                dve.wait_ge(mixed_ready, 1)
                nc.vector.tensor_tensor(xf[:, :, 0:P], spread[:, :, 0:P], per_node(inv[:]),
                                        ALU.mult).then_inc(mixed_ready, 1)
                for g, (a, b) in enumerate(GROUPS):
                    dve.wait_ge(z_made, g + 1)
                    y = core.banks(g, 1, (b - a) * P).rearrange("p (t c) -> p t c", c=P)
                    chain.link(nc.vector.tensor_tensor(z[:, a:b, :], z[:, a:b, :], y, ALU.add))

            @block.tensor
            def _(pe):
                pe.wait_ge(mixed_ready, 1)
                turn_tiles(pe, core, xa[:, :, 0:P], turned)
                pe.wait_ge(mixed_ready, 2)
                turn_tiles(pe, core, xf[:, :, 0:P], turned, 3)
                pe.wait_ge(loaded, 32)
                pe.wait_ge(kept, 6)
                for g, (a, b) in enumerate(GROUPS):
                    for t in range(a, b):
                        o = core.ps[:, g, (t - a) * P:(t - a + 1) * P]
                        nc.tensor.matmul(o, xff[:, t * P:(t + 1) * P], w1[:], start=True, stop=False)
                        mm = nc.tensor.matmul(o, xaf[:, t * P:(t + 1) * P], w2[:], start=False, stop=True)
                    mm.then_inc(z_made, 1)

            @block.scalar
            def _(act):
                for i, dst in enumerate((xaf, xff)):
                    for g, (a, w) in enumerate(PCHUNKS):
                        act.wait_ge(turned, 3 * i + g + 1)
                        nc.scalar.activation(dst[:, a:a + w], core.banks(3 * i + g, 1, w), ACT.Copy).then_inc(kept, 1)


def propagation_layer(core, h):
    nc = core.nc
    with ExitStack() as ctx:
        def sb(n, shape):
            return ctx.enter_context(nc.sbuf_tensor(f"g0_{n}", shape, F32))

        z = sb("z", [P, T, P])
        with ExitStack() as inner:
            def sbi(n, shape):
                return inner.enter_context(nc.sbuf_tensor(f"g0_{n}", shape, F32))

            xa, xf, mixed_xa, spread = [sbi(n, [P, T, P + 1]) for n in ("xa", "xf", "mixed_xa", "spread")]
            xaf = sbi("xaf", [P, NP])
            probs, sums = sbi("probs", [P, T, NP]), sbi("sums", [P, T])
            started = core.sem("g0_started")
            with nc.Block() as block:
                @block.vector
                def _(dve):
                    nc.vector.memset(xa[:, :, P:P + 1], 1.0).then_inc(started, 1)
                    nc.vector.memset(xf[:, :, P:P + 1], 1.0).then_inc(started, 1)
                    nc.vector.memset(probs[:, :, N:NP], 0.0).then_inc(started, 1)
                    nc.vector.tensor_copy(z[:], core.n[:]).then_inc(started, 1)
                    nc.vector.tensor_copy(xa[:, :, 0:P], core.n[:]).then_inc(started, 1)
                    nc.vector.tensor_copy(xf[:, :, 0:P], core.n[:]).then_inc(started, 1)

            w = {"w1": h["g0_w1"], "w2": h["g0_w2"], "w3": h["g0_w3"]}
            for n in range(STEPS):
                scores_stage(core, f"g0l{n}", core.nf if n == 0 else xaf, w, probs, sums)
                top_p_stage(core, f"g0p{n}", HALVINGS[n], ROUNDS[n], probs, sums, h["adj_t"], xf, spread, xa, mixed_xa)
                update_stage(core, f"g0u{n}", z, xa, xf, mixed_xa, spread, h["g0_u1"][n], h["g0_u2"][n], xaf)
                core.recycle()
        gat_norm_stage(core, "g0n", 1, z[:], None, h["g0_gain"], h["g0_shift"])


def load_stage(core, x, identity):
    nc = core.nc
    loaded, cleared = core.sems("x_loaded", "x_cleared")
    with nc.Block() as block:
        @block.vector
        def _(dve):
            nc.vector.memset(core.x[:, T - 1, :], 0.0).then_inc(cleared, 1)

        @block.sync
        def _(sp):
            full = (T - 1) * P
            sp.dma_start(core.x[:, 0:T - 1, :], x[0:full, :].rearrange("(t p) d -> p t d", p=P)).then_inc(loaded, 16)
            sp.dma_start(core.ident[:], identity).then_inc(loaded, 16)
            sp.wait_ge(cleared, 1)
            sp.dma_start(core.x[0:N - full, T - 1, :], x[full:N, :]).then_inc(loaded, 16)
            sp.wait_ge(loaded, 48)


def store_stage(core, out):
    nc = core.nc
    stored = core.sem("stored")
    with nc.Block() as block:
        @block.sync
        def _(sp):
            full = (T - 1) * P
            sp.dma_start(out[0:full, :].rearrange("(t p) d -> p t d", p=P), core.x[:, 0:T - 1, :]).then_inc(stored, 16)
            sp.dma_start(out[full:N, :], core.x[0:N - full, T - 1, :]).then_inc(stored, 16)
            sp.wait_ge(stored, 32)


def program(nc, h, out, only=None):
    with ExitStack() as ctx:
        core = Core(nc, ctx)
        comb = ctx.enter_context(nc.sbuf_tensor("comb", [P, T, 8], F32))
        load_stage(core, h["x"], h["identity"])

        def run(layer):
            return only is None or layer in only

        if run("g0"):
            layernorm_stage(core, "ln0g")
            propagation_layer(core, h)
            core.recycle()
        if run("f0"):
            router = ("r0", 8, h["f0_wr"], None, h["f0_b2"], comb, False, True, 0, core.nf)
            ffn_stage(core, "f0", None, router, 8, 1, ACT.Gelu, h["f0_w1"], h["f0_b1"], h["f0_w2"], comb, core.nf)
            core.recycle()
        if run("g1"):
            gat_layer(core, h, 1)
            core.recycle()
        if run("f1"):
            router = ("r1", 4, h["f1_wr"], h["f1_br"], h["f1_b3"], comb, True, False, 1, core.nf)
            deep_ffn_stage(core, "f1", router, 5, h["f1_w1"], h["f1_b1"], h["f1_w2"], h["f1_b2"], h["f1_w3"], comb, core.nf)
            core.recycle()
        if run("g2"):
            gat_layer(core, h, 2)
            core.recycle()
        if run("f2"):
            router = ("r2", 8, h["f2_wr"], h["f2_br"], h["f2_b2"], comb, False, False, 0, core.nf)
            ffn_stage(core, "f2", (h["f2_gamma"], h["f2_beta"]), router, 8, 2, ACT.Gelu, h["f2_w1"], h["f2_b1"], h["f2_w2"], comb, core.nf)
            core.recycle()
        if run("g3"):
            masked_attention(core, h)
            core.recycle()
        if run("f3"):
            router = ("r3", 8, h["f3_wr"], h["f3_br"], h["f3_b2"], comb, False, False, 0, core.nf)
            ffn_stage(core, "f3", None, router, 8, 4, ACT.Relu, h["f3_w1"], h["f3_b1"], h["f3_w2"], comb, core.nf)
        store_stage(core, out)


def kernel(**inputs):
    import numpy as np
    import concourse.bacc as bacc
    from concourse.bass_utils import run_bass_kernel_spmd

    i = {k: np.asarray(v) for k, v in inputs.items()}
    adj = np.zeros((NP, NP), np.float32)
    adj[0:N, 0:N] = i["adj"]
    adj[N:, 0] = 1.0

    def hidden_bias(b):
        return b.reshape(b.shape[0], -1, P).transpose(2, 0, 1)

    def second(w):
        return w.reshape(w.shape[0], -1, P, w.shape[2]).transpose(0, 2, 1, 3)

    ew2 = np.zeros((4, P, P), np.float32)
    ew2[:, :, 0:64] = i["L1_ffn_eW2"]
    ew3 = np.zeros((4, P, P), np.float32)
    ew3[:, 0:64, :] = i["L1_ffn_eW3"]
    eb2 = np.zeros((4, P), np.float32)
    eb2[:, 0:64] = i["L1_ffn_eb2"]

    def five(experts, shared):
        return np.concatenate([experts, shared[None]]).transpose(1, 0, 2)

    a = {
        "x": i["x"],
        "identity": np.eye(P, dtype=np.float32),
        "adj": adj,
        "adj_t": adj.reshape(T, P, T, P).transpose(0, 3, 2, 1),
        "g0_w1": i["L0_gnn_W1"].T, "g0_w2": i["L0_gnn_W2"].T, "g0_w3": i["L0_gnn_W3"].T,
        "g0_u1": i["L0_gnn_U1"].transpose(0, 2, 1), "g0_u2": i["L0_gnn_U2"].transpose(0, 2, 1),
        "g0_gain": i["L0_gnn_ln_g"], "g0_shift": i["L0_gnn_ln_b"],
        "f0_wr": i["L0_ffn_router_w"].T, "f0_w1": i["L0_ffn_w1"], "f0_b1": hidden_bias(i["L0_ffn_b1"]),
        "f0_w2": second(i["L0_ffn_w2"]), "f0_b2": i["L0_ffn_b2"],
        "g1_w": i["L1_gnn_W"], "g1_a": i["L1_gnn_a"][:, 0], "g1_gain": i["L1_gnn_gamma"],
        "g1_shift": i["L1_gnn_beta"],
        "f1_wr": i["L1_ffn_gW"], "f1_br": i["L1_ffn_gb"],
        "f1_w1": five(i["L1_ffn_eW1"], i["L1_ffn_sW1"]), "f1_w2": five(ew2, i["L1_ffn_sW2"]),
        "f1_w3": five(ew3, i["L1_ffn_sW3"]),
        "f1_b1": np.concatenate([i["L1_ffn_eb1"], i["L1_ffn_sb1"][None]]).T,
        "f1_b2": np.concatenate([eb2, i["L1_ffn_sb2"][None]]).T,
        "f1_b3": np.concatenate([i["L1_ffn_eb3"], i["L1_ffn_sb3"][None]]),
        "g2_w": i["L2_gnn_W"].T, "g2_b": i["L2_gnn_b"], "g2_s": i["L2_gnn_S"],
        "f2_gamma": i["L2_ffn_gamma"][:, None], "f2_beta": i["L2_ffn_beta"][:, None],
        "f2_wr": i["L2_ffn_Wr"], "f2_br": i["L2_ffn_br"], "f2_w1": i["L2_ffn_W1"],
        "f2_b1": hidden_bias(i["L2_ffn_b1"]), "f2_w2": second(i["L2_ffn_W2"]), "f2_b2": i["L2_ffn_b2"],
        "g3_w": i["L3_gnn_Wqkv"], "g3_b": i["L3_gnn_bqkv"], "g3_wo": i["L3_gnn_Wout"],
        "g3_bo": i["L3_gnn_bout"], "g3_gb": i["L3_gnn_graph_bias"].reshape(1),
        "f3_wr": i["L3_ffn_Wg"].T, "f3_br": i["L3_ffn_bg"], "f3_w1": i["L3_ffn_W1"].transpose(0, 2, 1),
        "f3_b1": hidden_bias(i["L3_ffn_b1"]), "f3_w2": second(i["L3_ffn_W2"].transpose(0, 2, 1)),
        "f3_b2": i["L3_ffn_b2"],
    }
    a = {f"in_{k}": np.ascontiguousarray(v) for k, v in a.items()}
    nc = bacc.Bacc("TRN2", target_bir_lowering=False, num_devices=1)
    h = {k[3:]: nc.dram_tensor(k, v.shape, F32, kind="ExternalInput").ap() for k, v in a.items()}
    out = nc.dram_tensor("out", (N, P), F32, kind="ExternalOutput").ap()
    program(nc, h, out)
    r = run_bass_kernel_spmd(nc, [a], core_ids=[0])
    return r.results[0]["out"]
```
